# Optimizing a Trainium2 kernel written in Bass

```python
import numpy as np
import jax
import jax.numpy as jnp

def _softmax(x, axis=-1):
    return jax.nn.softmax(x, axis=axis)

def _gelu(x):
    return jax.nn.gelu(x, approximate=True)

def _silu(x):
    return jax.nn.silu(x)

def _sigmoid(x):
    return jax.nn.sigmoid(x)

def _layernorm(x, axis=-1, eps=1e-05):
    m = jnp.mean(x, axis=axis, keepdims=True)
    v = jnp.var(x, axis=axis, keepdims=True)
    return (x - m) / jnp.sqrt(v + eps)

def _scatter_add(tgt, idx, src, axis=0):
    return tgt.at[idx].add(src)

def _segment_sum(src, seg, n):
    return jax.ops.segment_sum(src, seg, n)
kernel_name = 'mk_decoder_postln_d2_seqx_r4_408357'

def setup_inputs(seed: int=0):
    np.random.seed(seed)
    _w = jnp.asarray

    def _rec_inputs():
        import jax
        import jax.numpy as jnp
        _rk = jax.random.key(seed)
        x = 7.22e-05 + 1 * jax.random.normal(jax.random.fold_in(_rk, 1), (16, 256, 256), jnp.float32)
        _lenS = 256 - jax.random.randint(jax.random.fold_in(_rk, 7), (16,), 0, max(1, 256 // 4) + 1, jnp.int32)
        _lenS2 = 256 - jax.random.randint(jax.random.fold_in(_rk, 8), (16,), 0, max(1, 256 // 4) + 1, jnp.int32)
        _ctx_1024P = jax.random.normal(jax.random.fold_in(_rk, 11), (16, 16, 256), jnp.float32)
        _ctx_1024c = jax.random.dirichlet(jax.random.fold_in(_rk, 511), 0.3 * jnp.ones((16,), jnp.float32), (16, 256))
        _ctx_1024t = jnp.einsum('bsk,bkd->bsd', _ctx_1024c, _ctx_1024P)
        _ctx_1024t = _ctx_1024t * jax.lax.rsqrt(jnp.mean(jnp.square(_ctx_1024t)) + 1e-12) * 0.953939
        ctx_1024 = 4.13588e-05 + 0.999923 * (_ctx_1024t + 0.3 * jax.random.normal(jax.random.fold_in(_rk, 611), (16, 256, 256), jnp.float32))
        return (x, ctx_1024)
    x, ctx_1024 = _rec_inputs()

    def _L0_attn_setup():
        import jax, jax.numpy as jnp
        import numpy as np
        B, L, D = (2, 1024, 256)
        H = 16
        DK = D // H

        def _l2norm(x, eps=1e-12):
            n = jnp.sqrt(jnp.sum(x * x, axis=-1, keepdims=True))
            return x / jnp.maximum(n, eps)
        key = jax.random.key(seed)
        ks = jax.random.split(key, 16)
        s = 0.02
        inp = {'x': jax.random.normal(ks[0], (B, L, D), dtype=jnp.float32), 'Wq': jax.random.normal(ks[1], (D, D), dtype=jnp.float32) * s, 'Wk': jax.random.normal(ks[2], (D, D), dtype=jnp.float32) * s, 'Wv': jax.random.normal(ks[3], (D, D), dtype=jnp.float32) * s, 'Wb': jax.random.normal(ks[4], (D, H), dtype=jnp.float32) * s, 'Wo': jax.random.normal(ks[5], (D, D), dtype=jnp.float32) * s, 'Wfd': jax.random.normal(ks[6], (D, H), dtype=jnp.float32) * s, 'bfd': jax.random.normal(ks[7], (H,), dtype=jnp.float32) * s, 'Wsd': jax.random.normal(ks[8], (D, H), dtype=jnp.float32) * s, 'bsd': jax.random.normal(ks[9], (H,), dtype=jnp.float32) * s, 'Wtf1': jax.random.normal(ks[10], (DK, DK // 2), dtype=jnp.float32) * s, 'btf1': jax.random.normal(ks[11], (DK // 2,), dtype=jnp.float32) * s, 'Wtf2': jax.random.normal(ks[12], (DK // 2, 1), dtype=jnp.float32) * s, 'btf2': jax.random.normal(ks[13], (1,), dtype=jnp.float32) * s}
        return inp
    _L0_attn_all = _L0_attn_setup()
    _L0_attn_in = {k: v for k, v in _L0_attn_all.items() if k in ('Wq', 'Wk', 'Wv', 'Wb', 'Wo', 'Wfd', 'bfd', 'Wsd', 'bsd', 'Wtf1', 'btf1', 'Wtf2', 'btf2')}
    del _L0_attn_all

    def _L0_xattn_setup():
        import jax, jax.numpy as jnp
        import numpy as np
        import math
        DIM = 256
        HEADS = 16
        WINDOW = 64

        def _rope(x):
            b, s, d = x.shape
            half = d // 2
            inv_freq = 1.0 / 10000.0 ** (jnp.arange(half, dtype=jnp.float32) / half)
            ang = jnp.arange(s, dtype=jnp.float32)[:, None] * inv_freq[None, :]
            cos, sin = (jnp.cos(ang), jnp.sin(ang))
            x1, x2 = (x[..., :half], x[..., half:])
            return jnp.concatenate([x1 * cos - x2 * sin, x1 * sin + x2 * cos], axis=-1)
        key = jax.random.key(seed)
        ks = jax.random.split(key, 8)
        d = DIM
        q = jax.random.normal(ks[0], (2, 1024, d), dtype=jnp.float32)
        k = jax.random.normal(ks[1], (2, 1024, d), dtype=jnp.float32)
        v = jax.random.normal(ks[2], (2, 1024, d), dtype=jnp.float32)
        wq = jax.random.normal(ks[3], (d, d), dtype=jnp.float32) * 0.02
        wk = jax.random.normal(ks[4], (d, d), dtype=jnp.float32) * 0.02
        wv = jax.random.normal(ks[5], (d, d), dtype=jnp.float32) * 0.02
        wo_w = jax.random.normal(ks[6], (d, d), dtype=jnp.float32) * 0.02
        wo_b = jnp.zeros((d,), dtype=jnp.float32)
        return {'q': q, 'k': k, 'v': v, 'wq': wq, 'wk': wk, 'wv': wv, 'wo_w': wo_w, 'wo_b': wo_b}
    _L0_xattn_all = _L0_xattn_setup()
    _L0_xattn_in = {k: v for k, v in _L0_xattn_all.items() if k in ('wq', 'wk', 'wv', 'wo_w', 'wo_b')}
    del _L0_xattn_all

    def _L0_ffn_setup():
        import jax, jax.numpy as jnp
        import numpy as np
        B, S, D = (8, 128, 256)
        H = 16
        DFF = 1024
        E = 4
        K = 2
        EPS = 1e-05

        def _layernorm(x, w, b):
            m = x.mean(-1, keepdims=True)
            v = ((x - m) ** 2).mean(-1, keepdims=True)
            return (x - m) / jnp.sqrt(v + EPS) * w + b

        def _encoder_layer(x, iw, ib, ow, ob, l1w, l1b, l2w, l2b, n1w, n1b, n2w, n2b):
            b, s, d = x.shape
            hd = d // H
            qkv = x @ iw.T + ib
            q, k, v = jnp.split(qkv, 3, axis=-1)
            rs = lambda t: t.reshape(b, s, H, hd).transpose(0, 2, 1, 3)
            q, k, v = (rs(q), rs(k), rs(v))
            scale = jnp.asarray(hd, x.dtype) ** 0.5
            scores = jnp.einsum('bhqd,bhkd->bhqk', q, k) / scale
            attn = jax.nn.softmax(scores, axis=-1)
            o = jnp.einsum('bhqk,bhkd->bhqd', attn, v).transpose(0, 2, 1, 3).reshape(b, s, d)
            o = o @ ow.T + ob
            x = _layernorm(x + o, n1w, n1b)
            ff = jax.nn.relu(x @ l1w.T + l1b) @ l2w.T + l2b
            return _layernorm(x + ff, n2w, n2b)
        key = jax.random.key(seed)
        ks = jax.random.split(key, 12)
        g = lambda k, shape: jax.random.normal(k, shape, dtype=jnp.float32) * 0.02
        return {'x': jax.random.normal(ks[0], (B, S, D), dtype=jnp.float32), 'in_proj_w': g(ks[1], (E, 3 * D, D)), 'in_proj_b': g(ks[2], (E, 3 * D)), 'out_proj_w': g(ks[3], (E, D, D)), 'out_proj_b': g(ks[4], (E, D)), 'ln1_w': jnp.ones((E, D), jnp.float32), 'ln1_b': jnp.zeros((E, D), jnp.float32), 'lin1_w': g(ks[5], (E, DFF, D)), 'lin1_b': g(ks[6], (E, DFF)), 'lin2_w': g(ks[7], (E, D, DFF)), 'lin2_b': g(ks[8], (E, D)), 'ln2_w': jnp.ones((E, D), jnp.float32), 'ln2_b': jnp.zeros((E, D), jnp.float32), 'gate_w': g(ks[9], (E, D)), 'gate_b': g(ks[10], (E,))}
    _L0_ffn_all = _L0_ffn_setup()
    _L0_ffn_in = {k: v for k, v in _L0_ffn_all.items() if k in ('in_proj_w', 'in_proj_b', 'out_proj_w', 'out_proj_b', 'ln1_w', 'ln1_b', 'lin1_w', 'lin1_b', 'lin2_w', 'lin2_b', 'ln2_w', 'ln2_b', 'gate_w', 'gate_b')}
    del _L0_ffn_all

    def _L1_attn_setup():
        import jax, jax.numpy as jnp
        import numpy as np
        D_OUT = 256
        key = jax.random.key(seed)
        k1, k2 = jax.random.split(key)
        x = jax.random.normal(k1, (4, 512, 256), dtype=jnp.float32)
        W_qkv = jax.random.normal(k2, (256, 3 * D_OUT), dtype=jnp.float32) * 0.02
        return {'x': x, 'W_qkv': W_qkv}
    _L1_attn_all = _L1_attn_setup()
    _L1_attn_in = {k: v for k, v in _L1_attn_all.items() if k in ('W_qkv',)}
    del _L1_attn_all

    def _L1_xattn_setup():
        import jax, jax.numpy as jnp
        import numpy as np
        B, S, H, NH = (2, 512, 256, 4)
        DH = H // NH
        EPS = 1e-06

        def _parallel_stabilized(qh, kh, vh, ig, fg):
            log_fg = jax.nn.log_sigmoid(fg)
            cs = jnp.cumsum(log_fg, axis=2)
            ltr = jnp.tril(jnp.ones((qh.shape[2], qh.shape[2]), dtype=bool))
            log_fg_mat = jnp.where(ltr, cs - jnp.swapaxes(cs, 2, 3), -jnp.inf)
            log_D = log_fg_mat + jnp.swapaxes(ig, 2, 3)
            max_log_D = jnp.max(log_D, axis=-1, keepdims=True)
            D = jnp.exp(log_D - max_log_D)
            qk = jnp.einsum('bhsd,bhtd->bhst', qh, kh) / jnp.sqrt(jnp.float32(DH))
            C = qk * D
            normalizer = jnp.maximum(jnp.abs(jnp.sum(C, axis=-1, keepdims=True)), jnp.exp(-max_log_D))
            return jnp.einsum('bhst,bhtd->bhsd', C / (normalizer + EPS), vh)
        key = jax.random.key(seed)
        ks = jax.random.split(key, 6)
        q = jax.random.normal(ks[0], (B, S, H), dtype=jnp.float32)
        k = jax.random.normal(ks[1], (B, S, H), dtype=jnp.float32)
        v = jax.random.normal(ks[2], (B, S, H), dtype=jnp.float32)
        igate_kernel = jax.random.normal(ks[3], (3 * H, NH), dtype=jnp.float32) * 0.02
        fgate_kernel = jax.random.normal(ks[4], (3 * H, NH), dtype=jnp.float32) * 0.02
        igate_bias = jax.random.normal(ks[5], (NH,), dtype=jnp.float32) * 0.1
        fgate_bias = jnp.linspace(3.0, 6.0, NH, dtype=jnp.float32)
        outnorm_scale = jnp.ones((H,), dtype=jnp.float32)
        return {'q': q, 'k': k, 'v': v, 'igate_kernel': igate_kernel, 'igate_bias': igate_bias, 'fgate_kernel': fgate_kernel, 'fgate_bias': fgate_bias, 'outnorm_scale': outnorm_scale}
    _L1_xattn_all = _L1_xattn_setup()
    _L1_xattn_in = {k: v for k, v in _L1_xattn_all.items() if k in ('igate_kernel', 'igate_bias', 'fgate_kernel', 'fgate_bias', 'outnorm_scale')}
    del _L1_xattn_all

    def _L1_ffn_setup():
        import jax, jax.numpy as jnp
        import numpy as np
        N_EXPERTS = 32
        TOP_K = 8
        N_GROUP = 4
        TOPK_GROUP = 2
        ROUTED_SCALING = 2.5

        def _gate(x, gate_w, gate_bias):
            T, E = (x.shape[0], gate_w.shape[0])
            logits = jnp.einsum('th,eh->te', x, gate_w)
            scores = jax.nn.sigmoid(logits)
            scores_choice = scores + gate_bias[None, :]
            grp = scores_choice.reshape(T, N_GROUP, E // N_GROUP)
            top2, _ = jax.lax.top_k(grp, 2)
            group_scores = top2.sum(-1)
            _, grp_idx = jax.lax.top_k(group_scores, TOPK_GROUP)
            group_mask = jax.nn.one_hot(grp_idx, N_GROUP, dtype=scores.dtype).sum(1)
            expert_mask = jnp.repeat(group_mask, E // N_GROUP, axis=1)
            masked = jnp.where(expert_mask > 0, scores_choice, 0.0)
            _, topk_idx = jax.lax.top_k(masked, TOP_K)
            topk_w = jnp.take_along_axis(scores, topk_idx, axis=1)
            topk_w = topk_w / (topk_w.sum(-1, keepdims=True) + 1e-20)
            topk_w = topk_w * ROUTED_SCALING
            return (topk_idx, topk_w)

        def _mlp(x, wg, wu, wd):
            return jnp.einsum('...i,hi->...h', jax.nn.silu(jnp.einsum('...h,ih->...i', x, wg)) * jnp.einsum('...h,ih->...i', x, wu), wd)
        key = jax.random.key(seed)
        ks = jax.random.split(key, 9)
        B, S, H, I = (2, 128, 256, 128)
        w = 0.02
        return {'hidden_states': jax.random.normal(ks[0], (B, S, H), jnp.float32), 'gate_w': jax.random.normal(ks[1], (N_EXPERTS, H), jnp.float32) * w, 'gate_bias': jax.random.normal(ks[2], (N_EXPERTS,), jnp.float32) * w, 'expert_gate': jax.random.normal(ks[3], (N_EXPERTS, I, H), jnp.float32) * w, 'expert_up': jax.random.normal(ks[4], (N_EXPERTS, I, H), jnp.float32) * w, 'expert_down': jax.random.normal(ks[5], (N_EXPERTS, H, I), jnp.float32) * w, 'shared_gate': jax.random.normal(ks[6], (2 * I, H), jnp.float32) * w, 'shared_up': jax.random.normal(ks[7], (2 * I, H), jnp.float32) * w, 'shared_down': jax.random.normal(ks[8], (H, 2 * I), jnp.float32) * w}
    _L1_ffn_all = _L1_ffn_setup()
    _L1_ffn_in = {k: v for k, v in _L1_ffn_all.items() if k in ('gate_w', 'gate_bias', 'expert_gate', 'expert_up', 'expert_down', 'shared_gate', 'shared_up', 'shared_down')}
    del _L1_ffn_all
    return {'x': x, 'ctx_1024': ctx_1024, 'L0_attn_Wq': _L0_attn_in['Wq'], 'L0_attn_Wk': _L0_attn_in['Wk'], 'L0_attn_Wv': _L0_attn_in['Wv'], 'L0_attn_Wb': _L0_attn_in['Wb'], 'L0_attn_Wo': _L0_attn_in['Wo'], 'L0_attn_Wfd': _L0_attn_in['Wfd'], 'L0_attn_bfd': _L0_attn_in['bfd'], 'L0_attn_Wsd': _L0_attn_in['Wsd'], 'L0_attn_bsd': _L0_attn_in['bsd'], 'L0_attn_Wtf1': _L0_attn_in['Wtf1'], 'L0_attn_btf1': _L0_attn_in['btf1'], 'L0_attn_Wtf2': _L0_attn_in['Wtf2'], 'L0_attn_btf2': _L0_attn_in['btf2'], 'L0_xattn_wq': _L0_xattn_in['wq'], 'L0_xattn_wk': _L0_xattn_in['wk'], 'L0_xattn_wv': _L0_xattn_in['wv'], 'L0_xattn_wo_w': _L0_xattn_in['wo_w'], 'L0_xattn_wo_b': _L0_xattn_in['wo_b'], 'L0_ffn_in_proj_w': _L0_ffn_in['in_proj_w'], 'L0_ffn_in_proj_b': _L0_ffn_in['in_proj_b'], 'L0_ffn_out_proj_w': _L0_ffn_in['out_proj_w'], 'L0_ffn_out_proj_b': _L0_ffn_in['out_proj_b'], 'L0_ffn_ln1_w': _L0_ffn_in['ln1_w'], 'L0_ffn_ln1_b': _L0_ffn_in['ln1_b'], 'L0_ffn_lin1_w': _L0_ffn_in['lin1_w'], 'L0_ffn_lin1_b': _L0_ffn_in['lin1_b'], 'L0_ffn_lin2_w': _L0_ffn_in['lin2_w'], 'L0_ffn_lin2_b': _L0_ffn_in['lin2_b'], 'L0_ffn_ln2_w': _L0_ffn_in['ln2_w'], 'L0_ffn_ln2_b': _L0_ffn_in['ln2_b'], 'L0_ffn_gate_w': _L0_ffn_in['gate_w'], 'L0_ffn_gate_b': _L0_ffn_in['gate_b'], 'L1_attn_W_qkv': _L1_attn_in['W_qkv'], 'L1_xattn_igate_kernel': _L1_xattn_in['igate_kernel'], 'L1_xattn_igate_bias': _L1_xattn_in['igate_bias'], 'L1_xattn_fgate_kernel': _L1_xattn_in['fgate_kernel'], 'L1_xattn_fgate_bias': _L1_xattn_in['fgate_bias'], 'L1_xattn_outnorm_scale': _L1_xattn_in['outnorm_scale'], 'L1_ffn_gate_w': _L1_ffn_in['gate_w'], 'L1_ffn_gate_bias': _L1_ffn_in['gate_bias'], 'L1_ffn_expert_gate': _L1_ffn_in['expert_gate'], 'L1_ffn_expert_up': _L1_ffn_in['expert_up'], 'L1_ffn_expert_down': _L1_ffn_in['expert_down'], 'L1_ffn_shared_gate': _L1_ffn_in['shared_gate'], 'L1_ffn_shared_up': _L1_ffn_in['shared_up'], 'L1_ffn_shared_down': _L1_ffn_in['shared_down']}

def reference(x, ctx_1024, L0_attn_Wq, L0_attn_Wk, L0_attn_Wv, L0_attn_Wb, L0_attn_Wo, L0_attn_Wfd, L0_attn_bfd, L0_attn_Wsd, L0_attn_bsd, L0_attn_Wtf1, L0_attn_btf1, L0_attn_Wtf2, L0_attn_btf2, L0_xattn_wq, L0_xattn_wk, L0_xattn_wv, L0_xattn_wo_w, L0_xattn_wo_b, L0_ffn_in_proj_w, L0_ffn_in_proj_b, L0_ffn_out_proj_w, L0_ffn_out_proj_b, L0_ffn_ln1_w, L0_ffn_ln1_b, L0_ffn_lin1_w, L0_ffn_lin1_b, L0_ffn_lin2_w, L0_ffn_lin2_b, L0_ffn_ln2_w, L0_ffn_ln2_b, L0_ffn_gate_w, L0_ffn_gate_b, L1_attn_W_qkv, L1_xattn_igate_kernel, L1_xattn_igate_bias, L1_xattn_fgate_kernel, L1_xattn_fgate_bias, L1_xattn_outnorm_scale, L1_ffn_gate_w, L1_ffn_gate_bias, L1_ffn_expert_gate, L1_ffn_expert_up, L1_ffn_expert_down, L1_ffn_shared_gate, L1_ffn_shared_up, L1_ffn_shared_down):
    import jax
    import jax.numpy as jnp

    def _L0_attn_ref(x, Wq, Wk, Wv, Wb, Wo, Wfd, bfd, Wsd, bsd, Wtf1, btf1, Wtf2, btf2):
        import jax, jax.numpy as jnp
        import numpy as np
        B, L, D = (2, 1024, 256)
        H = 16
        DK = D // H

        def _l2norm(x, eps=1e-12):
            n = jnp.sqrt(jnp.sum(x * x, axis=-1, keepdims=True))
            return x / jnp.maximum(n, eps)
        b, l, d = x.shape
        h, dk = (H, DK)

        def heads(y):
            return y.reshape(b, l, h, dk).transpose(0, 2, 1, 3)
        q = _l2norm(heads(x @ Wq))
        k = _l2norm(heads(x @ Wk))
        v = heads(x @ Wv)
        beta = jax.nn.sigmoid(x @ Wb).transpose(0, 2, 1)
        fast_decay = jax.nn.sigmoid(x @ Wfd + bfd).transpose(0, 2, 1)
        slow_decay = jax.nn.sigmoid(x @ Wsd + bsd).transpose(0, 2, 1)
        beta_e = beta[..., None]
        v_scaled = v * beta_e
        k_beta = k * beta_e
        hmid = jax.nn.silu(k_beta @ Wtf1 + btf1)
        token_flux = jnp.clip(jax.nn.sigmoid(hmid @ Wtf2 + btf2), 0.01, 0.99)
        log_fast = jnp.log(fast_decay + 1e-06)
        log_slow = jnp.log(slow_decay + 1e-06)
        fast_cs = jnp.cumsum(log_fast, axis=-1)
        slow_cs = jnp.cumsum(log_slow, axis=-1)
        fast_w = jnp.exp(fast_cs[:, :, -1:] - fast_cs)[..., None]
        slow_w = jnp.exp(slow_cs[:, :, -1:] - slow_cs)[..., None]
        k_fast = k_beta * fast_w
        k_slow = k_beta * slow_w
        M_fast = jnp.einsum('bhld,bhle->bhde', k_fast, v_scaled)
        M_slow = jnp.einsum('bhld,bhle->bhde', k_slow, v_scaled)
        M_fast = M_fast / (fast_w.sum(axis=2)[..., None] + 1e-06)
        M_slow = M_slow / (slow_w.sum(axis=2)[..., None] + 1e-06)
        o_fast = jnp.einsum('bhld,bhde->bhle', q, M_fast)
        o_slow = jnp.einsum('bhld,bhde->bhle', q, M_slow)
        alpha = 0.5 + 0.3 * token_flux
        o = alpha * o_fast + (1.0 - alpha) * o_slow
        o = o.transpose(0, 2, 1, 3).reshape(b, l, d)
        return o @ Wo

    def _L0_xattn_ref(q, k, v, wq, wk, wv, wo_w, wo_b):
        import jax, jax.numpy as jnp
        import numpy as np
        import math
        DIM = 256
        HEADS = 16
        WINDOW = 64

        def _rope(x):
            b, s, d = x.shape
            half = d // 2
            inv_freq = 1.0 / 10000.0 ** (jnp.arange(half, dtype=jnp.float32) / half)
            ang = jnp.arange(s, dtype=jnp.float32)[:, None] * inv_freq[None, :]
            cos, sin = (jnp.cos(ang), jnp.sin(ang))
            x1, x2 = (x[..., :half], x[..., half:])
            return jnp.concatenate([x1 * cos - x2 * sin, x1 * sin + x2 * cos], axis=-1)
        b, s, d = q.shape
        h, W = (HEADS, WINDOW)
        dk = d // h
        B = W
        nb = s // B
        qp = _rope(jnp.einsum('bsd,ed->bse', q, wq))
        kp = _rope(jnp.einsum('bsd,ed->bse', k, wk))
        vp = jnp.einsum('bsd,ed->bse', v, wv)
        qh = qp.reshape(b, s, h, dk).transpose(0, 2, 1, 3)
        kh = kp.reshape(b, s, h, dk).transpose(0, 2, 1, 3)
        vh = vp.reshape(b, s, h, dk).transpose(0, 2, 1, 3)
        kpad = jnp.pad(kh, ((0, 0), (0, 0), (B, B), (0, 0)))
        vpad = jnp.pad(vh, ((0, 0), (0, 0), (B, B), (0, 0)))
        kblk = kpad.reshape(b, h, nb + 2, B, dk)
        vblk = vpad.reshape(b, h, nb + 2, B, dk)
        kband = jnp.concatenate([kblk[:, :, i:i + nb] for i in range(3)], axis=3)
        vband = jnp.concatenate([vblk[:, :, i:i + nb] for i in range(3)], axis=3)
        qb = qh.reshape(b, h, nb, B, dk)
        scores = jnp.einsum('bhnqd,bhnkd->bhnqk', qb, kband) * math.sqrt(dk)
        n_idx = jnp.arange(nb)[:, None, None]
        qi = jnp.arange(B)[None, :, None]
        ki = jnp.arange(3 * B)[None, None, :]
        kpos = (n_idx - 1) * B + ki
        rel = ki - B - qi
        valid = (rel >= -W) & (rel <= W) & (kpos >= 0) & (kpos < s)
        neg = jnp.asarray(jnp.finfo(scores.dtype).min, scores.dtype)
        scores = jnp.where(valid[None, None], scores, neg)
        attn = jax.nn.softmax(scores, axis=-1)
        out = jnp.einsum('bhnqk,bhnkd->bhnqd', attn, vband)
        out = out.reshape(b, h, s, dk).transpose(0, 2, 1, 3).reshape(b, s, d)
        return jnp.einsum('bsd,ed->bse', out, wo_w) + wo_b

    def _L0_ffn_ref(x, in_proj_w, in_proj_b, out_proj_w, out_proj_b, ln1_w, ln1_b, lin1_w, lin1_b, lin2_w, lin2_b, ln2_w, ln2_b, gate_w, gate_b):
        import jax, jax.numpy as jnp
        import numpy as np
        B, S, D = (8, 128, 256)
        H = 16
        DFF = 1024
        E = 4
        K = 2
        EPS = 1e-05

        def _layernorm(x, w, b):
            m = x.mean(-1, keepdims=True)
            v = ((x - m) ** 2).mean(-1, keepdims=True)
            return (x - m) / jnp.sqrt(v + EPS) * w + b

        def _encoder_layer(x, iw, ib, ow, ob, l1w, l1b, l2w, l2b, n1w, n1b, n2w, n2b):
            b, s, d = x.shape
            hd = d // H
            qkv = x @ iw.T + ib
            q, k, v = jnp.split(qkv, 3, axis=-1)
            rs = lambda t: t.reshape(b, s, H, hd).transpose(0, 2, 1, 3)
            q, k, v = (rs(q), rs(k), rs(v))
            scale = jnp.asarray(hd, x.dtype) ** 0.5
            scores = jnp.einsum('bhqd,bhkd->bhqk', q, k) / scale
            attn = jax.nn.softmax(scores, axis=-1)
            o = jnp.einsum('bhqk,bhkd->bhqd', attn, v).transpose(0, 2, 1, 3).reshape(b, s, d)
            o = o @ ow.T + ob
            x = _layernorm(x + o, n1w, n1b)
            ff = jax.nn.relu(x @ l1w.T + l1b) @ l2w.T + l2b
            return _layernorm(x + ff, n2w, n2b)
        gate_logits = x.mean(axis=1) @ gate_w.T + gate_b
        _, top_idx = jax.lax.top_k(gate_logits, K)
        gate_weights = jax.nn.softmax(gate_logits, axis=-1)
        mask = jnp.zeros_like(gate_weights).at[jnp.arange(x.shape[0])[:, None], top_idx].set(1.0)
        expert_outs = jax.vmap(_encoder_layer, in_axes=(None, 0, 0, 0, 0, 0, 0, 0, 0, 0, 0, 0, 0))(x, in_proj_w, in_proj_b, out_proj_w, out_proj_b, lin1_w, lin1_b, lin2_w, lin2_b, ln1_w, ln1_b, ln2_w, ln2_b)
        return jnp.einsum('be,ebsd->bsd', gate_weights * mask, expert_outs)

    def _L1_attn_ref(x, W_qkv):
        import jax, jax.numpy as jnp
        import numpy as np
        D_OUT = 256
        B, N, _ = x.shape
        scale = D_OUT ** 0.5
        qkv = jnp.einsum('bnd,de->bne', x, W_qkv)
        q, k, v = jnp.split(qkv, 3, axis=-1)
        scores = jnp.einsum('bnd,bmd->bnm', q, k) / scale
        causal = jnp.triu(jnp.ones((N, N), dtype=bool), k=1)
        scores = jnp.where(causal, -jnp.inf, scores)
        attn = jax.nn.softmax(scores, axis=-1)
        return jnp.einsum('bnm,bmd->bnd', attn, v)

    def _L1_xattn_ref(q, k, v, igate_kernel, igate_bias, fgate_kernel, fgate_bias, outnorm_scale):
        import jax, jax.numpy as jnp
        import numpy as np
        B, S, H, NH = (2, 512, 256, 4)
        DH = H // NH
        EPS = 1e-06

        def _parallel_stabilized(qh, kh, vh, ig, fg):
            log_fg = jax.nn.log_sigmoid(fg)
            cs = jnp.cumsum(log_fg, axis=2)
            ltr = jnp.tril(jnp.ones((qh.shape[2], qh.shape[2]), dtype=bool))
            log_fg_mat = jnp.where(ltr, cs - jnp.swapaxes(cs, 2, 3), -jnp.inf)
            log_D = log_fg_mat + jnp.swapaxes(ig, 2, 3)
            max_log_D = jnp.max(log_D, axis=-1, keepdims=True)
            D = jnp.exp(log_D - max_log_D)
            qk = jnp.einsum('bhsd,bhtd->bhst', qh, kh) / jnp.sqrt(jnp.float32(DH))
            C = qk * D
            normalizer = jnp.maximum(jnp.abs(jnp.sum(C, axis=-1, keepdims=True)), jnp.exp(-max_log_D))
            return jnp.einsum('bhst,bhtd->bhsd', C / (normalizer + EPS), vh)
        Bq, Sq, Hq = q.shape
        x = jnp.concatenate([q, k, v], axis=-1)
        ig = x @ igate_kernel + igate_bias
        fg = x @ fgate_kernel + fgate_bias
        ig = jnp.transpose(ig, (0, 2, 1))[..., None]
        fg = jnp.transpose(fg, (0, 2, 1))[..., None]
        qh = jnp.transpose(q.reshape(Bq, Sq, NH, DH), (0, 2, 1, 3))
        kh = jnp.transpose(k.reshape(Bq, Sq, NH, DH), (0, 2, 1, 3))
        vh = jnp.transpose(v.reshape(Bq, Sq, NH, DH), (0, 2, 1, 3))
        h = _parallel_stabilized(qh, kh, vh, ig, fg)
        mean = jnp.mean(h, axis=-1, keepdims=True)
        var = jnp.mean((h - mean) ** 2, axis=-1, keepdims=True)
        h_norm = (h - mean) * jax.lax.rsqrt(var + 1e-05)
        h_norm = h_norm * outnorm_scale.reshape(1, NH, 1, DH)
        out = jnp.transpose(h_norm, (0, 2, 1, 3)).reshape(Bq, Sq, Hq)
        return out

    def _L1_ffn_ref(hidden_states, gate_w, gate_bias, expert_gate, expert_up, expert_down, shared_gate, shared_up, shared_down):
        import jax, jax.numpy as jnp
        import numpy as np
        N_EXPERTS = 32
        TOP_K = 8
        N_GROUP = 4
        TOPK_GROUP = 2
        ROUTED_SCALING = 2.5

        def _gate(x, gate_w, gate_bias):
            T, E = (x.shape[0], gate_w.shape[0])
            logits = jnp.einsum('th,eh->te', x, gate_w)
            scores = jax.nn.sigmoid(logits)
            scores_choice = scores + gate_bias[None, :]
            grp = scores_choice.reshape(T, N_GROUP, E // N_GROUP)
            top2, _ = jax.lax.top_k(grp, 2)
            group_scores = top2.sum(-1)
            _, grp_idx = jax.lax.top_k(group_scores, TOPK_GROUP)
            group_mask = jax.nn.one_hot(grp_idx, N_GROUP, dtype=scores.dtype).sum(1)
            expert_mask = jnp.repeat(group_mask, E // N_GROUP, axis=1)
            masked = jnp.where(expert_mask > 0, scores_choice, 0.0)
            _, topk_idx = jax.lax.top_k(masked, TOP_K)
            topk_w = jnp.take_along_axis(scores, topk_idx, axis=1)
            topk_w = topk_w / (topk_w.sum(-1, keepdims=True) + 1e-20)
            topk_w = topk_w * ROUTED_SCALING
            return (topk_idx, topk_w)

        def _mlp(x, wg, wu, wd):
            return jnp.einsum('...i,hi->...h', jax.nn.silu(jnp.einsum('...h,ih->...i', x, wg)) * jnp.einsum('...h,ih->...i', x, wu), wd)
        orig_shape = hidden_states.shape
        H = orig_shape[-1]
        residuals = hidden_states
        x = hidden_states.reshape(-1, H)
        topk_idx, topk_w = _gate(x, gate_w, gate_bias)
        g = jnp.einsum('th,eih->eti', x, expert_gate)
        u = jnp.einsum('th,eih->eti', x, expert_up)
        outs = jnp.einsum('eti,ehi->eth', jax.nn.silu(g) * u, expert_down)
        outs_t = jnp.transpose(outs, (1, 0, 2))
        gathered = jnp.take_along_axis(outs_t, topk_idx[:, :, None], axis=1)
        final = (gathered * topk_w[:, :, None]).sum(1)
        shared = _mlp(residuals, shared_gate, shared_up, shared_down)
        return final.reshape(orig_shape) + shared
    x = _layernorm(x + _L0_attn_ref(x, L0_attn_Wq, L0_attn_Wk, L0_attn_Wv, L0_attn_Wb, L0_attn_Wo, L0_attn_Wfd, L0_attn_bfd, L0_attn_Wsd, L0_attn_bsd, L0_attn_Wtf1, L0_attn_btf1, L0_attn_Wtf2, L0_attn_btf2), axis=-1)
    x = _layernorm(x + _L0_xattn_ref(x, ctx_1024, ctx_1024, L0_xattn_wq, L0_xattn_wk, L0_xattn_wv, L0_xattn_wo_w, L0_xattn_wo_b), axis=-1)
    x = _layernorm(x + _L0_ffn_ref(x, L0_ffn_in_proj_w, L0_ffn_in_proj_b, L0_ffn_out_proj_w, L0_ffn_out_proj_b, L0_ffn_ln1_w, L0_ffn_ln1_b, L0_ffn_lin1_w, L0_ffn_lin1_b, L0_ffn_lin2_w, L0_ffn_lin2_b, L0_ffn_ln2_w, L0_ffn_ln2_b, L0_ffn_gate_w, L0_ffn_gate_b), axis=-1)
    x = _layernorm(x + _L1_attn_ref(x, L1_attn_W_qkv), axis=-1)
    x = _layernorm(x + _L1_xattn_ref(x, ctx_1024, ctx_1024, L1_xattn_igate_kernel, L1_xattn_igate_bias, L1_xattn_fgate_kernel, L1_xattn_fgate_bias, L1_xattn_outnorm_scale), axis=-1)
    x = _layernorm(x + _L1_ffn_ref(x, L1_ffn_gate_w, L1_ffn_gate_bias, L1_ffn_expert_gate, L1_ffn_expert_up, L1_ffn_expert_down, L1_ffn_shared_gate, L1_ffn_shared_up, L1_ffn_shared_down), axis=-1)
    return x

_drawn_inputs = setup_inputs


def setup_inputs(seed=0):
    import zlib

    import numpy as np

    out = dict(_drawn_inputs(seed))
    spreads = {'L0_xattn_wo_b': (0.0, 0.1),
     'L0_ffn_ln1_w': (1.0, 0.2),
     'L0_ffn_ln1_b': (0.0, 0.288),
     'L0_ffn_ln2_w': (1.0, 0.2),
     'L0_ffn_ln2_b': (0.0, 0.286),
     'L1_xattn_outnorm_scale': (1.0, 0.2)}
    factors = {'L0_attn_Wq': 8.0,
     'L0_attn_Wk': 8.0,
     'L0_attn_Wv': 8.0,
     'L0_attn_Wb': 8.0,
     'L0_attn_Wo': 8.0,
     'L0_attn_Wfd': 8.0,
     'L0_attn_bfd': 8.0,
     'L0_attn_Wsd': 8.0,
     'L0_attn_bsd': 8.0,
     'L0_attn_Wtf1': 23.207,
     'L0_attn_btf1': 35.255,
     'L0_attn_Wtf2': 8.0,
     'L0_ffn_in_proj_w': 8.0,
     'L0_ffn_in_proj_b': 8.0,
     'L0_ffn_out_proj_w': 8.0,
     'L0_ffn_out_proj_b': 8.0,
     'L0_ffn_lin1_b': 8.0,
     'L0_ffn_lin2_b': 8.0,
     'L1_xattn_igate_bias': 64.0,
     'L1_ffn_gate_w': 6.205,
     'L1_ffn_gate_bias': 8.0,
     'L1_ffn_expert_gate': 5.409,
     'L1_ffn_expert_up': 5.346,
     'L1_ffn_expert_down': 5.345,
     'L1_ffn_shared_gate': 3.421,
     'L1_ffn_shared_up': 3.404,
     'L1_ffn_shared_down': 3.391}
    for name, (base, spread) in spreads.items():
        noise = np.random.default_rng([zlib.crc32(name.encode()), seed]).standard_normal(out[name].shape)
        drawn = base * np.exp(spread * noise) if base else spread * noise
        out[name] = jnp.asarray(drawn.astype(out[name].dtype))
    for name, factor in factors.items():
        out[name] = (out[name] * factor).astype(out[name].dtype)
    return out
```

```python
from contextlib import ExitStack

import concourse.bass as bass
from concourse import mybir

F32 = mybir.dt.float32
BF16 = mybir.dt.bfloat16
U32 = mybir.dt.uint32
ALU = mybir.AluOpType
ACT = mybir.ActivationFunctionType
AX = mybir.AxisListType

P = 128
BATCH, SEQ, DIM = 16, 256, 256
HEADS, HD = 16, 16
KT = DIM // P
PAIRS = BATCH // 2
TILES = 4
TOK = TILES * P
WINDOW = 64
EXPERTS0, DFF = 4, 1024
FB = DFF // P
EXPERTS1, INNER = 32, 128
ALL_EXPERTS = EXPERTS1 + 2
LN_EPS = 1e-5
MASKED = -1e30
FAR = -3e38
UNITS = 32


class Signal:

    def __init__(self, ctx, nc, name, per, base=0):
        self.sem = ctx.enter_context(nc.semaphore(name))
        self.per = per
        self.base = base

    def __call__(self, it, k):
        return self.sem, it * self.per + (self.base + k)

    def after(self, iterations):
        later = Signal.__new__(Signal)
        later.sem, later.per, later.base = self.sem, self.per, self.base + iterations * self.per
        return later


def build(nc, d, out):
    with ExitStack() as ctx:
        def sb(name, shape, dt=F32):
            return ctx.enter_context(nc.sbuf_tensor(name, shape, dt))

        def signal(name, per, base=0):
            return Signal(ctx, nc, name, per, base)

        PS = ctx.enter_context(nc.psum_tensor("PS", [P, 8, 512], F32))
        xs = {n: nc.dram_tensor(f"scratch_{n}", (32 * P, DIM), F32).ap() for n in ("x2", "x3", "x5")}
        xsT = {n: nc.dram_tensor(f"scratch_{n}T", (DIM, 32 * P), F32).ap() for n in ("x2", "x3", "x5")}
        route_dram = nc.dram_tensor("scratch_route", (32 * P, ALL_EXPERTS), F32).ap()

        identity = sb("identity", [P, P])
        identity16 = sb("identity16", [P, P], BF16)
        ones = sb("ones", [P, P])
        after = sb("after", [P, P])
        upto = sb("upto", [P, P])
        minus_half = sb("minus_half", [P, P])
        mean_col = sb("mean_col", [P, 1])
        eps6 = sb("eps6", [P, 1])
        window_mask = sb("window_mask", [P, 2, SEQ], BF16)
        causal_mask = sb("causal_mask", [P, 2, SEQ], BF16)
        even_rows = sb("even_rows", [P, 1])
        odd_rows = sb("odd_rows", [P, 1])
        block_diag = sb("block_diag", [P, P])
        head_rows = sb("head_rows", [4, 4, P])
        expert_index = sb("expert_index", [1, 2 * BATCH + 4], U32)
        gate_weight = sb("gate_weight", [P, 2 * BATCH + 4])

        x = sb("x", [P, TILES, DIM])
        xT = sb("xT", [P, KT, TOK])
        cT = sb("cT", [P, KT, TOK])
        c = sb("c", [P, TILES, DIM])
        qT = sb("qT", [P, KT, TOK])
        kTe = sb("kTe", [P, KT, TOK])
        kTo = sb("kTo", [P, KT, TOK])
        V1 = sb("V1", [P, TILES, HEADS, HD + 1])
        prob = sb("prob", [P, 3, 2, SEQ])
        probT = sb("probT", [P, 2, 2, 2, P])
        neg_max = sb("neg_max", [P, 4, 2])
        inv_sum = sb("inv_sum", [P, HEADS])
        o = sb("o", [P, TILES, DIM])
        oT = sb("oT", [P, KT, TOK])
        rr = sb("rr", [P, TILES, DIM])
        xn = sb("xn", [P, TILES, DIM])
        xnT = sb("xnT", [P, KT, TOK])
        xb = sb("xb", [P, TILES, DIM])
        y = sb("y", [P, TILES, DIM])
        yT = sb("yT", [P, KT, TOK])
        stats = sb("stats", [P, TILES, 6])
        mv = sb("mv", [P, TILES, 2])
        var_eps = sb("var_eps", [P, TILES])
        rstd = sb("rstd", [P, TILES])

        consts_ready = signal("consts_ready", 1)
        dve_chain = ctx.enter_context(nc.semaphore("dve_chain"))
        pool_chain = ctx.enter_context(nc.semaphore("pool_chain"))

        links = {}

        def link(eng, chain, ins):
            links[eng] = links.get(eng, 0) + 1
            ins.then_inc(chain, 1)
            eng.wait_ge(chain, links[eng])

        def restart(eng, chain):
            eng.sem_clear(chain)
            links[eng] = 0

        def tokens(t):
            return slice(t * P, (t + 1) * P)

        def attention_signals(name):
            return {k: signal(f"{name}_{k}", n) for k, n in
                    (("scores", UNITS), ("max", UNITS), ("exp", UNITS), ("turned", UNITS),
                     ("copied", UNITS), ("pv", UNITS), ("normed", 4))}

        def unit(u):
            return u // 16, (u // 8) % 2, u % 8

        def pe_attention(pe, it, a, mask):
            for u in range(UNITS + 3):
                if u < UNITS:
                    s, qt, pair = unit(u)
                    ki, r = pair // 4, 32 * (pair % 4)
                    if u >= 3:
                        pe.wait_ge(*a["exp"](it, u - 2))
                    for hh, kx in enumerate((kTe, kTo)):
                        if mask is not None:
                            pe.matmul(PS[:, u % 3, hh * SEQ:(hh + 1) * SEQ], identity16[:, :], mask[:, qt, :],
                                      start=True, stop=False)
                        last = pe.matmul(PS[:, u % 3, hh * SEQ:(hh + 1) * SEQ],
                                         qT[r:r + 32, ki, s * SEQ + qt * P:s * SEQ + (qt + 1) * P],
                                         kx[r:r + 32, ki, s * SEQ:(s + 1) * SEQ],
                                         start=(mask is None), stop=True)
                    last.then_inc(a["scores"].sem, 1)
                if 2 <= u < UNITS + 2:
                    v = u - 2
                    pe.wait_ge(*a["exp"](it, v + 1))
                    if v >= 2:
                        pe.wait_ge(*a["copied"](it, v - 1))
                    for hh in range(2):
                        for kt in range(2):
                            col = (2 * hh + kt) * P
                            last = pe.transpose(PS[:, 3 + v % 2, col:col + P],
                                                prob[:, v % 3, hh, kt * P:(kt + 1) * P], identity[:, :])
                    last.then_inc(a["turned"].sem, 1)
                if u >= 3:
                    v = u - 3
                    s, qt, pair = unit(v)
                    pe.wait_ge(*a["copied"](it, v + 1))
                    if pair == 0 and v > 0:
                        pe.wait_ge(*a["normed"](it, v // 8))
                    for hh in range(2):
                        h = 2 * pair + hh
                        for kt in range(2):
                            last = pe.matmul(PS[:, 5, h * (HD + 1):(h + 1) * (HD + 1)], probT[:, v % 2, hh, kt, :],
                                             V1[:, 2 * s + kt, h, :], start=(kt == 0), stop=(kt == 1))
                    last.then_inc(a["pv"].sem, 1)

        def act_attention(act, it, a):
            for u in range(UNITS):
                act.wait_ge(*a["max"](it, u + 1))
                if u >= 3:
                    act.wait_ge(*a["turned"](it, u - 2))
                for hh in range(2):
                    last = act.activation(prob[:, u % 3, hh, :], PS[:, u % 3, hh * SEQ:(hh + 1) * SEQ], ACT.Exp,
                                          bias=neg_max[:, u % 4, hh:hh + 1])
                last.then_inc(a["exp"].sem, 1)

        def dve_attention(dve, it, a):
            for u in range(UNITS + 3):
                if u < UNITS:
                    dve.wait_ge(*a["scores"](it, u + 1))
                    dve.tensor_reduce(neg_max[:, u % 4, :], PS[:, u % 3, :].rearrange("p (h k) -> p h k", h=2),
                                      AX.X, ALU.max, negate=True).then_inc(a["max"].sem, 1)
                if 2 <= u < UNITS + 2:
                    v = u - 2
                    dve.wait_ge(*a["turned"](it, v + 1))
                    if v >= 2:
                        dve.wait_ge(*a["pv"](it, v - 1))
                    dve.tensor_copy(probT[:, v % 2, :, :, :].rearrange("p h k q -> p (h k q)"),
                                    PS[:, 3 + v % 2, :]).then_inc(a["copied"].sem, 1)
                if u >= 3 and unit(u - 3)[2] == 7:
                    v = u - 3
                    s, qt, _ = unit(v)
                    dve.wait_ge(*a["pv"](it, v + 1))
                    heads = PS[:, 5, 0:HEADS * (HD + 1)].rearrange("p (h d) -> p h d", h=HEADS)
                    link(dve, dve_chain, dve.reciprocal(inv_sum[:, :], heads[:, :, HD]))
                    dve.tensor_tensor(o[:, 2 * s + qt, :].rearrange("p (h d) -> p h d", h=HEADS), heads[:, :, 0:HD],
                                      inv_sum[:, :].unsqueeze(2).to_broadcast([P, HEADS, HD]),
                                      ALU.mult).then_inc(a["normed"].sem, 1)

        def pe_turn(pe, src, bank, tiles=TILES):
            for t in range(tiles):
                for ki in range(KT):
                    last = pe.transpose(PS[:, bank + t // 2, ((t % 2) * 2 + ki) * P:((t % 2) * 2 + ki + 1) * P],
                                        src[:, t, ki * P:(ki + 1) * P], identity[:, :])
            return last

        def act_turned(act, dst, bank, tiles=TILES):
            for b in range(tiles // 2):
                last = act.activation(
                    dst[:, :, 2 * b * P:(2 * b + 2) * P].rearrange("p k (t j) -> p t k j", t=2),
                    PS[:, bank + b, :].rearrange("p (t k j) -> p t k j", t=2, k=2), ACT.Copy)
            return last

        def dve_stats(dve, src, ready, tiles=TILES):
            for t in range(tiles):
                ins = dve.bn_stats(stats[:, t, :], src[:, t, :])
            link(dve, dve_chain, ins)
            for t in range(tiles):
                ins = dve.bn_aggr(mv[:, t, :], stats[:, t, :])
            link(dve, dve_chain, ins)
            dve.tensor_scalar(var_eps[:, 0:tiles], mv[:, 0:tiles, 1], LN_EPS, None, ALU.add).then_inc(ready.sem, 1)

        def dve_normalise(dve, dst, src, tiles=TILES):
            for t in range(tiles):
                ins = dve.tensor_scalar(dst[:, t, :], src[:, t, :], mv[:, t, 0:1], rstd[:, t:t + 1],
                                        ALU.subtract, ALU.mult)
            return ins

        def pool_rstd(pool, it, var_ready, rstd_ready, k=1, tiles=TILES):
            pool.wait_ge(*var_ready(it, k))
            pool.tensor_tensor(rstd[:, 0:tiles], var_eps[:, 0:tiles], minus_half[:, 0:tiles], ALU.pow).then_inc(rstd_ready.sem, 1)

        phase1_buffers, phase2_buffers = ExitStack(), ExitStack()
        sb1 = lambda name, shape, dt=F32: phase1_buffers.enter_context(nc.sbuf_tensor(name, shape, dt))
        wqk = sb1("wqk", [P, KT, 2 * DIM])
        wvg = sb1("wvg", [P, KT, DIM + 48])
        wo = sb1("wo", [P, KT, DIM])
        xwq, xwk, xwv, xwo = (sb1(f"x{n}", [P, KT, DIM]) for n in ("wq", "wk", "wv", "wo"))
        wtf1 = sb1("wtf1", [P, KT, P])
        wtf2 = sb1("wtf2", [P, HEADS])
        gate0 = sb1("gate0", [P, KT, EXPERTS0])
        gate0_bias = sb1("gate0_bias", [1, EXPERTS0])
        decay_bias = sb1("decay_bias", [P, 48])
        btf1 = sb1("btf1", [P, 1])
        btf2 = sb1("btf2", [P, 1])
        nbtf1 = sb1("nbtf1", [P, 1])
        nbtf2 = sb1("nbtf2", [P, 1])
        wo_b = sb1("wo_b", [P, DIM])
        cosT = sb1("cosT", [P, TOK])
        sinT = sb1("sinT", [P, TOK])
        big = sb1("big", [P, TILES, 512])
        kw = big[:, :, :].rearrange("p t (f d) -> p t f d", f=2)
        qk = sb1("qk", [P, TILES, 512])
        vs = sb1("vs", [P, TILES, DIM])
        qkT = sb1("qkT", [P, 4, TOK])
        gate_sb = sb1("gate_sb", [P, TILES, 48])
        gate_exp = sb1("gate_exp", [P, TILES, 48])
        sig = sb1("sig", [P, TILES, 48])
        log_decay = sb1("log_decay", [P, TILES, 32])
        decay = sb1("decay", [P, TILES, 32])
        sumsq = sb1("sumsq", [P, P])
        inv_norm = sb1("inv_norm", [P, P])
        inv_decay_sum = sb1("inv_decay_sum", [P, 64])
        memory = sb1("memory", [P, 2, 2, KT, P])
        hid_exp = sb1("hid_exp", [P, TOK])
        hid = sb1("hid", [P, TOK])
        flux = sb1("flux", [P, TILES * HEADS])
        alpha = sb1("alpha", [P, TILES, HEADS])
        one_minus = sb1("one_minus", [P, TILES, HEADS])
        rope_a = sb1("rope_a", [P, TOK])
        rope_b = sb1("rope_b", [P, TOK])
        meanT = sb1("meanT", [P, 4])
        logits8 = sb1("logits8", [1, 2, 8])
        top8 = sb1("top8", [1, 2, 8])
        top8_index = sb1("top8_index", [1, 2, 8], U32)
        neg_top = sb1("neg_top", [1, 2])
        logit_exp = sb1("logit_exp", [1, 2, 6])
        logit_sum = sb1("logit_sum", [1, 2])
        chosen_weight = sb1("chosen_weight", [1, 4])

        weights1_loaded = signal("weights1_loaded", 0)
        in1 = signal("in1", 48)
        one = {n: signal(f"l0_{n}", 1) for n in (
            "qkvg", "sq", "gz", "gexp", "sumsq", "rnorm", "sig", "kb", "logd", "suffix", "decay", "turned", "qkT",
            "kw", "mem", "memory", "hid", "hexp", "hidden", "flux", "fexp", "o_ps", "o", "oturned", "oT", "y",
            "var", "rstd", "x1", "x1turned", "x1T", "kv", "kT", "V1", "q", "qT",
            "oturned2", "oT2", "y2", "x1b", "var2", "rstd2", "x2", "x2turned", "x2T", "mean", "meanT",
            "logits", "top", "lexp", "chosen", "spread", "chosen_out")}
        att1 = attention_signals("att")
        stored1 = signal("stored1", 32, base=32)

        mask_stage = [big[:, n, :].rearrange("p (t k) -> p t k", t=2) for n in range(2)]
        X1_WEIGHTS = [(wqk, "wqk"), (wvg, "wvg"), (wo, "wo"), (xwq, "xwq"), (xwk, "xwk"), (xwv, "xwv"), (xwo, "xwo"),
                      (wtf1, "wtf1"), (wtf2, "wtf2"), (gate0, "gate0"), (gate0_bias, "gate0_bias"),
                      (decay_bias, "decay_bias"), (btf1, "btf1"), (btf2, "btf2"), (wo_b, "wo_b"),
                      (cosT, "cosT"), (sinT, "sinT"), (even_rows, "even_rows"), (odd_rows, "odd_rows"),
                      (block_diag, "block_diag"), (head_rows, "head_rows"), (identity, "identity"),
                      (after, "after"), (upto, "upto"), (mask_stage[0], "window_mask"), (mask_stage[1], "causal_mask")]
        WEIGHTS1 = 16 * len(X1_WEIGHTS)

        def rows(ap, it, n):
            return ap[bass.ds(it * (n * P), n * P), :].rearrange("(t p) f -> p t f", p=P)

        def columns(ap, it, n):
            return ap[:, bass.ds(it * n * P, n * P)].rearrange("(k p) t -> p k t", p=P)

        def sp_load1(sp, it):
            sp.dma_start(xT[:, :, :], columns(d["xT"], it, TILES)).then_inc(in1.sem, 16)
            sp.dma_start(cT[:, :, :], columns(d["ctxT"], it, TILES)).then_inc(in1.sem, 16)
            sp.dma_start(x[:, :, :], rows(d["x"], it, TILES)).then_inc(in1.sem, 16)

        def sp_store1(sp, it):
            sp.wait_ge(*one["x2"](it, 1))
            sp.dma_start(rows(xs["x2"], it, TILES), y[:, :, :]).then_inc(stored1.sem, 16)
            sp.wait_ge(*one["x2T"](it, 1))
            sp.dma_start(columns(xsT["x2"], it, TILES), yT[:, :, :]).then_inc(stored1.sem, 16)

        def sp_phase1(sp):
            sp.sem_inc(stored1.sem, 32)
            for dst, name in X1_WEIGHTS:
                sp.dma_start(dst[tuple(slice(None) for _ in dst.shape)], d[name]).then_inc(weights1_loaded.sem, 16)
            sp_load1(sp, 0)
            with sp.Fori(0, PAIRS - 1) as it:
                sp.wait_ge(*one["x1"](it, 1))
                sp.wait_ge(*one["kv"](it, 1))
                sp_load1(sp, it + 1)
                sp_store1(sp, it)
            sp_store1(sp, PAIRS - 1)
            sp.wait_ge(*stored1(PAIRS - 1, 32))

        def pe_phase1(pe):
            pe.wait_ge(weights1_loaded.sem, WEIGHTS1)
            pe.wait_ge(*consts_ready(0, 1))
            with pe.Fori(0, PAIRS) as it:
                pe.wait_ge(*in1(it, 48))
                for t in range(TILES):
                    for ki in range(KT):
                        pe.matmul(PS[:, t, :], xT[:, ki, tokens(t)], wqk[:, ki, :], start=(ki == 0), stop=(ki == 1))
                    for ki in range(KT):
                        last = pe.matmul(PS[:, 4 + t, 0:DIM + 48], xT[:, ki, tokens(t)], wvg[:, ki, :],
                                         start=(ki == 0), stop=(ki == 1))
                last.then_inc(one["qkvg"].sem, 1)
                pe.wait_ge(*one["kb"](it, 1))
                pe.wait_ge(*one["logd"](it, 1))
                for s in range(2):
                    first, second = log_decay[:, 2 * s, :], log_decay[:, 2 * s + 1, :]
                    pe.matmul(PS[:, 0, 64 * s:64 * s + 32], after[:, :], first, start=True, stop=False)
                    pe.matmul(PS[:, 0, 64 * s:64 * s + 32], ones[:, :], second, start=False, stop=True)
                    last = pe.matmul(PS[:, 0, 64 * s + 32:64 * s + 64], after[:, :], second, start=True, stop=True)
                last.then_inc(one["suffix"].sem, 1)
                for t in range(TILES):
                    for cc in range(4):
                        last = pe.transpose(PS[:, 1 + t, cc * P:(cc + 1) * P], qk[:, t, cc * P:(cc + 1) * P],
                                            identity[:, :])
                last.then_inc(one["turned"].sem, 1)
                pe.wait_ge(*one["kw"](it, 1))
                for s in range(2):
                    for tt in range(2):
                        pe.matmul(PS[:, 7, 32 * s:32 * s + 32], ones[:, :], decay[:, 2 * s + tt, :],
                                  start=(tt == 0), stop=(tt == 1))
                    for fs in range(2):
                        for half in range(KT):
                            for tt in range(2):
                                last = pe.matmul(PS[:, 5 + s, (fs * 2 + half) * P:(fs * 2 + half + 1) * P],
                                                 kw[:, 2 * s + tt, fs, half * P:(half + 1) * P],
                                                 vs[:, 2 * s + tt, half * P:(half + 1) * P],
                                                 start=(tt == 0), stop=(tt == 1))
                last.then_inc(one["mem"].sem, 1)
                pe.wait_ge(*one["decay"](it, 1))
                pe.wait_ge(*one["qkT"](it, 1))
                for ki in range(KT):
                    last = pe.matmul(PS[:, 0, :], wtf1[:, ki, :], qkT[:, 2 + ki, :], start=(ki == 0), stop=(ki == 1))
                last.then_inc(one["hid"].sem, 1)
                pe.wait_ge(*one["hidden"](it, 1))
                for t in range(TILES):
                    last = pe.matmul(PS[:, 1, t * HEADS:(t + 1) * HEADS], hid[:, tokens(t)], wtf2[:, :],
                                     start=True, stop=True)
                last.then_inc(one["flux"].sem, 1)
                pe.wait_ge(*one["memory"](it, 1))
                for t in range(TILES):
                    for half in range(KT):
                        last = pe.matmul(PS[:, 2 + t, half * 2 * P:(half + 1) * 2 * P], qkT[:, half, tokens(t)],
                                         memory[:, t // 2, :, half, :],
                                         start=True, stop=True)
                last.then_inc(one["o_ps"].sem, 1)
                pe.wait_ge(*one["o"](it, 1))
                pe_turn(pe, o, 6).then_inc(one["oturned"].sem, 1)
                for blk in range(2):
                    for ki in range(KT):
                        pe.matmul(PS[:, 4 + blk, :], xwk[:, ki, blk * P:(blk + 1) * P], cT[:, ki, :],
                                  start=(ki == 0), stop=(ki == 1))
                for t in range(TILES):
                    for ki in range(KT):
                        last = pe.matmul(PS[:, 2 + t // 2, (t % 2) * DIM:(t % 2 + 1) * DIM], cT[:, ki, tokens(t)],
                                         xwv[:, ki, :], start=(ki == 0), stop=(ki == 1))
                last.then_inc(one["kv"].sem, 1)
                pe.wait_ge(*one["oT"](it, 1))
                for t in range(TILES):
                    for ki in range(KT):
                        last = pe.matmul(PS[:, t // 2, (t % 2) * DIM:(t % 2 + 1) * DIM], oT[:, ki, tokens(t)],
                                         wo[:, ki, :], start=(ki == 0), stop=(ki == 1))
                last.then_inc(one["y"].sem, 1)
                pe.wait_ge(*one["x1"](it, 1))
                pe_turn(pe, xn, 6).then_inc(one["x1turned"].sem, 1)
                pe.wait_ge(*one["x1T"](it, 1))
                for blk in range(2):
                    for ki in range(KT):
                        last = pe.matmul(PS[:, blk, :], xwq[:, ki, blk * P:(blk + 1) * P], xnT[:, ki, :],
                                         start=(ki == 0), stop=(ki == 1))
                last.then_inc(one["q"].sem, 1)
                pe.wait_ge(*one["V1"](it, 1))
                pe.wait_ge(*one["qT"](it, 1))
                pe_attention(pe, it, att1, window_mask)
                pe.wait_ge(*att1["normed"](it, 4))
                pe_turn(pe, o, 6).then_inc(one["oturned2"].sem, 1)
                pe.wait_ge(*one["oT2"](it, 1))
                for t in range(TILES):
                    for ki in range(KT):
                        last = pe.matmul(PS[:, t // 2, (t % 2) * DIM:(t % 2 + 1) * DIM], oT[:, ki, tokens(t)],
                                         xwo[:, ki, :], start=(ki == 0), stop=(ki == 1))
                last.then_inc(one["y2"].sem, 1)
                pe.wait_ge(*one["x2"](it, 1))
                pe_turn(pe, y, 6).then_inc(one["x2turned"].sem, 1)
                for s in range(2):
                    for half in range(KT):
                        for tt in range(2):
                            last = pe.matmul(PS[:, 4, s * 2 + half:s * 2 + half + 1],
                                             y[:, 2 * s + tt, half * P:(half + 1) * P], mean_col[:, :],
                                             start=(tt == 0), stop=(tt == 1))
                last.then_inc(one["mean"].sem, 1)
                pe.wait_ge(*one["meanT"](it, 1))
                for s in range(2):
                    for ki in range(KT):
                        last = pe.matmul(PS[0:1, 5, s * 8:s * 8 + EXPERTS0], meanT[:, s * 2 + ki:s * 2 + ki + 1],
                                         gate0[:, ki, :], start=(ki == 0), stop=(ki == 1))
                last.then_inc(one["logits"].sem, 1)
                pe.wait_ge(*one["chosen"](it, 1))
                pe.matmul(PS[:, 4, 0:4], ones[0:1, :], chosen_weight[:, :], start=True, stop=True)\
                    .then_inc(one["spread"].sem, 1)
                pe.wait_ge(*one["x2T"](it, 1))
                pe.wait_ge(*one["chosen_out"](it, 1))

        def act_phase1(act):
            act.wait_ge(weights1_loaded.sem, WEIGHTS1)
            act.wait_ge(*consts_ready(0, 1))
            with act.Fori(0, PAIRS) as it:
                act.wait_ge(*one["qkvg"](it, 1))
                act.activation(big[:, :, :], PS[:, 0:4, :], ACT.Square).then_inc(one["sq"].sem, 1)
                act.wait_ge(*one["gz"](it, 1))
                act.activation(gate_exp[:, :, :], gate_sb[:, :, :], ACT.Exp, scale=-1.0).then_inc(one["gexp"].sem, 1)
                act.wait_ge(*one["sig"](it, 1))
                act.activation(log_decay[:, :, :], sig[:, :, 16:48], ACT.Ln, bias=eps6[:, :])\
                    .then_inc(one["logd"].sem, 1)
                act.wait_ge(*one["suffix"](it, 1))
                act.activation(decay[:, :, :], PS[:, 0, 0:128].rearrange("p (t h) -> p t h", t=TILES), ACT.Exp)\
                    .then_inc(one["decay"].sem, 1)
                act.wait_ge(*one["turned"](it, 1))
                act.activation(qkT[:, :, :].rearrange("p c (t j) -> p t c j", t=TILES),
                               PS[:, 1:5, :].rearrange("p t (c j) -> p t c j", c=4), ACT.Copy)\
                    .then_inc(one["qkT"].sem, 1)
                act.wait_ge(*one["hid"](it, 1))
                act.activation(hid_exp[:, :], PS[:, 0, :], ACT.Exp, bias=nbtf1[:, :], scale=-1.0)\
                    .then_inc(one["hexp"].sem, 1)
                act.wait_ge(*one["flux"](it, 1))
                act.activation(flux[:, :], PS[:, 1, 0:64], ACT.Exp, bias=nbtf2[:, :], scale=-1.0)\
                    .then_inc(one["fexp"].sem, 1)
                act.wait_ge(*one["oturned"](it, 1))
                act_turned(act, oT, 6).then_inc(one["oT"].sem, 1)
                act.wait_ge(*one["kv"](it, 1))
                for b in range(2):
                    last = act.activation(V1[:, 2 * b:2 * b + 2, :, 0:HD],
                                          PS[:, 2 + b, :].rearrange("p (t h e) -> p t h e", t=2, h=HEADS), ACT.Copy)
                last.then_inc(one["V1"].sem, 1)
                act.wait_ge(*one["x1turned"](it, 1))
                act_turned(act, xnT, 6).then_inc(one["x1T"].sem, 1)
                act_attention(act, it, att1)
                act.wait_ge(*one["oturned2"](it, 1))
                act_turned(act, oT, 6).then_inc(one["oT2"].sem, 1)
                act.wait_ge(*one["x2turned"](it, 1))
                act.wait_ge(*stored1(it, 0))
                act_turned(act, yT, 6).then_inc(one["x2T"].sem, 1)
                act.wait_ge(*one["top"](it, 1))
                for s in range(2):
                    act.activation(logit_exp[:, s, 0:EXPERTS0], logits8[:, s, 0:EXPERTS0], ACT.Exp,
                                   bias=neg_top[:, s:s + 1], accum_out=logit_sum[:, s:s + 1])
                    last = act.activation(logit_exp[:, s, 4:6], top8[:, s, 0:2], ACT.Exp, bias=neg_top[:, s:s + 1])
                last.then_inc(one["lexp"].sem, 1)

        def dve_phase1(dve):
            dve.wait_ge(weights1_loaded.sem, WEIGHTS1)
            link(dve, dve_chain, dve.memset(V1[:, :, :, :], 1.0))
            dve.memset(logits8[:, :, :], FAR)
            dve.tensor_scalar(nbtf1[:, :], btf1[:, :], -1.0, None, ALU.mult)
            link(dve, dve_chain, dve.tensor_scalar(nbtf2[:, :], btf2[:, :], -1.0, None, ALU.mult))
            dve.memset(eps6[:, :], 1e-6)
            dve.tensor_copy(window_mask[:, :, :], mask_stage[0])
            dve.tensor_copy(causal_mask[:, :, :], mask_stage[1])
            dve.tensor_copy(identity16[:, :], identity[:, :])
            dve.memset(mean_col[:, :], 1.0 / SEQ)
            dve.memset(minus_half[:, :], -0.5)
            dve.memset(ones[:, :], 1.0).then_inc(consts_ready.sem, 1)
            dve.wait_ge(*consts_ready(0, 1))
            with dve.Fori(0, PAIRS) as it:
                restart(dve, dve_chain)
                heads = lambda ap: ap.rearrange("p t (h e) -> p t h e", e=HD)
                spread = lambda ap: ap.unsqueeze(3).to_broadcast([P, TILES, HEADS, HD])
                dve.wait_ge(*one["qkvg"](it, 1))
                dve.tensor_tensor(gate_sb[:, :, :], PS[:, 4:8, DIM:DIM + 48],
                                  decay_bias[:, :].unsqueeze(1).to_broadcast([P, TILES, 48]),
                                  ALU.add).then_inc(one["gz"].sem, 1)
                dve.wait_ge(*one["sq"](it, 1))
                link(dve, dve_chain, dve.tensor_reduce(sumsq[:, :], big[:, :, :].rearrange("p t (h e) -> p (t h) e", e=HD),
                                                       AX.X, ALU.add))
                dve.tensor_scalar(sumsq[:, :], sumsq[:, :], 1e-24, None, ALU.max).then_inc(one["sumsq"].sem, 1)
                dve.wait_ge(*one["gexp"](it, 1))
                link(dve, dve_chain, dve.tensor_scalar(gate_exp[:, :, :], gate_exp[:, :, :], 1.0, None, ALU.add))
                dve.reciprocal(sig[:, :, :], gate_exp[:, :, :]).then_inc(one["sig"].sem, 1)
                dve.wait_ge(*one["sig"](it, 1))
                dve.tensor_tensor(heads(vs[:, :, :]), heads(PS[:, 4:8, 0:DIM]), spread(sig[:, :, 0:HEADS]), ALU.mult)
                dve.wait_ge(*one["rnorm"](it, 1))
                link(dve, dve_chain, dve.tensor_tensor(
                    qk[:, :, :].rearrange("p t (h e) -> p (t h) e", e=HD),
                    PS[:, 0:4, :].rearrange("p t (h e) -> p (t h) e", e=HD),
                    inv_norm[:, :].unsqueeze(2).to_broadcast([P, P, HD]), ALU.mult))
                kbeta = heads(qk[:, :, DIM:2 * DIM])
                dve.tensor_tensor(kbeta, kbeta, spread(sig[:, :, 0:HEADS]), ALU.mult).then_inc(one["kb"].sem, 1)
                dve.wait_ge(*one["kb"](it, 1))
                dve.wait_ge(*one["decay"](it, 1))
                for fs in range(2):
                    last = dve.tensor_tensor(heads(kw[:, :, fs, :]), kbeta,
                                             spread(decay[:, :, fs * HEADS:(fs + 1) * HEADS]), ALU.mult)
                last.then_inc(one["kw"].sem, 1)
                dve.wait_ge(*one["mem"](it, 1))
                link(dve, dve_chain, dve.tensor_scalar(inv_decay_sum[:, :], PS[:, 7, 0:64], 1e-6, None, ALU.add))
                link(dve, dve_chain, dve.reciprocal(inv_decay_sum[:, :], inv_decay_sum[:, :]))
                for s in range(2):
                    scaled = memory[:, s, :, :, :].rearrange("p f k (h e) -> p (f k h) e", e=HD)
                    flat_memory = memory[:, s, :, :, :].rearrange("p f k e -> p (f k) e")
                    link(dve, dve_chain, dve.tensor_tensor(
                        scaled, PS[:, 5 + s, :].rearrange("p (g e) -> p g e", e=HD),
                        inv_decay_sum[:, 32 * s:32 * s + 32].unsqueeze(2).to_broadcast([P, 32, HD]), ALU.mult))
                    last = dve.tensor_tensor(flat_memory, flat_memory,
                                             block_diag[:, :].unsqueeze(1).to_broadcast([P, 4, P]), ALU.mult)
                last.then_inc(one["memory"].sem, 1)
                dve.wait_ge(*one["hexp"](it, 1))
                link(dve, dve_chain, dve.tensor_scalar(hid_exp[:, :], hid_exp[:, :], 1.0, None, ALU.add))
                link(dve, dve_chain, dve.reciprocal(hid_exp[:, :], hid_exp[:, :]))
                dve.scalar_tensor_tensor(out=hid[:, :], in0=PS[:, 0, :], scalar=btf1[:, :], in1=hid_exp[:, :],
                                         op0=ALU.add, op1=ALU.mult).then_inc(one["hidden"].sem, 1)
                dve.wait_ge(*one["fexp"](it, 1))
                link(dve, dve_chain, dve.tensor_scalar(flux[:, :], flux[:, :], 1.0, None, ALU.add))
                link(dve, dve_chain, dve.reciprocal(flux[:, :], flux[:, :]))
                link(dve, dve_chain, dve.tensor_scalar(flux[:, :], flux[:, :], 0.01, 0.99, ALU.max, ALU.min))
                flat = lambda ap: ap.rearrange("p t h -> p (t h)")
                link(dve, dve_chain, dve.tensor_scalar(flat(alpha[:, :, :]), flux[:, :], 0.3, 0.5, ALU.mult, ALU.add))
                link(dve, dve_chain, dve.tensor_scalar(flat(one_minus[:, :, :]), flat(alpha[:, :, :]), -1.0, 1.0,
                                                       ALU.mult, ALU.add))
                dve.wait_ge(*one["o_ps"](it, 1))
                for t in range(TILES):
                    for fs, (dst, w) in enumerate(((o, alpha), (rr, one_minus))):
                        last = dve.tensor_tensor(
                            dst[:, t, :].rearrange("p (k h e) -> p k h e", k=KT, e=HD),
                            PS[:, 2 + t, :].rearrange("p (k f h e) -> p k f h e", k=KT, f=2, e=HD)[:, :, fs, :, :],
                            w[:, t, :].rearrange("p (k h) -> p k h", k=KT).unsqueeze(3).to_broadcast([P, KT, 8, HD]),
                            ALU.mult)
                link(dve, dve_chain, last)
                dve.tensor_tensor(o[:, :, :], o[:, :, :], rr[:, :, :], ALU.add).then_inc(one["o"].sem, 1)

                def rope(pa, pb, scale, outs):
                    for sign, first, second, blk in ((ALU.subtract, cosT, sinT, 0), (ALU.add, sinT, cosT, 1)):
                        dve.scalar_tensor_tensor(out=rope_a[:, :], in0=pa, scalar=scale, in1=first[:, :],
                                                 op0=ALU.mult, op1=ALU.mult)
                        link(dve, dve_chain, dve.scalar_tensor_tensor(out=rope_b[:, :], in0=pb, scalar=scale,
                                                                      in1=second[:, :], op0=ALU.mult, op1=ALU.mult))
                        if len(outs) == 1:
                            last = dve.tensor_tensor(outs[0][0][:, blk, :], rope_a[:, :], rope_b[:, :], sign)
                            link(dve, dve_chain, last)
                            continue
                        link(dve, dve_chain, dve.tensor_tensor(rope_a[:, :], rope_a[:, :], rope_b[:, :], sign))
                        for dst, rows_kept in outs:
                            last = dve.tensor_scalar(dst[:, blk, :], rope_a[:, :], rows_kept[:, :], None, ALU.mult)
                        link(dve, dve_chain, last)

                dve.wait_ge(*one["kv"](it, 1))
                rope(PS[:, 4, :], PS[:, 5, :], 1.0, ((kTe, even_rows), (kTo, odd_rows)))
                pair2 = lambda b: PS[:, b:b + 2, :].rearrange("p b (t f) -> p (b t) f", t=2)
                dve.wait_ge(*one["y"](it, 1))
                link(dve, dve_chain, dve.tensor_tensor(rr[:, :, :], pair2(0), x[:, :, :], ALU.add))
                dve_stats(dve, rr, one["var"])
                dve.wait_ge(*one["rstd"](it, 1))
                dve_normalise(dve, xn, rr).then_inc(one["x1"].sem, 1)
                dve.wait_ge(*one["q"](it, 1))
                rope(PS[:, 0, :], PS[:, 1, :], float(HD) ** 0.5, ((qT, None),))
                dve.sem_inc(one["qT"].sem, 1)
                dve_attention(dve, it, att1)
                dve.wait_ge(*one["y2"](it, 1))
                dve.wait_ge(*one["x1b"](it, 1))
                link(dve, dve_chain, dve.tensor_tensor(rr[:, :, :], pair2(0), xb[:, :, :], ALU.add))
                dve_stats(dve, rr, one["var2"])
                dve.wait_ge(*one["rstd2"](it, 1))
                dve.wait_ge(*stored1(it, 0))
                dve_normalise(dve, y, rr).then_inc(one["x2"].sem, 1)
                dve.wait_ge(*one["mean"](it, 1))
                dve.tensor_copy(meanT[:, :], PS[:, 4, 0:4]).then_inc(one["meanT"].sem, 1)
                dve.wait_ge(*one["logits"](it, 1))
                link(dve, dve_chain, dve.tensor_tensor(
                    logits8[:, :, 0:EXPERTS0], PS[0:1, 5, 0:16].rearrange("p (s e) -> p s e", s=2)[:, :, 0:EXPERTS0],
                    gate0_bias[:, :].unsqueeze(1).to_broadcast([1, 2, EXPERTS0]), ALU.add))
                for s in range(2):
                    last = dve.max(top8[:, s, :], logits8[:, s, :])
                link(dve, dve_chain, last)
                dve.tensor_scalar(neg_top[:, :], top8[:, :, 0], -1.0, None, ALU.mult).then_inc(one["top"].sem, 1)
                for s in range(2):
                    last = dve.max_index(top8_index[:, s, :], top8[:, s, :], logits8[:, s, :])
                link(dve, dve_chain, last)
                dve.tensor_copy(expert_index[:, bass.ds(it * 4, 4)].rearrange("p (s e) -> p s e", s=2),
                                top8_index[:, :, 0:2])
                dve.wait_ge(*one["lexp"](it, 1))
                link(dve, dve_chain, dve.reciprocal(logit_sum[:, :], logit_sum[:, :]))
                dve.tensor_tensor(chosen_weight[:, :].rearrange("p (s e) -> p s e", s=2), logit_exp[:, :, 4:6],
                                  logit_sum[:, :].unsqueeze(2).to_broadcast([1, 2, 2]),
                                  ALU.mult).then_inc(one["chosen"].sem, 1)
                dve.wait_ge(*one["spread"](it, 1))
                dve.tensor_copy(gate_weight[:, bass.ds(it * 4, 4)], PS[:, 4, 0:4]).then_inc(one["chosen_out"].sem, 1)
                dve.wait_ge(*one["chosen_out"](it, 1))

        def pool_phase1(pool):
            pool.wait_ge(weights1_loaded.sem, WEIGHTS1)
            pool.wait_ge(*consts_ready(0, 1))
            with pool.Fori(0, PAIRS) as it:
                pool.wait_ge(*one["sumsq"](it, 1))
                pool.tensor_tensor(inv_norm[:, :], sumsq[:, :], minus_half[:, :], ALU.pow).then_inc(one["rnorm"].sem, 1)
                pool_rstd(pool, it, one["var"], one["rstd"])
                pool.wait_ge(*one["x1"](it, 1))
                pool.tensor_tensor(xb[:, :, :], xn[:, :, :], wo_b[:, :].unsqueeze(1).to_broadcast([P, TILES, DIM]),
                                   ALU.add).then_inc(one["x1b"].sem, 1)
                pool_rstd(pool, it, one["var2"], one["rstd2"])

        phase1_buffers.close()
        ctx.enter_context(phase2_buffers)
        sb2 = lambda name, shape, dt=F32: phase2_buffers.enter_context(nc.sbuf_tensor(name, shape, dt))
        W_QKV, W_OUT, W_UP, W_DOWN = 2 * 768 + DIM + 4, 2 * DIM + 3 * DIM, KT * DFF + FB, FB * DIM + 3 * DIM
        w_qkv = sb2("w_qkv", [P, 2, W_QKV])
        w_out = sb2("w_out", [P, 2, W_OUT])
        w_up = sb2("w_up", [P, 2, W_UP])
        w_down = sb2("w_down", [P, 2, W_DOWN])
        hT = sb2("hT", [P, 2, FB, SEQ])

        in2 = signal("in2", 16)
        in2x = signal("in2x", 16)
        loaded2 = {n: signal(f"{n}_loaded", 32) for n in ("qkv", "out", "up", "down")}
        two = {n: signal(f"f_{n}", per) for n, per in (
            ("qkv", 2), ("in", 2), ("xb", 1), ("oturned", 1), ("oT", 1), ("y", 1), ("var", 3), ("rstd", 3), ("xp", 1),
            ("xpb", 1), ("xpturned", 1), ("xpT", 1), ("h", 8), ("h_act", 4), ("h_dve", 4), ("y2", 1),
            ("x3", 1), ("x3turned", 1), ("x3T", 1), ("normed2", 1))}
        att2 = {k: s.after(PAIRS) for k, s in att1.items()}
        stored2 = signal("stored2", 32, base=32)
        PIECES = (("qkv", w_qkv, "f_qkv"), ("out", w_out, "f_out"), ("up", w_up, "f_up"), ("down", w_down, "f_down"))

        def sp_piece(sp, it, expert, n):
            name, dst, src = PIECES[n]
            for e in range(2):
                sp.dma_start(dst[:, e, :], d[src][bass.ds(expert[e], 1), :, :].rearrange("a p n -> p (a n)"))\
                    .then_inc(loaded2[name].sem, 16)

        def sp_experts(sp, it):
            return [sp.value_load(expert_index[0:1, bass.ds(it * 2 + e, 1)], min_val=0, max_val=EXPERTS0 - 1)
                    for e in range(2)]

        def sp_store2(sp, it):
            sp.wait_ge(*two["x3"](it, 1))
            sp.dma_start(rows(xs["x3"], it, 2), y[:, 0:2, :]).then_inc(stored2.sem, 16)
            sp.wait_ge(*two["x3T"](it, 1))
            sp.dma_start(columns(xsT["x3"], it, 2), yT[:, :, 0:SEQ]).then_inc(stored2.sem, 16)

        def sp_phase2(sp):
            sp.sem_inc(stored2.sem, 32)
            sp.wait_ge(*one["chosen_out"](PAIRS - 1, 1))
            sp.dma_start(xT[:, :, 0:SEQ], columns(xsT["x2"], 0, 2)).then_inc(in2.sem, 16)
            sp.dma_start(x[:, 0:2, :], rows(xs["x2"], 0, 2)).then_inc(in2x.sem, 16)
            expert = sp_experts(sp, 0)
            for n in range(4):
                sp_piece(sp, 0, expert, n)
            with sp.Fori(0, BATCH - 1) as it:
                expert = sp_experts(sp, it + 1)
                sp.wait_ge(*two["qkv"](it, 2))
                sp.wait_ge(*two["in"](it, 2))
                sp.dma_start(xT[:, :, 0:SEQ], columns(xsT["x2"], it + 1, 2)).then_inc(in2.sem, 16)
                sp_piece(sp, it + 1, expert, 0)
                sp.wait_ge(*two["xp"](it, 1))
                sp_piece(sp, it + 1, expert, 1)
                sp.wait_ge(*two["h_act"](it, 4))
                sp.wait_ge(*two["h_dve"](it, 4))
                sp_piece(sp, it + 1, expert, 2)
                sp.wait_ge(*two["normed2"](it, 1))
                sp_piece(sp, it + 1, expert, 3)
                sp.dma_start(x[:, 0:2, :], rows(xs["x2"], it + 1, 2)).then_inc(in2x.sem, 16)
                sp_store2(sp, it)
            sp_store2(sp, BATCH - 1)
            sp.wait_ge(*stored2(BATCH - 1, 32))

        def pe_phase2(pe):
            with pe.Fori(0, BATCH) as it:
                pe.wait_ge(*in2(it, 16))
                pe.wait_ge(*loaded2["qkv"](it, 32))
                for e in range(2):
                    for blk in range(4):
                        for ki in range(KT):
                            pe.matmul(PS[:, 2 * e + blk // 2, (blk % 2) * SEQ:(blk % 2 + 1) * SEQ],
                                      w_qkv[:, e, ki * 768 + blk * P:ki * 768 + (blk + 1) * P], xT[:, ki, 0:SEQ],
                                      start=(ki == 0), stop=(ki == 1))
                    for tt in range(2):
                        for ki in range(KT):
                            last = pe.matmul(PS[:, 4 + e, tt * DIM:(tt + 1) * DIM], xT[:, ki, tokens(tt)],
                                             w_qkv[:, e, ki * 768 + 2 * DIM:ki * 768 + 3 * DIM],
                                             start=(ki == 0), stop=(ki == 1))
                    last.then_inc(two["qkv"].sem, 1)
                pe.wait_ge(*two["in"](it, 2))
                pe_attention(pe, it, att2, None)
                pe.wait_ge(*att2["normed"](it, 4))
                pe_turn(pe, o, 6).then_inc(two["oturned"].sem, 1)
                pe.wait_ge(*loaded2["out"](it, 32))
                pe.wait_ge(*two["oT"](it, 1))
                for t in range(TILES):
                    for ki in range(KT):
                        last = pe.matmul(PS[:, t // 2, (t % 2) * DIM:(t % 2 + 1) * DIM], oT[:, ki, tokens(t)],
                                         w_out[:, t // 2, ki * DIM:(ki + 1) * DIM], start=(ki == 0), stop=(ki == 1))
                last.then_inc(two["y"].sem, 1)
                pe.wait_ge(*two["xp"](it, 1))
                pe_turn(pe, xn, 6).then_inc(two["xpturned"].sem, 1)
                pe.wait_ge(*loaded2["up"](it, 32))
                pe.wait_ge(*two["xpT"](it, 1))
                for e in range(2):
                    for blk in range(FB):
                        for ki in range(KT):
                            last = pe.matmul(PS[:, 4 * e + blk // 2, (blk % 2) * SEQ:(blk % 2 + 1) * SEQ],
                                             w_up[:, e, ki * DFF + blk * P:ki * DFF + (blk + 1) * P],
                                             xnT[:, ki, e * SEQ:(e + 1) * SEQ], start=(ki == 0), stop=(ki == 1))
                        if blk % 2:
                            last.then_inc(two["h"].sem, 1)
                pe.wait_ge(*loaded2["down"](it, 32))
                for e in range(2):
                    pe.wait_ge(*two["h_act"](it, 2 * (e + 1)))
                    pe.wait_ge(*two["h_dve"](it, 2 * (e + 1)))
                    for tt in range(2):
                        for ki in range(FB):
                            last = pe.matmul(PS[:, 4 * e, tt * DIM:(tt + 1) * DIM], hT[:, e, ki, tokens(tt)],
                                             w_down[:, e, ki * DIM:(ki + 1) * DIM], start=(ki == 0), stop=(ki == FB - 1))
                last.then_inc(two["y2"].sem, 1)
                pe.wait_ge(*two["x3"](it, 1))
                pe_turn(pe, y, 6, 2).then_inc(two["x3turned"].sem, 1)

        def act_phase2(act):
            with act.Fori(0, BATCH) as it:
                act_attention(act, it, att2)
                act.wait_ge(*two["oturned"](it, 1))
                act_turned(act, oT, 6).then_inc(two["oT"].sem, 1)
                act.wait_ge(*two["xpturned"](it, 1))
                act_turned(act, xnT, 6).then_inc(two["xpT"].sem, 1)
                for b in range(0, 8, 2):
                    act.wait_ge(*two["h"](it, b + 1))
                    for j in range(2):
                        e, blk = b // 4, 2 * (b % 4) + j
                        last = act.activation(hT[:, e, blk, :], PS[:, b, j * SEQ:(j + 1) * SEQ], ACT.Relu,
                                              bias=w_up[:, e, KT * DFF + blk:KT * DFF + blk + 1])
                    last.then_inc(two["h_act"].sem, 1)
                act.wait_ge(*two["x3turned"](it, 1))
                act.wait_ge(*stored2(it, 0))
                act_turned(act, yT, 6, 2).then_inc(two["x3T"].sem, 1)

        def dve_phase2(dve):
            with dve.Fori(0, BATCH) as it:
                restart(dve, dve_chain)
                bias0 = 2 * 768 + DIM
                for e in range(2):
                    dve.wait_ge(*two["qkv"](it, e + 1))
                    cols = slice(e * SEQ, (e + 1) * SEQ)
                    for blk in range(KT):
                        src = slice(blk * SEQ, (blk + 1) * SEQ)
                        dve.tensor_scalar(qT[:, blk, cols], PS[:, 2 * e, src], w_qkv[:, e, bias0 + blk:bias0 + blk + 1],
                                          float(HD) ** -0.5, ALU.add, ALU.mult)
                        for dst, rows_kept in ((kTe, even_rows), (kTo, odd_rows)):
                            dve.tensor_scalar(dst[:, blk, cols], PS[:, 2 * e + 1, src],
                                              w_qkv[:, e, bias0 + 2 + blk:bias0 + 3 + blk], rows_kept[:, :],
                                              ALU.add, ALU.mult)
                    for tt in range(2):
                        last = dve.tensor_tensor(
                            V1[:, 2 * e + tt, :, 0:HD],
                            PS[:, 4 + e, tt * DIM:(tt + 1) * DIM].rearrange("p (h e) -> p h e", h=HEADS),
                            w_qkv[:, e, 2 * 768:2 * 768 + DIM].rearrange("p (h e) -> p h e", h=HEADS), ALU.add)
                    last.then_inc(two["in"].sem, 1)
                dve_attention(dve, it, att2)
                halves = lambda ap, e: ap[:, 2 * e:2 * e + 2, :]
                row = lambda w, e, start: w[:, e, start:start + DIM].unsqueeze(1).to_broadcast([P, 2, DIM])

                def scale_shift(w, start):
                    for e in range(2):
                        last = dve.tensor_tensor(halves(xn, e), halves(xn, e), row(w, e, start), ALU.mult)
                    link(dve, dve_chain, last)
                    for e in range(2):
                        last = dve.tensor_tensor(halves(xn, e), halves(xn, e), row(w, e, start + DIM), ALU.add)
                    return last

                dve.wait_ge(*two["y"](it, 1))
                dve.wait_ge(*two["xb"](it, 1))
                link(dve, dve_chain, dve.tensor_tensor(
                    rr[:, :, :], PS[:, 0:2, :].rearrange("p b (t f) -> p (b t) f", t=2), xb[:, :, :], ALU.add))
                dve_stats(dve, rr, two["var"])
                dve.wait_ge(*two["rstd"](it, 1))
                link(dve, dve_chain, dve_normalise(dve, xn, rr))
                scale_shift(w_out, 3 * DIM).then_inc(two["xp"].sem, 1)
                for b in range(1, 8, 2):
                    dve.wait_ge(*two["h"](it, b + 1))
                    for j in range(2):
                        e, blk = b // 4, 2 * (b % 4) + j
                        last = dve.tensor_scalar(hT[:, e, blk, :], PS[:, b, j * SEQ:(j + 1) * SEQ],
                                                 w_up[:, e, KT * DFF + blk:KT * DFF + blk + 1], 0.0, ALU.add, ALU.max)
                    last.then_inc(two["h_dve"].sem, 1)
                dve.wait_ge(*two["y2"](it, 1))
                dve.wait_ge(*two["xpb"](it, 1))
                for e in range(2):
                    last = dve.tensor_tensor(halves(rr, e), PS[:, 4 * e, :].rearrange("p (t f) -> p t f", t=2),
                                             halves(xb, e), ALU.add)
                link(dve, dve_chain, last)
                dve_stats(dve, rr, two["var"])
                dve.wait_ge(*two["rstd"](it, 2))
                link(dve, dve_chain, dve_normalise(dve, xn, rr))
                link(dve, dve_chain, scale_shift(w_down, FB * DIM + DIM))
                flat = lambda ap: ap.rearrange("p t f -> p (t f)")
                link(dve, dve_chain, dve.scalar_tensor_tensor(
                    out=flat(halves(rr, 0)), in0=flat(halves(xn, 0)), scalar=gate_weight[:, bass.ds(it * 2, 1)],
                    in1=flat(x[:, 0:2, :]), op0=ALU.mult, op1=ALU.add))
                dve.scalar_tensor_tensor(
                    out=flat(halves(rr, 0)), in0=flat(halves(xn, 1)), scalar=gate_weight[:, bass.ds(it * 2 + 1, 1)],
                    in1=flat(halves(rr, 0)), op0=ALU.mult, op1=ALU.add).then_inc(two["normed2"].sem, 1)
                dve.wait_ge(*two["normed2"](it, 1))
                dve_stats(dve, rr, two["var"], 2)
                dve.wait_ge(*two["rstd"](it, 3))
                dve.wait_ge(*stored2(it, 0))
                dve_normalise(dve, y, rr, 2).then_inc(two["x3"].sem, 1)

        def pool_phase2(pool):
            with pool.Fori(0, BATCH) as it:
                pool.wait_ge(*in2x(it, 16))
                pool.wait_ge(*loaded2["out"](it, 32))
                for e in range(2):
                    last = pool.tensor_tensor(xb[:, 2 * e:2 * e + 2, :], x[:, 0:2, :],
                                              w_out[:, e, 2 * DIM:3 * DIM].unsqueeze(1).to_broadcast([P, 2, DIM]), ALU.add)
                last.then_inc(two["xb"].sem, 1)
                pool_rstd(pool, it, two["var"], two["rstd"], 1)
                pool.wait_ge(*two["xp"](it, 1))
                pool.wait_ge(*loaded2["down"](it, 32))
                for e in range(2):
                    last = pool.tensor_tensor(xb[:, 2 * e:2 * e + 2, :], xn[:, 2 * e:2 * e + 2, :],
                                              w_down[:, e, FB * DIM:FB * DIM + DIM].unsqueeze(1).to_broadcast([P, 2, DIM]),
                                              ALU.add)
                last.then_inc(two["xpb"].sem, 1)
                pool_rstd(pool, it, two["var"], two["rstd"], 2)
                pool_rstd(pool, it, two["var"], two["rstd"], 3, 2)

        phase2_buffers.close()
        phase3_buffers = ExitStack()
        ctx.enter_context(phase3_buffers)
        sb3 = lambda name, shape, dt=F32: phase3_buffers.enter_context(nc.sbuf_tensor(name, shape, dt))
        NH, DH = 4, 64
        SLOT_HEADS = (0, 2, 1, 3)
        GROUPS = 4
        aw = sb3("aw", [P, KT, 3 * DIM])
        mgate = sb3("mgate", [P, 3 * KT, 2 * NH])
        mgate_bias = sb3("mgate_bias", [P, 2 * NH])
        outnorm = sb3("outnorm", [P, DIM])
        gate1 = sb3("gate1", [P, KT, EXPERTS1])
        gate1_bias = sb3("gate1_bias", [P, EXPERTS1])
        av = sb3("av", [P, TILES, DIM])
        aprob = sb3("aprob", [P, TILES, SEQ])
        aprobT = sb3("aprobT", [P, 2, 3 * P])
        neg_max3 = sb3("neg_max3", [P, TILES])
        row_sum = sb3("row_sum", [P, TILES])
        gates = sb3("gates", [P, TILES, 2 * NH])
        abs_f = sb3("abs_f", [P, TILES, NH])
        min_f = sb3("min_f", [P, TILES, NH])
        log_f = sb3("log_f", [P, TILES, NH])
        cum = sb3("cum", [P, TILES, NH])
        source = sb3("source", [P, TILES, NH])
        sourceT = sb3("sourceT", [NH, TOK])
        neg_run = sb3("neg_run", [P, TILES, NH])
        Dm = sb3("Dm", [P, 2, NH, SEQ])
        Cm = sb3("Cm", [P, 2, NH, SEQ])
        CT = sb3("CT", [P, 2, NH, SEQ])
        row_C = sb3("row_C", [P, TILES, NH])
        floor = sb3("floor", [P, TILES, NH])
        hm = sb3("hm", [P, TILES, DIM])
        hsq = sb3("hsq", [P, TILES, DIM])
        hmean = sb3("hmean", [P, TILES * NH])
        hvar = sb3("hvar", [P, TILES * NH])
        score = sb3("score", [P, TILES, EXPERTS1])
        choice = sb3("choice", [P, TILES, EXPERTS1])
        group8 = sb3("group8", [P, TILES, GROUPS, 8])
        group10 = sb3("group10", [P, TILES, 10])
        group_top = sb3("group_top", [P, TILES, 8])
        group_want = sb3("group_want", [P, TILES, 8])
        group_hit = sb3("group_hit", [P, TILES, 10])
        expert_top = sb3("expert_top", [P, TILES, 8])
        route = sb3("route", [P, TILES, ALL_EXPERTS])
        route_sum = sb3("route_sum", [P, TILES])

        W3 = [(aw, "aw"), (mgate, "mgate"), (mgate_bias, "mgate_bias"), (outnorm, "outnorm"), (gate1, "gate1"),
              (gate1_bias, "gate1_bias")]
        weights3_loaded = signal("weights3_loaded", 0)
        in3 = signal("in3", 64)
        three = {n: signal(f"l1_{n}", per) for n, per in (
            ("qkv", 1), ("k", 1), ("v", 1), ("scores", 4), ("max", 4), ("exp", 4), ("turned", 2), ("probT", 2),
            ("out", 1), ("var", 2), ("rstd", 2), ("x4", 1), ("x4turned", 1), ("x4T", 1),
            ("gates", 1), ("abs", 1), ("fexp", 1), ("flog", 1), ("logf", 1), ("cum", 1), ("source", 1),
            ("sourceturned", 1), ("sourceT", 1), ("ab", 4), ("run", 4), ("D", 4), ("C", 4), ("Cturned", 4), ("CT", 4),
            ("h", 4), ("hout", 4), ("floor", 1), ("fl", 1), ("hc", 1), ("hsq", 1), ("hvar", 1), ("hrstd", 1),
            ("x5", 1), ("x5turned", 1), ("x5T", 1), ("logits", 1), ("lexp", 1), ("route", 1))}
        stored3 = signal("stored3", 48, base=48)

        def sp_load3(sp, it):
            sp.dma_start(xT[:, :, :], columns(xsT["x3"], it, TILES)).then_inc(in3.sem, 16)
            sp.dma_start(x[:, :, :], rows(xs["x3"], it, TILES)).then_inc(in3.sem, 16)
            sp.dma_start(cT[:, :, :], columns(d["ctxT"], it, TILES)).then_inc(in3.sem, 16)
            sp.dma_start(c[:, :, :], rows(d["ctx"], it, TILES)).then_inc(in3.sem, 16)

        def sp_store3(sp, it):
            sp.wait_ge(*three["x5"](it, 1))
            sp.dma_start(rows(xs["x5"], it, TILES), y[:, :, :]).then_inc(stored3.sem, 16)
            sp.wait_ge(*three["x5T"](it, 1))
            sp.dma_start(columns(xsT["x5"], it, TILES), yT[:, :, :]).then_inc(stored3.sem, 16)
            sp.wait_ge(*three["route"](it, 1))
            sp.dma_start(rows(route_dram, it, TILES), route[:, :, :]).then_inc(stored3.sem, 16)

        def sp_phase3(sp):
            sp.sem_inc(stored3.sem, 48)
            for dst, name in W3:
                sp.dma_start(dst[tuple(slice(None) for _ in dst.shape)], d[name]).then_inc(weights3_loaded.sem, 16)
            sp_load3(sp, 0)
            with sp.Fori(0, PAIRS - 1) as it:
                sp.wait_ge(*three["h"](it, 4))
                sp_load3(sp, it + 1)
                sp_store3(sp, it)
            sp_store3(sp, PAIRS - 1)
            sp.wait_ge(*stored3(PAIRS - 1, 48))

        def width(t):
            return (t % 2 + 1) * P

        def pe_phase3(pe):
            pe.wait_ge(weights3_loaded.sem, 16 * len(W3))
            with pe.Fori(0, PAIRS) as it:
                pe.wait_ge(*in3(it, 64))
                for blk in range(4):
                    for ki in range(KT):
                        pe.matmul(PS[:, blk, :], aw[:, ki, blk * P:(blk + 1) * P], xT[:, ki, :],
                                  start=(ki == 0), stop=(ki == 1))
                for t in range(TILES):
                    for ki in range(KT):
                        last = pe.matmul(PS[:, 4 + t // 2, (t % 2) * DIM:(t % 2 + 1) * DIM], xT[:, ki, tokens(t)],
                                         aw[:, ki, 2 * DIM:3 * DIM], start=(ki == 0), stop=(ki == 1))
                last.then_inc(three["qkv"].sem, 1)
                pe.wait_ge(*three["k"](it, 1))
                for t in range(TILES):
                    s, w = t // 2, width(t)
                    pe.matmul(PS[:, t, 0:w], identity16[:, :], causal_mask[:, t % 2, 0:w], start=True, stop=False)
                    for ki in range(KT):
                        last = pe.matmul(PS[:, t, 0:w], qT[:, ki, tokens(t)], kTe[:, ki, s * SEQ:s * SEQ + w],
                                         start=False, stop=(ki == 1))
                    last.then_inc(three["scores"].sem, 1)
                pe.wait_ge(*three["v"](it, 1))
                for s in range(2):
                    pe.wait_ge(*three["exp"](it, 2 * s + 2))
                    for slot, (qt, kt) in enumerate(((0, 0), (1, 0), (1, 1))):
                        last = pe.transpose(PS[:, 4 + s, slot * P:(slot + 1) * P],
                                            aprob[:, 2 * s + qt, kt * P:(kt + 1) * P], identity[:, :])
                    last.then_inc(three["turned"].sem, 1)
                for s in range(2):
                    pe.wait_ge(*three["probT"](it, s + 1))
                    for slot, (qt, kt) in enumerate(((0, 0), (1, 0), (1, 1))):
                        last = pe.matmul(PS[:, 6 + s, qt * DIM:(qt + 1) * DIM], aprobT[:, s, slot * P:(slot + 1) * P],
                                         av[:, 2 * s + kt, :], start=(kt == 0), stop=(kt == qt))
                last.then_inc(three["out"].sem, 1)
                pe.wait_ge(*three["x4"](it, 1))
                pe_turn(pe, xn, 0).then_inc(three["x4turned"].sem, 1)
                pe.wait_ge(*three["x4T"](it, 1))
                for t in range(TILES):
                    for blk in range(3 * KT):
                        lhs = (xnT if blk < KT else cT)[:, blk % KT, tokens(t)]
                        last = pe.matmul(PS[:, 2, t * 2 * NH:(t + 1) * 2 * NH], lhs, mgate[:, blk, :],
                                         start=(blk == 0), stop=(blk == 3 * KT - 1))
                last.then_inc(three["gates"].sem, 1)
                pe.wait_ge(*three["logf"](it, 1))
                for s in range(2):
                    pe.matmul(PS[:, 3, 2 * s * NH:(2 * s + 1) * NH], upto[:, :], log_f[:, 2 * s, :],
                              start=True, stop=True)
                    pe.matmul(PS[:, 3, (2 * s + 1) * NH:(2 * s + 2) * NH], ones[:, :], log_f[:, 2 * s, :],
                              start=True, stop=False)
                    last = pe.matmul(PS[:, 3, (2 * s + 1) * NH:(2 * s + 2) * NH], upto[:, :], log_f[:, 2 * s + 1, :],
                                     start=False, stop=True)
                last.then_inc(three["cum"].sem, 1)
                pe.wait_ge(*three["source"](it, 1))
                for t in range(TILES):
                    last = pe.transpose(PS[0:NH, 4, tokens(t)], source[:, t, :], identity[:, :])
                last.then_inc(three["sourceturned"].sem, 1)
                pe.wait_ge(*three["sourceT"](it, 1))
                def mix_scores(t):
                    s, w, base = t // 2, width(t), 4 * (t % 2)
                    if t >= 2:
                        pe.wait_ge(*three["hout"](it, t - 1))
                    for slot, h in enumerate(SLOT_HEADS):
                        bank, col = base + slot // 2, (slot % 2) * SEQ
                        pe.matmul(PS[:, bank, col:col + w], identity16[:, :], causal_mask[:, t % 2, 0:w],
                                  start=True, stop=False)
                        pe.matmul(PS[:, bank, col:col + w], head_rows[:, h, :], sourceT[:, s * SEQ:s * SEQ + w],
                                  start=False, stop=True)
                    for slot, h in enumerate(SLOT_HEADS):
                        bank, col, r = base + 2 + slot // 2, (slot % 2) * SEQ, DH * (h % 2)
                        last = pe.matmul(PS[:, bank, col:col + w], xnT[r:r + DH, h // 2, tokens(t)],
                                         cT[r:r + DH, h // 2, s * SEQ:s * SEQ + w], start=True, stop=True)
                    last.then_inc(three["ab"].sem, 1)

                def mix_values(t):
                    s, base = t // 2, 4 * (t % 2)
                    pe.wait_ge(*three["C"](it, t + 1))
                    for slot in range(NH):
                        for kt in range(t % 2 + 1):
                            col = (slot % 2) * SEQ + kt * P
                            last = pe.transpose(PS[:, base + slot // 2, col:col + P],
                                                Cm[:, t % 2, slot, kt * P:(kt + 1) * P], identity[:, :])
                    last.then_inc(three["Cturned"].sem, 1)
                    pe.wait_ge(*three["CT"](it, t + 1))
                    for slot, h in enumerate(SLOT_HEADS):
                        for kt in range(t % 2 + 1):
                            last = pe.matmul(PS[:, base + 2, h * DH:(h + 1) * DH], CT[:, t % 2, slot, kt * P:(kt + 1) * P],
                                             c[:, 2 * s + kt, h * DH:(h + 1) * DH], start=(kt == 0), stop=(kt == t % 2))
                    last.then_inc(three["h"].sem, 1)

                mix_scores(0)
                for t in range(TILES):
                    if t + 1 < TILES:
                        mix_scores(t + 1)
                    mix_values(t)
                pe.wait_ge(*three["x5"](it, 1))
                pe_turn(pe, y, 0).then_inc(three["x5turned"].sem, 1)
                pe.wait_ge(*three["x5T"](it, 1))
                for t in range(TILES):
                    for ki in range(KT):
                        last = pe.matmul(PS[:, 4, t * EXPERTS1:(t + 1) * EXPERTS1], yT[:, ki, tokens(t)],
                                         gate1[:, ki, :], start=(ki == 0), stop=(ki == 1))
                last.then_inc(three["logits"].sem, 1)
                pe.wait_ge(*three["lexp"](it, 1))

        def act_phase3(act):
            with act.Fori(0, PAIRS) as it:
                act.wait_ge(*three["qkv"](it, 1))
                act.activation(qT[:, :, :], PS[:, 0:2, :], ACT.Copy, scale=float(DIM) ** -0.5)
                act.activation(kTe[:, :, :], PS[:, 2:4, :], ACT.Copy).then_inc(three["k"].sem, 1)
                for t in range(TILES):
                    act.wait_ge(*three["max"](it, t + 1))
                    act.activation(aprob[:, t, 0:width(t)], PS[:, t, 0:width(t)], ACT.Exp, bias=neg_max3[:, t:t + 1],
                                   accum_out=row_sum[:, t:t + 1]).then_inc(three["exp"].sem, 1)
                for s in range(2):
                    act.wait_ge(*three["turned"](it, s + 1))
                    act.activation(aprobT[:, s, :], PS[:, 4 + s, 0:3 * P], ACT.Copy).then_inc(three["probT"].sem, 1)
                act.wait_ge(*three["x4turned"](it, 1))
                act_turned(act, xnT, 0).then_inc(three["x4T"].sem, 1)
                act.wait_ge(*three["abs"](it, 1))
                act.activation(abs_f[:, :, :], abs_f[:, :, :], ACT.Exp, scale=-1.0).then_inc(three["fexp"].sem, 1)
                act.wait_ge(*three["fexp"](it, 1))
                act.activation(abs_f[:, :, :], abs_f[:, :, :], ACT.Ln, bias=1.0).then_inc(three["flog"].sem, 1)
                act.wait_ge(*three["sourceturned"](it, 1))
                act.activation(sourceT[:, :], PS[0:NH, 4, :], ACT.Copy).then_inc(three["sourceT"].sem, 1)

                def mix_exp(t):
                    act.wait_ge(*three["run"](it, t + 1))
                    if t >= 2:
                        act.wait_ge(*three["C"](it, t - 1))
                    for slot, h in enumerate(SLOT_HEADS):
                        src = PS[:, 4 * (t % 2) + slot // 2, (slot % 2) * SEQ:(slot % 2) * SEQ + width(t)]
                        last = act.activation(Dm[:, t % 2, slot, 0:width(t)], src, ACT.Exp, bias=neg_run[:, t, h:h + 1])
                    last.then_inc(three["D"].sem, 1)

                mix_exp(0)
                for t in range(TILES):
                    if t + 1 < TILES:
                        mix_exp(t + 1)
                    act.wait_ge(*three["Cturned"](it, t + 1))
                    base = 4 * (t % 2)
                    act.activation(CT[:, t % 2, :, 0:width(t)],
                                   PS[:, base:base + 2, :].rearrange("p b (h k) -> p (b h) k", h=2)[:, :, 0:width(t)],
                                   ACT.Copy).then_inc(three["CT"].sem, 1)
                act.wait_ge(*three["floor"](it, 1))
                act.activation(floor[:, :, :], floor[:, :, :], ACT.Exp).then_inc(three["fl"].sem, 1)
                act.wait_ge(*three["hc"](it, 1))
                act.activation(hsq[:, :, :], hm[:, :, :], ACT.Square).then_inc(three["hsq"].sem, 1)
                act.wait_ge(*three["x5turned"](it, 1))
                act.wait_ge(*stored3(it, 0))
                act_turned(act, yT, 0).then_inc(three["x5T"].sem, 1)
                act.wait_ge(*three["logits"](it, 1))
                act.activation(score[:, :, :], PS[:, 4, 0:TILES * EXPERTS1].rearrange("p (t e) -> p t e", t=TILES),
                               ACT.Exp, scale=-1.0).then_inc(three["lexp"].sem, 1)

        def dve_phase3(dve):
            dve.wait_ge(weights3_loaded.sem, 16 * len(W3))
            restart(dve, dve_chain)
            dve.memset(group10[:, :, :], FAR)
            dve.memset(group_want[:, :, :], FAR)
            link(dve, dve_chain, dve.memset(route[:, :, EXPERTS1:ALL_EXPERTS], 1.0))
            with dve.Fori(0, PAIRS) as it:
                restart(dve, dve_chain)

                def chained(ins):
                    link(dve, dve_chain, ins)

                dve.wait_ge(*three["qkv"](it, 1))
                dve.tensor_copy(av[:, :, :], PS[:, 4:6, :].rearrange("p b (t f) -> p (b t) f", t=2))\
                    .then_inc(three["v"].sem, 1)
                for t in range(TILES):
                    dve.wait_ge(*three["scores"](it, t + 1))
                    dve.tensor_reduce(neg_max3[:, t:t + 1], PS[:, t, 0:width(t)], AX.X, ALU.max, negate=True)\
                        .then_inc(three["max"].sem, 1)
                dve.wait_ge(*three["exp"](it, 4))
                chained(dve.reciprocal(row_sum[:, :], row_sum[:, :]))
                dve.wait_ge(*three["out"](it, 1))
                for t in range(TILES):
                    last = dve.scalar_tensor_tensor(out=rr[:, t, :], in0=PS[:, 6 + t // 2, (t % 2) * DIM:(t % 2 + 1) * DIM],
                                                    scalar=row_sum[:, t:t + 1], in1=x[:, t, :],
                                                    op0=ALU.mult, op1=ALU.add)
                chained(last)
                dve_stats(dve, rr, three["var"])
                dve.wait_ge(*three["rstd"](it, 1))
                dve_normalise(dve, xn, rr).then_inc(three["x4"].sem, 1)
                dve.wait_ge(*three["gates"](it, 1))
                chained(dve.tensor_tensor(gates[:, :, :], PS[:, 2, 0:TILES * 2 * NH].rearrange("p (t g) -> p t g", t=TILES),
                                          mgate_bias[:, :].unsqueeze(1).to_broadcast([P, TILES, 2 * NH]), ALU.add))
                forget = gates[:, :, NH:2 * NH]
                dve.scalar_tensor_tensor(out=abs_f[:, :, :], in0=forget, scalar=-1.0, in1=forget,
                                         op0=ALU.mult, op1=ALU.max).then_inc(three["abs"].sem, 1)
                chained(dve.tensor_scalar(min_f[:, :, :], forget, 0.0, None, ALU.min))
                dve.wait_ge(*three["flog"](it, 1))
                dve.tensor_tensor(log_f[:, :, :], min_f[:, :, :], abs_f[:, :, :], ALU.subtract)\
                    .then_inc(three["logf"].sem, 1)
                dve.wait_ge(*three["cum"](it, 1))
                chained(dve.tensor_copy(cum[:, :, :], PS[:, 3, 0:TILES * NH].rearrange("p (t g) -> p t g", t=TILES)))
                dve.tensor_tensor(source[:, :, :], gates[:, :, 0:NH], cum[:, :, :], ALU.subtract)\
                    .then_inc(three["source"].sem, 1)

                by_slot = lambda ap: ap.rearrange("p (b h) -> p h b", h=2)

                def mix_max(t):
                    dve.wait_ge(*three["ab"](it, t + 1))
                    base = 4 * (t % 2)
                    src = PS[:, base:base + 2, :].rearrange("p b (h k) -> p b h k", h=2)[:, :, :, 0:width(t)]
                    dve.tensor_reduce(by_slot(neg_run[:, t, :]), src, AX.X, ALU.max, negate=True).then_inc(three["run"].sem, 1)

                def mix_c(t):
                    dve.wait_ge(*three["D"](it, t + 1))
                    if t >= 2:
                        dve.wait_ge(*three["Cturned"](it, t - 1))
                    base = 4 * (t % 2) + 2
                    src = PS[:, base:base + 2, :].rearrange("p b (h k) -> p (b h) k", h=2)[:, :, 0:width(t)]
                    dst = Cm[:, t % 2, :, 0:width(t)]
                    dve.scalar_tensor_tensor(out=dst, in0=src, scalar=float(DH) ** -0.5, in1=Dm[:, t % 2, :, 0:width(t)],
                                             op0=ALU.mult, op1=ALU.mult).then_inc(three["C"].sem, 1)
                    dve.wait_ge(*three["C"](it, t + 1))
                    chained(dve.tensor_reduce(by_slot(row_C[:, t, :]), dst.rearrange("p (b h) k -> p b h k", b=2),
                                              AX.X, ALU.add))

                mix_max(0)
                mix_c(0)
                for t in range(TILES):
                    if t + 1 < TILES:
                        mix_max(t + 1)
                        mix_c(t + 1)
                    dve.wait_ge(*three["h"](it, t + 1))
                    dve.tensor_copy(hm[:, t, :], PS[:, 4 * (t % 2) + 2, 0:DIM]).then_inc(three["hout"].sem, 1)
                flat = lambda ap: ap.rearrange("p t h -> p (t h)")
                dve.tensor_tensor(floor[:, :, :], neg_run[:, :, :], cum[:, :, :], ALU.subtract)\
                    .then_inc(three["floor"].sem, 1)
                chained(dve.scalar_tensor_tensor(out=flat(row_C[:, :, :]), in0=flat(row_C[:, :, :]), scalar=-1.0,
                                                 in1=flat(row_C[:, :, :]), op0=ALU.mult, op1=ALU.max))
                dve.wait_ge(*three["fl"](it, 1))
                chained(dve.tensor_tensor(row_C[:, :, :], row_C[:, :, :], floor[:, :, :], ALU.max))
                chained(dve.tensor_scalar(row_C[:, :, :], row_C[:, :, :], 1e-6, None, ALU.add))
                chained(dve.reciprocal(row_C[:, :, :], row_C[:, :, :]))
                per_head = hm[:, :, :].rearrange("p t (h e) -> p (t h) e", h=NH)
                spread = lambda ap: ap.unsqueeze(2).to_broadcast([P, TILES * NH, DH])
                dve.wait_ge(*three["hout"](it, 4))
                chained(dve.tensor_tensor(per_head, per_head, spread(flat(row_C[:, :, :])), ALU.mult))
                chained(dve.tensor_reduce(hmean[:, :], per_head, AX.X, ALU.add))
                chained(dve.tensor_scalar(hmean[:, :], hmean[:, :], 1.0 / DH, None, ALU.mult))
                dve.tensor_tensor(per_head, per_head, spread(hmean[:, :]), ALU.subtract).then_inc(three["hc"].sem, 1)
                dve.wait_ge(*three["hsq"](it, 1))
                chained(dve.tensor_reduce(hvar[:, :], hsq[:, :, :].rearrange("p t (h e) -> p (t h) e", h=NH), AX.X, ALU.add))
                dve.tensor_scalar(hvar[:, :], hvar[:, :], 1.0 / DH, 1e-5, ALU.mult, ALU.add).then_inc(three["hvar"].sem, 1)
                dve.wait_ge(*three["hrstd"](it, 1))
                chained(dve.tensor_tensor(per_head, per_head, spread(hvar[:, :]), ALU.mult))
                chained(dve.tensor_tensor(hm[:, :, :], hm[:, :, :],
                                          outnorm[:, :].unsqueeze(1).to_broadcast([P, TILES, DIM]), ALU.mult))
                chained(dve.tensor_tensor(rr[:, :, :], hm[:, :, :], xn[:, :, :], ALU.add))
                dve_stats(dve, rr, three["var"])
                dve.wait_ge(*three["rstd"](it, 2))
                dve.wait_ge(*stored3(it, 0))
                dve_normalise(dve, y, rr).then_inc(three["x5"].sem, 1)
                dve.wait_ge(*three["lexp"](it, 1))
                chained(dve.tensor_scalar(score[:, :, :], score[:, :, :], 1.0, None, ALU.add))
                chained(dve.reciprocal(score[:, :, :], score[:, :, :]))
                chained(dve.tensor_tensor(choice[:, :, :], score[:, :, :],
                                          gate1_bias[:, :].unsqueeze(1).to_broadcast([P, TILES, EXPERTS1]), ALU.add))
                for t in range(TILES):
                    for g in range(GROUPS):
                        last = dve.max(group8[:, t, g, :], choice[:, t, 8 * g:8 * g + 8])
                chained(last)
                chained(dve.tensor_tensor(group10[:, :, 0:GROUPS], group8[:, :, :, 0], group8[:, :, :, 1], ALU.add))
                for t in range(TILES):
                    last = dve.max(group_top[:, t, :], group10[:, t, :])
                chained(last)
                chained(dve.tensor_copy(group_want[:, :, 0:2], group_top[:, :, 0:2]))
                for t in range(TILES):
                    last = dve.match_replace(group_hit[:, t, :], group_want[:, t, :], group10[:, t, :], -FAR)
                chained(last)
                chained(dve.tensor_scalar(group_hit[:, :, :], group_hit[:, :, :], 1e38, None, ALU.is_ge))
                by_group = lambda ap: ap.rearrange("p t (g e) -> p t g e", g=GROUPS)
                chained(dve.tensor_tensor(by_group(choice[:, :, :]), by_group(choice[:, :, :]),
                                          group_hit[:, :, 0:GROUPS].unsqueeze(3).to_broadcast([P, TILES, GROUPS, 8]),
                                          ALU.mult))
                chained(dve.tensor_scalar(choice[:, :, :], choice[:, :, :], 0.0, None, ALU.add))
                for t in range(TILES):
                    last = dve.max(expert_top[:, t, :], choice[:, t, :])
                chained(last)
                for t in range(TILES):
                    last = dve.match_replace(choice[:, t, :], expert_top[:, t, :], choice[:, t, :], -FAR)
                chained(last)
                chained(dve.tensor_scalar(choice[:, :, :], choice[:, :, :], 1e38, None, ALU.is_ge))
                chained(dve.tensor_tensor(score[:, :, :], score[:, :, :], choice[:, :, :], ALU.mult))
                chained(dve.tensor_reduce(route_sum[:, :], score[:, :, :], AX.X, ALU.add))
                chained(dve.tensor_scalar(route_sum[:, :], route_sum[:, :], 1e-20, None, ALU.add))
                chained(dve.reciprocal(route_sum[:, :], route_sum[:, :]))
                chained(dve.tensor_scalar(route_sum[:, :], route_sum[:, :], 2.5, None, ALU.mult))
                dve.tensor_tensor(route[:, :, 0:EXPERTS1], score[:, :, :],
                                  route_sum[:, :].unsqueeze(2).to_broadcast([P, TILES, EXPERTS1]), ALU.mult)\
                    .then_inc(three["route"].sem, 1)
                dve.wait_ge(*three["route"](it, 1))

        def pool_phase3(pool):
            with pool.Fori(0, PAIRS) as it:
                pool_rstd(pool, it, three["var"], three["rstd"], 1)
                pool.wait_ge(*three["hvar"](it, 1))
                pool.tensor_tensor(hvar[:, :], hvar[:, :], minus_half[:, 0:TILES * NH], ALU.pow)\
                    .then_inc(three["hrstd"].sem, 1)
                pool_rstd(pool, it, three["var"], three["rstd"], 2)

        phase3_buffers.close()
        sb4 = lambda name, shape, dt=F32: ctx.enter_context(nc.sbuf_tensor(name, shape, dt))
        NT = BATCH * SEQ // P
        NG = NT // TILES
        W_EXPERT = 2 * KT * INNER + DIM
        xT4 = sb4("xT4", [P, KT, NT * P])
        acc = sb4("acc", [P, NT, DIM])
        route4 = sb4("route4", [P, NT, ALL_EXPERTS])
        w_expert = sb4("w_expert", [P, 2, W_EXPERT])
        silu_g = sb4("silu_g", [P, 2, TOK])
        hT4 = sb4("hT4", [P, 2, TOK])

        in4 = signal("in4", 0)
        expert_loaded = [signal(f"expert_loaded{j}", 16) for j in range(2)]
        STEPS = 2 * NG
        four = {n: signal(f"e_{n}", STEPS, base) for n, base in
                (("gu", 0), ("silu", 0), ("hidden", 2), ("down", 0), ("added", 2))}
        four_ln = {n: signal(f"z_{n}", 1) for n in ("var", "rstd", "out")}
        stored4 = signal("stored4", 16, base=16)

        def sp_phase4(sp):
            sp.sem_inc(stored4.sem, 16)
            sp.wait_ge(*three["route"](PAIRS - 1, 1))
            sp.dma_start(xT4[:, :, :], xsT["x5"].rearrange("(k p) t -> p k t", p=P)).then_inc(in4.sem, 16)
            sp.dma_start(acc[:, :, :], xs["x5"].rearrange("(t p) f -> p t f", p=P)).then_inc(in4.sem, 16)
            sp.dma_start(route4[:, :, :], route_dram.rearrange("(t p) e -> p t e", p=P)).then_inc(in4.sem, 16)
            load = lambda e, j: sp.dma_start(
                w_expert[:, j, :], d["experts"][bass.ds(e, 1), :, :].rearrange("a p n -> p (a n)"))\
                .then_inc(expert_loaded[j].sem, 16)
            load(0, 0)
            load(1, 1)
            with sp.Fori(0, ALL_EXPERTS // 2 - 1) as it:
                for j in range(2):
                    sp.wait_ge(*four["down"](it, NG * (j + 1)))
                    load((it + 1) * 2 + j, j)
            with sp.Fori(0, NG) as g:
                sp.wait_ge(*four_ln["out"](g, 1))
                sp.dma_start(rows(out, g, TILES), y[:, :, :]).then_inc(stored4.sem, 16)
            sp.wait_ge(*stored4(NG - 1, 16))

        def pe_phase4(pe):
            pe.wait_ge(in4.sem, 48)
            with pe.Fori(0, ALL_EXPERTS // 2) as it:
                def up(n):
                    j, g = n // NG, n % NG
                    if g == 0:
                        pe.wait_ge(*expert_loaded[j](it, 16))
                    pe.wait_ge(*four["hidden"](it, n - 1))
                    for m in range(2):
                        for ki in range(KT):
                            col = (ki * 2 + m) * INNER
                            last = pe.matmul(PS[:, 2 * (n % 2) + m, :], w_expert[:, j, col:col + INNER],
                                             xT4[:, ki, g * TOK:(g + 1) * TOK], start=(ki == 0), stop=(ki == 1))
                    last.then_inc(four["gu"].sem, 1)

                def down(n):
                    j = n // NG
                    pe.wait_ge(*four["hidden"](it, n + 1))
                    pe.wait_ge(*four["added"](it, n - 1))
                    for t in range(TILES):
                        last = pe.matmul(PS[:, 4 + 2 * (n % 2) + t // 2, (t % 2) * DIM:(t % 2 + 1) * DIM],
                                         hT4[:, n % 2, tokens(t)], w_expert[:, j, 2 * KT * INNER:],
                                         start=True, stop=True)
                    last.then_inc(four["down"].sem, 1)

                up(0)
                for n in range(1, STEPS):
                    up(n)
                    down(n - 1)
                down(STEPS - 1)

        def act_phase4(act):
            with act.Fori(0, ALL_EXPERTS // 2) as it:
                for n in range(STEPS):
                    act.wait_ge(*four["gu"](it, n + 1))
                    act.wait_ge(*four["hidden"](it, n - 1))
                    act.activation(silu_g[:, n % 2, :], PS[:, 2 * (n % 2), :], ACT.Silu).then_inc(four["silu"].sem, 1)

        def dve_phase4(dve):
            dve.wait_ge(in4.sem, 48)
            dve.sem_inc(four["hidden"].sem, 2)
            dve.sem_inc(four["added"].sem, 2)
            with dve.Fori(0, ALL_EXPERTS // 2) as it:
                def hidden(n):
                    dve.wait_ge(*four["silu"](it, n + 1))
                    if n >= 2:
                        dve.wait_ge(*four["down"](it, n - 1))
                    dve.tensor_tensor(hT4[:, n % 2, :], silu_g[:, n % 2, :], PS[:, 2 * (n % 2) + 1, :], ALU.mult)\
                        .then_inc(four["hidden"].sem, 1)

                def add(n):
                    j, g = n // NG, n % NG
                    dve.wait_ge(*four["down"](it, n + 1))
                    for t in range(TILES):
                        tile = TILES * g + t
                        last = dve.scalar_tensor_tensor(
                            out=acc[:, tile, :], in0=PS[:, 4 + 2 * (n % 2) + t // 2, (t % 2) * DIM:(t % 2 + 1) * DIM],
                            scalar=route4[:, tile, bass.ds(it * 2 + j, 1)], in1=acc[:, tile, :],
                            op0=ALU.mult, op1=ALU.add)
                    last.then_inc(four["added"].sem, 1)

                hidden(0)
                for n in range(1, STEPS):
                    hidden(n)
                    add(n - 1)
                add(STEPS - 1)
            dve.wait_ge(*four["added"](ALL_EXPERTS // 2 - 1, STEPS))
            with dve.Fori(0, NG) as g:
                restart(dve, dve_chain)
                link(dve, dve_chain, dve.tensor_copy(rr[:, :, :], acc[:, bass.ds(g * TILES, TILES), :]))
                dve_stats(dve, rr, four_ln["var"])
                dve.wait_ge(*four_ln["rstd"](g, 1))
                dve.wait_ge(*stored4(g, 0))
                dve_normalise(dve, y, rr).then_inc(four_ln["out"].sem, 1)
                dve.wait_ge(*four_ln["out"](g, 1))

        def pool_phase4(pool):
            with pool.Fori(0, NG) as g:
                pool_rstd(pool, g, four_ln["var"], four_ln["rstd"])

        block = ctx.enter_context(nc.Block())

        @block.sync
        def _(sp):
            sp_phase1(sp)
            sp_phase2(sp)
            sp_phase3(sp)
            sp_phase4(sp)

        @block.tensor
        def _(pe):
            pe_phase1(pe)
            pe_phase2(pe)
            pe_phase3(pe)
            pe_phase4(pe)

        @block.scalar
        def _(act):
            act_phase1(act)
            act_phase2(act)
            act_phase3(act)
            act_phase4(act)

        @block.vector
        def _(dve):
            dve_phase1(dve)
            dve_phase2(dve)
            dve_phase3(dve)
            dve_phase4(dve)

        @block.gpsimd
        def _(pool):
            pool_phase1(pool)
            pool_phase2(pool)
            pool_phase3(pool)
            pool_phase4(pool)


def more_layout(f, h, np):
    E = "L0_ffn_"
    g = lambda n: f[E + n]
    qkv, outp, up, down = [], [], [], []
    for e in range(EXPERTS0):
        b = g("in_proj_b")[e]
        qkv.append(np.concatenate([_rows(g("in_proj_w")[e].T).reshape(128, -1), _spread(b[512:768]),
                                   _column(b[0:512])], 1))
        outp.append(np.concatenate([_rows(g("out_proj_w")[e].T).reshape(128, -1), _spread(g("out_proj_b")[e]),
                                    _spread(g("ln1_w")[e]), _spread(g("ln1_b")[e])], 1))
        up.append(np.concatenate([_rows(g("lin1_w")[e].T).reshape(128, -1), _column(g("lin1_b")[e])], 1))
        down.append(np.concatenate([_rows(g("lin2_w")[e].T).reshape(128, -1), _spread(g("lin2_b")[e]),
                                    _spread(g("ln2_w")[e]), _spread(g("ln2_b")[e])], 1))
    for n, v in (("f_qkv", qkv), ("f_out", outp), ("f_up", up), ("f_down", down)):
        h[n] = np.stack(v)
    h["aw"] = _rows(f["L1_attn_W_qkv"])
    M = "L1_xattn_"
    h["mgate"] = _rows(np.concatenate([f[M + "igate_kernel"], f[M + "fgate_kernel"]], 1))
    h["mgate_bias"] = _spread(np.concatenate([f[M + "igate_bias"], f[M + "fgate_bias"]]))
    h["outnorm"] = _spread(f[M + "outnorm_scale"])
    h["gate1"] = _rows(f["L1_ffn_gate_w"].T)
    h["gate1_bias"] = _spread(f["L1_ffn_gate_bias"])
    F = "L1_ffn_"
    gate = np.concatenate([f[F + "expert_gate"], f[F + "shared_gate"].reshape(2, INNER, DIM)])
    up1 = np.concatenate([f[F + "expert_up"], f[F + "shared_up"].reshape(2, INNER, DIM)])
    down1 = np.concatenate([f[F + "expert_down"], f[F + "shared_down"].reshape(DIM, 2, INNER).transpose(1, 0, 2)])
    both = np.concatenate([gate.transpose(0, 2, 1).reshape(-1, KT, 128, INNER),
                           up1.transpose(0, 2, 1).reshape(-1, KT, 128, INNER)], 3)
    both = both.transpose(0, 2, 1, 3).reshape(-1, 128, KT * 2 * INNER)
    h["experts"] = np.concatenate([both, down1.transpose(0, 2, 1)], 2)


def _rows(w, rows=128):
    import numpy as np
    return np.ascontiguousarray(w.reshape(w.shape[0] // rows, rows, w.shape[1]).transpose(1, 0, 2))


def _spread(v):
    import numpy as np
    return np.ascontiguousarray(np.broadcast_to(np.asarray(v).reshape(1, -1), (128, np.asarray(v).size)))


def _column(v):
    import numpy as np
    return np.ascontiguousarray(np.asarray(v).reshape(-1, 128).T)


def layout(a):
    import numpy as np
    f = {k: np.asarray(v) for k, v in a.items()}
    P = 128
    h = {}
    h["x"] = f["x"].reshape(-1, DIM)
    h["xT"] = np.ascontiguousarray(h["x"].T)
    h["ctx"] = f["ctx_1024"].reshape(-1, DIM)
    h["ctxT"] = np.ascontiguousarray(h["ctx"].T)
    L = "L0_attn_"
    h["wqk"] = _rows(np.concatenate([f[L + "Wq"], f[L + "Wk"]], 1))
    h["wvg"] = _rows(np.concatenate([f[L + "Wv"], f[L + "Wb"], f[L + "Wfd"], f[L + "Wsd"]], 1))
    h["decay_bias"] = _spread(np.concatenate([np.zeros(16, np.float32), f[L + "bfd"], f[L + "bsd"]]))
    h["wo"] = _rows(f[L + "Wo"])
    w1 = np.zeros((P, KT, P), np.float32)
    w2 = np.zeros((P, HEADS), np.float32)
    for n in range(HEADS):
        w1[16 * (n % 8):16 * (n % 8) + 16, n // 8, 8 * n:8 * n + 8] = f[L + "Wtf1"]
        w2[8 * n:8 * n + 8, n:n + 1] = f[L + "Wtf2"]
    h["wtf1"], h["wtf2"] = w1, w2
    h["btf1"] = np.ascontiguousarray(np.tile(f[L + "btf1"], HEADS).reshape(P, 1))
    h["btf2"] = _spread(f[L + "btf2"])
    X = "L0_xattn_"
    for n, k in (("xwq", "wq"), ("xwk", "wk"), ("xwv", "wv"), ("xwo", "wo_w")):
        h[n] = _rows(f[X + k].T)
    h["wo_b"] = _spread(f[X + "wo_b"])
    h["gate0"] = _rows(f["L0_ffn_gate_w"].T)
    h["gate0_bias"] = f["L0_ffn_gate_b"].reshape(1, -1)
    half = DIM // 2
    inv_freq = (1.0 / np.float32(10000.0) ** (np.arange(half, dtype=np.float32) / half)).astype(np.float32)
    angle = (np.arange(SEQ, dtype=np.float32)[:, None] * inv_freq[None, :]).astype(np.float32).T
    h["cosT"] = np.ascontiguousarray(np.tile(np.cos(angle), (1, 2)).astype(np.float32))
    h["sinT"] = np.ascontiguousarray(np.tile(np.sin(angle), (1, 2)).astype(np.float32))
    row = np.arange(P)
    h["even_rows"] = ((row // HD) % 2 == 0).astype(np.float32)[:, None]
    h["odd_rows"] = ((row // HD) % 2 == 1).astype(np.float32)[:, None]
    h["block_diag"] = (row[:, None] // HD == row[None, :] // HD).astype(np.float32)
    heads = np.zeros((4, 4, P), np.float32)
    for n in range(4):
        heads[n, n, :] = 1.0
    h["head_rows"] = heads
    h["identity"] = np.eye(P, dtype=np.float32)
    h["after"] = (row[:, None] > row[None, :]).astype(np.float32)
    h["upto"] = (row[:, None] <= row[None, :]).astype(np.float32)
    q = (np.arange(2)[:, None] * P + row[None, :])[:, :, None]
    k = np.arange(SEQ)[None, None, :]
    window = np.where(np.abs(k - q) <= WINDOW, 0.0, MASKED)
    causal = np.where(k <= q, 0.0, MASKED)
    for n, m in (("window_mask", window), ("causal_mask", causal)):
        h[n] = np.ascontiguousarray(m.transpose(1, 0, 2).astype(np.float32))
    more_layout(f, h, np)
    return h


def kernel(**inputs):
    import numpy as np
    import concourse.bacc as bacc
    from concourse import mybir as mb
    from concourse.bass_utils import run_bass_kernel_spmd

    arrays = {n: np.ascontiguousarray(v) for n, v in layout(inputs).items()}
    nc = bacc.Bacc("TRN2", target_bir_lowering=False, num_devices=1)
    d = {n: nc.dram_tensor(f"in_{n}", v.shape, mb.dt.from_np(v.dtype), kind="ExternalInput").ap()
         for n, v in arrays.items()}
    out = nc.dram_tensor("out", (BATCH * SEQ, DIM), F32, kind="ExternalOutput").ap()
    build(nc, d, out)
    r = run_bass_kernel_spmd(nc, [{f"in_{n}": v for n, v in arrays.items()}], core_ids=[0])
    return r.results[0]["out"].reshape(BATCH, SEQ, DIM)
```

```python
from contextlib import ExitStack

import concourse.bass as bass
from concourse import mybir

F32 = mybir.dt.float32
BF16 = mybir.dt.bfloat16
U32 = mybir.dt.uint32
F32R = mybir.dt.float32r
ALU = mybir.AluOpType
ACT = mybir.ActivationFunctionType
AX = mybir.AxisListType

P = 128
BATCH, SEQ, DIM = 16, 256, 256
HEADS, HD = 16, 16
KT = DIM // P
PAIRS = BATCH // 2
TILES = 4
TOK = TILES * P
WINDOW = 64
EXPERTS0, DFF = 4, 1024
FB = DFF // P
EXPERTS1, INNER = 32, 128
ALL_EXPERTS = EXPERTS1 + 2
LN_EPS = 1e-5
MASKED = -1e30
FAR = -3e38
UNITS = 2 * HEADS
QUADS = UNITS // 4
BATCH_UNITS = 8
BATCHES = UNITS // BATCH_UNITS
LAG = 12
PROBS = 6
BLOCKS = HEADS // 2


class Signal:

    def __init__(self, ctx, nc, name, per, base=0):
        self.sem = ctx.enter_context(nc.semaphore(name))
        self.per = per
        self.base = base

    def __call__(self, it, k):
        return self.sem, it * self.per + (self.base + k)

    def after(self, iterations, per=None):
        later = Signal.__new__(Signal)
        later.sem, later.per, later.base = self.sem, self.per if per is None else per, self.base + iterations * self.per
        return later


def build(nc, d, out):
    with ExitStack() as ctx:
        def sb(name, shape, dt=F32):
            return ctx.enter_context(nc.sbuf_tensor(name, shape, dt))

        def signal(name, per, base=0):
            return Signal(ctx, nc, name, per, base)

        PS = ctx.enter_context(nc.psum_tensor("PS", [P, 8, 512], F32))
        xs = {n: nc.dram_tensor(f"scratch_{n}", (32 * P, DIM), F32).ap() for n in ("x2", "x3", "x5")}
        xsT = {n: nc.dram_tensor(f"scratch_{n}T", (DIM, 32 * P), F32).ap() for n in ("x2", "x3", "x5")}
        route_dram = nc.dram_tensor("scratch_route", (32 * P, ALL_EXPERTS), F32).ap()

        identity = sb("identity", [P, P])
        identity16 = sb("identity16", [P, P], BF16)
        ones = sb("ones", [P, P])
        after = sb("after", [P, P])
        upto = sb("upto", [P, P])
        minus_half = sb("minus_half", [P, TILES * 4])
        mean_col = sb("mean_col", [P, 1])
        eps6 = sb("eps6", [P, 1])
        window_mask = sb("window_mask", [P, 2, SEQ], BF16)
        causal_mask = sb("causal_mask", [P, 2, SEQ], BF16)
        block_diag = sb("block_diag", [P, P])
        expert_index = sb("expert_index", [1, 2 * BATCH + 4], U32)
        gate_weight = sb("gate_weight", [P, 2 * BATCH + 4])

        x = sb("x", [P, TILES, DIM])
        xT = sb("xT", [P, KT, TOK])
        cT = sb("cT", [P, KT, TOK])
        qT = sb("qT", [P, KT, TOK])
        kT = sb("kT", [P, KT, TOK])
        o = sb("o", [P, TILES, DIM])
        oT = sb("oT", [P, KT, TOK])
        outT = oT[:, :, :].rearrange("p k (a q) -> p (k a) q", a=2)
        rr = sb("rr", [P, TILES, DIM])
        xn = sb("xn", [P, TILES, DIM])
        xnT = sb("xnT", [P, KT, TOK])
        xb = sb("xb", [P, TILES, DIM])
        y = sb("y", [P, TILES, DIM])
        yT = sb("yT", [P, KT, TOK])
        stats = sb("stats", [P, TILES, 6])
        mv = sb("mv", [P, TILES, 2])
        var_eps = sb("var_eps", [P, TILES])
        rstd = sb("rstd", [P, TILES])

        attention_shared = ExitStack()
        sba = lambda name, shape, dt=F32: attention_shared.enter_context(nc.sbuf_tensor(name, shape, dt))
        q_high, q_low, k_high, k_low = (sba(n, [P, KT, TOK], F32R) for n in ("q_high", "q_low", "k_high", "k_low"))
        stack_q = sba("stack_q", [P, 2, 4, P], F32R)
        stack_k = sba("stack_k", [P, 2, 4, P], F32R)
        pick_head = sba("pick_head", [P, BATCH_UNITS, P], F32R)
        V1 = sba("V1", [P, TILES, HEADS, 32])
        prob = sba("prob", [P, PROBS, 2, SEQ])
        neg_max = sba("neg_max", [P, 2, HEADS])
        max_split = sba("max_split", [P, 2, P], F32R)
        maxT = sba("maxT", [P, 2, SEQ], F32R)
        inv_sum = sba("inv_sum", [P, 2, 2, HEADS])

        consts_ready = signal("consts_ready", 1)
        dve_chain = ctx.enter_context(nc.semaphore("dve_chain"))
        pool_chain = ctx.enter_context(nc.semaphore("pool_chain"))

        links = {}

        def link(eng, chain, ins):
            links[eng] = links.get(eng, 0) + 1
            ins.then_inc(chain, 1)
            eng.wait_ge(chain, links[eng])

        def restart(eng, chain):
            eng.sem_clear(chain)
            links[eng] = 0

        def tokens(t):
            return slice(t * P, (t + 1) * P)

        def attention_signals():
            return {k: signal(f"att_{k}", n) for k, n in
                    (("input", 1), ("V1", 1), ("high", KT), ("low", KT), ("stacked", 2 * BLOCKS), ("q", BLOCKS), ("k", BLOCKS),
                     ("scores", UNITS), ("max", UNITS), ("maxsplit", BATCHES), ("maxturned", BATCHES), ("maxT", BATCHES),
                     ("scoresT", UNITS), ("exp", UNITS), ("pv", QUADS), ("outT", 2), ("outturned", 2), ("normed", 2))}

        def stack_bank(n):
            return 2 + (n + 4) % 5

        def pe_attention(pe, it, a, mask):
            def stack(g):
                if g % 4 == 0:
                    pe.wait_ge(*a["low"](it, g // 4 + 1))
                for n in (2 * g, 2 * g + 1):
                    if n >= 5:
                        pe.wait_ge(*a[("q", "k")[(n - 5) % 2]](it, (n - 5) // 2 + 1))
                    high, low, place = ((q_high, q_low, stack_q), (k_high, k_low, stack_k))[n % 2]
                    bank = stack_bank(n)
                    pe.matmul(PS[:, bank, :], place[:, 0, g % 4, :], high[:, g // 4, :], start=True, stop=False)
                    pe.matmul(PS[:, bank, :], place[:, 1, g % 4, :], low[:, g // 4, :], start=False, stop=True)\
                        .then_inc(a["stacked"].sem, 1)

            def scores(n):
                s, h = n // HEADS, n % HEADS
                g, r = h // 2, 64 * (h % 2)
                if n >= 2:
                    pe.wait_ge(*a["max"](it, n - 1))
                if mask is not None:
                    pe.matmul(PS[:, h % 2, :], identity16[:, :], mask[:, :, :], start=True, stop=False)
                for qt in range(2):
                    last = pe.matmul(PS[:, h % 2, qt * SEQ:(qt + 1) * SEQ],
                                     stacked_q[r:r + 64, g, s * SEQ + qt * P:s * SEQ + (qt + 1) * P],
                                     stacked_k[r:r + 64, g, s * SEQ:(s + 1) * SEQ], start=(mask is None),
                                     stop=(mask is None or qt == 1))
                last.then_inc(a["scores"].sem, 1)

            def scores_t(n):
                s, h = n // HEADS, n % HEADS
                g, r = h // 2, 64 * (h % 2)
                bank, slot = 2 + h % 2, n // BATCH_UNITS % 2
                if n >= 2:
                    pe.wait_ge(*a["exp"](it, n - 1))
                if mask is not None:
                    pe.matmul(PS[:, bank, :], identity16[:, :], mask[:, :, :], start=True, stop=False)
                pe.matmul(PS[:, bank, :].rearrange("p (k q) -> p k q", k=2), pick_head[:, n % BATCH_UNITS, :],
                          maxT[:, slot, :].unsqueeze(1).to_broadcast([P, 2, SEQ]), start=(mask is None), stop=False)
                for kt in range(2):
                    last = pe.matmul(PS[:, bank, kt * SEQ:(kt + 1) * SEQ],
                                     stacked_k[r:r + 64, g, s * SEQ + kt * P:s * SEQ + (kt + 1) * P],
                                     stacked_q[r:r + 64, g, s * SEQ:(s + 1) * SEQ], start=False, stop=(kt == 1))
                last.then_inc(a["scoresT"].sem, 1)

            def values(quad):
                pe.wait_ge(*a["exp"](it, 4 * quad + 4))
                for kt in range(2):
                    for n in range(4 * quad, 4 * quad + 4):
                        s, h = n // HEADS, n % HEADS
                        last = pe.matmul(PS[32 * (h % 4):32 * (h % 4) + 32, 4 + 2 * s + h // 8,
                                            (h // 4 % 2) * SEQ:(h // 4 % 2 + 1) * SEQ],
                                         V1[:, 2 * s + kt, h, :], prob[:, n % PROBS, kt, :], start=(kt == 0), stop=(kt == 1))
                last.then_inc(a["pv"].sem, 1)

            def turn_max(b):
                pe.wait_ge(*a["maxsplit"](it, b + 1))
                for qt in range(2):
                    last = pe.transpose(PS[:, 7, qt * P:(qt + 1) * P], max_split[:, qt, :].bitcast(F32), identity[:, :])
                last.then_inc(a["maxturned"].sem, 1)

            def turn_out(s):
                pe.wait_ge(*a["outT"](it, s + 1))
                for qt in range(2):
                    for g in range(4):
                        last = pe.transpose(PS[:, 4 + 2 * s + qt, g * P:(g + 1) * P],
                                            outT[:, g, qt * P:(qt + 1) * P], identity[:, :])
                last.then_inc(a["outturned"].sem, 1)

            stack(0)
            stack(1)
            pe.wait_ge(*a["V1"](it, 1))
            for n in range(UNITS + LAG):
                if n % 2 == 0 and n // 2 + 2 < BLOCKS:
                    stack(n // 2 + 2)
                if n % 2 == 0 and n // 2 < BLOCKS:
                    pe.wait_ge(*a["k"](it, n // 2 + 1))
                if n < UNITS:
                    scores(n)
                if n % BATCH_UNITS == 1 and 1 < n <= UNITS + 1:
                    turn_max(n // BATCH_UNITS - 1)
                t = n - LAG
                if t >= 0:
                    if t % BATCH_UNITS == 0:
                        pe.wait_ge(*a["maxT"](it, t // BATCH_UNITS + 1))
                    scores_t(t)
                    if t >= 5 and t % 4 == 1:
                        values(t // 4 - 1)
                    if t == HEADS + 6:
                        turn_out(0)
            values(QUADS - 1)
            turn_out(1)

        def act_attention(act, it, a, q_scale):
            act.wait_ge(*a["input"](it, 1))
            for ki in range(KT):
                act.activation(q_high[:, ki, :], qT[:, ki, :], ACT.Copy, scale=q_scale)
                act.activation(k_high[:, ki, :], kT[:, ki, :], ACT.Copy).then_inc(a["high"].sem, 1)
            for n in range(2 * BLOCKS):
                act.wait_ge(*a["stacked"](it, n + 1))
                dst, done = ((stacked_q, "q"), (stacked_k, "k"))[n % 2]
                act.activation(dst[:, n // 2, :], PS[:, stack_bank(n), :], ACT.Copy).then_inc(a[done].sem, 1)
            for n in range(UNITS):
                act.wait_ge(*a["scoresT"](it, n + 1))
                if n >= PROBS:
                    act.wait_ge(*a["pv"](it, (n - PROBS) // 4 + 1))
                act.activation(prob[:, n % PROBS, :, :].rearrange("p k q -> p (k q)"), PS[:, 2 + n % 2, :], ACT.Exp)\
                    .then_inc(a["exp"].sem, 1)
                if n == HEADS + 6:
                    act.wait_ge(*a["pv"](it, QUADS // 2))
                    act.activation(oT[:, :, :], PS[:, 4:6, :], ACT.Copy)\
                        .then_inc(a["outT"].sem, 1)
            act.wait_ge(*a["pv"](it, QUADS))
            act.wait_ge(*a["outturned"](it, 1))
            act.activation(oT[:, :, :], PS[:, 6:8, :], ACT.Copy)\
                .then_inc(a["outT"].sem, 1)

        def dve_attention(dve, it, a, q_scale, evacuate_values=None):
            for ki in range(KT):
                dve.wait_ge(*a["high"](it, ki + 1))
                dve.scalar_tensor_tensor(out=q_low[:, ki, :], in0=qT[:, ki, :], scalar=q_scale,
                                         in1=q_high[:, ki, :].bitcast(F32), op0=ALU.mult, op1=ALU.subtract)
                dve.tensor_tensor(k_low[:, ki, :], kT[:, ki, :], k_high[:, ki, :].bitcast(F32), ALU.subtract)\
                    .then_inc(a["low"].sem, 1)

            def copy_max(b):
                dve.wait_ge(*a["maxturned"](it, b + 1))
                if b >= 2:
                    dve.wait_ge(*a["scoresT"](it, (b - 1) * BATCH_UNITS))
                dve.tensor_copy(maxT[:, b % 2, :], PS[:, 7, 0:SEQ]).then_inc(a["maxT"].sem, 1)

            if evacuate_values is not None:
                evacuate_values()
            for n in range(UNITS):
                h = n % HEADS
                dve.wait_ge(*a["scores"](it, n + 1))
                dve.tensor_reduce(neg_max[:, :, h], PS[:, h % 2, :].rearrange("p (q k) -> p q k", q=2),
                                  AX.X, ALU.max, negate=True).then_inc(a["max"].sem, 1)
                b = n // BATCH_UNITS
                if n % BATCH_UNITS == BATCH_UNITS - 1:
                    dve.wait_ge(*a["max"](it, n + 1))
                    split = max_split[:, :, :].rearrange("p q (w r) -> p q w r", w=2)
                    twice = neg_max[:, :, h + 1 - BATCH_UNITS:h + 1].unsqueeze(2).to_broadcast([P, 2, 2, BATCH_UNITS])
                    high = split[:, :, :, 0:BATCH_UNITS]
                    link(dve, dve_chain, dve.tensor_copy(high, twice))
                    dve.tensor_tensor(split[:, :, :, BATCH_UNITS:2 * BATCH_UNITS], twice, high.bitcast(F32), ALU.subtract)\
                        .then_inc(a["maxsplit"].sem, 1)
                if n % BATCH_UNITS == 1 and b > 0:
                    copy_max(b - 1)
            copy_max(BATCHES - 1)
            for s in range(2):
                dve.wait_ge(*a["outturned"](it, s + 1))
                heads = PS[:, 4 + 2 * s:6 + 2 * s, :].rearrange("p q (h e) -> p q h e", e=32)
                link(dve, dve_chain, dve.reciprocal(inv_sum[:, s, :, :], heads[:, :, :, HD]))
                dve.tensor_tensor(o[:, 2 * s:2 * s + 2, :].rearrange("p q (h e) -> p q h e", e=HD), heads[:, :, :, 0:HD],
                                  inv_sum[:, s, :, :].unsqueeze(3).to_broadcast([P, 2, HEADS, HD]), ALU.mult)\
                    .then_inc(a["normed"].sem, 1)

        def pe_turn(pe, src, bank, tiles=TILES):
            for t in range(tiles):
                for ki in range(KT):
                    last = pe.transpose(PS[:, bank + t // 2, ((t % 2) * 2 + ki) * P:((t % 2) * 2 + ki + 1) * P],
                                        src[:, t, ki * P:(ki + 1) * P], identity[:, :])
            return last

        def act_turned(act, dst, bank, tiles=TILES):
            for b in range(tiles // 2):
                last = act.activation(
                    dst[:, :, 2 * b * P:(2 * b + 2) * P].rearrange("p k (t j) -> p t k j", t=2),
                    PS[:, bank + b, :].rearrange("p (t k j) -> p t k j", t=2, k=2), ACT.Copy)
            return last

        def dve_stats(dve, src, ready, tiles=TILES):
            for t in range(tiles):
                ins = dve.bn_stats(stats[:, t, :], src[:, t, :])
            link(dve, dve_chain, ins)
            for t in range(tiles):
                ins = dve.bn_aggr(mv[:, t, :], stats[:, t, :])
            link(dve, dve_chain, ins)
            dve.tensor_scalar(var_eps[:, 0:tiles], mv[:, 0:tiles, 1], LN_EPS, None, ALU.add).then_inc(ready.sem, 1)

        def dve_normalise(dve, dst, src, tiles=TILES):
            for t in range(tiles):
                ins = dve.tensor_scalar(dst[:, t, :], src[:, t, :], mv[:, t, 0:1], rstd[:, t:t + 1],
                                        ALU.subtract, ALU.mult)
            return ins

        def pool_rstd(pool, it, var_ready, rstd_ready, k=1, tiles=TILES):
            pool.wait_ge(*var_ready(it, k))
            pool.tensor_tensor(rstd[:, 0:tiles], var_eps[:, 0:tiles], minus_half[:, 0:tiles], ALU.pow).then_inc(rstd_ready.sem, 1)

        attention_buffers, phase1_buffers, phase2_buffers = ExitStack(), ExitStack(), ExitStack()
        stacked_q, stacked_k = (attention_buffers.enter_context(nc.sbuf_tensor(n, [P, BLOCKS, TOK], F32R))
                                for n in ("stacked_q", "stacked_k"))
        attention_buffers.close()
        STACKED = 2 * BLOCKS * TOK
        sb1 = lambda name, shape, dt=F32: phase1_buffers.enter_context(nc.sbuf_tensor(name, shape, dt))
        big = sb1("big", [P, TILES, 512])
        kw = big[:, :, :].rearrange("p t (f d) -> p t f d", f=2)
        qk = sb1("qk", [P, TILES, 512])
        vs = sb1("vs", [P, TILES, DIM])
        qkT = sb1("qkT", [P, 4, TOK])
        sb1("under_stacked1", [P, STACKED - TILES * (512 + 512 + DIM) - 4 * TOK])
        wqk = sb1("wqk", [P, KT, 2 * DIM])
        wvg = sb1("wvg", [P, KT, DIM + 48])
        wo = sb1("wo", [P, KT, DIM])
        xwq, xwk, xwv, xwo = (sb1(f"x{n}", [P, KT, DIM]) for n in ("wq", "wk", "wv", "wo"))
        wtf1 = sb1("wtf1", [P, KT, P])
        wtf2 = sb1("wtf2", [P, HEADS])
        gate0 = sb1("gate0", [P, KT, EXPERTS0])
        gate0_bias = sb1("gate0_bias", [1, EXPERTS0])
        decay_bias = sb1("decay_bias", [P, 48])
        btf1 = sb1("btf1", [P, 1])
        btf2 = sb1("btf2", [P, 1])
        nbtf1 = sb1("nbtf1", [P, 1])
        nbtf2 = sb1("nbtf2", [P, 1])
        wo_b = sb1("wo_b", [P, DIM])
        cosT = sb1("cosT", [P, TOK])
        sinT = sb1("sinT", [P, TOK])
        gate_sb = sb1("gate_sb", [P, TILES, 48])
        gate_exp = sb1("gate_exp", [P, TILES, 48])
        sig = sb1("sig", [P, TILES, 48])
        log_decay = sb1("log_decay", [P, TILES, 32])
        decay = sb1("decay", [P, TILES, 32])
        sumsq = sb1("sumsq", [P, P])
        root = sb1("root", [P, P])
        inv_norm = sb1("inv_norm", [P, P])
        inv_decay_sum = sb1("inv_decay_sum", [P, 64])
        memory = sb1("memory", [P, 2, 2, KT, P])
        hid_exp = sb1("hid_exp", [P, TOK])
        hid = sb1("hid", [P, TOK])
        flux = sb1("flux", [P, TILES * HEADS])
        alpha = sb1("alpha", [P, TILES, HEADS])
        one_minus = sb1("one_minus", [P, TILES, HEADS])
        rope_a = sb1("rope_a", [P, TOK])
        rope_b = sb1("rope_b", [P, TOK])
        meanT = sb1("meanT", [P, 4])
        logits8 = sb1("logits8", [1, 2, 8])
        top8 = sb1("top8", [1, 2, 8])
        top8_index = sb1("top8_index", [1, 2, 8], U32)
        neg_top = sb1("neg_top", [1, 2])
        logit_exp = sb1("logit_exp", [1, 2, 6])
        logit_sum = sb1("logit_sum", [1, 2])
        chosen_weight = sb1("chosen_weight", [1, 4])

        weights_loaded = signal("weights_loaded", 0)
        in1 = signal("in1", 48)
        one = {n: signal(f"l0_{n}", 2 if n in ("var", "rstd") else 1) for n in (
            "qkvg", "sq", "gz", "gexp", "sumsq", "root", "sig", "kb", "logd", "suffix", "decay", "turned", "qkT",
            "kw", "mem", "memory", "hid", "hexp", "hidden", "flux", "fexp", "o_ps", "o", "oturned", "oT", "y",
            "var", "rstd", "x1", "x1turned", "x1T", "kv", "q",
            "oturned2", "oT2", "y2", "x1b", "x2", "x2turned", "x2T", "mean", "meanT",
            "logits", "top", "lexp", "chosen", "spread", "chosen_out")}
        att1 = attention_signals()
        stored1 = signal("stored1", 32, base=32)

        mask_stage = [big[:, n, :].rearrange("p (t k) -> p t k", t=2) for n in range(2)]
        stack_stage = [qkT[:, 2 * n:2 * n + 2, :].rearrange("p n (g r) -> p n g r", g=4) for n in range(2)]
        X1_WEIGHTS = [(wqk, "wqk"), (wvg, "wvg"), (wo, "wo"), (xwq, "xwq"), (xwk, "xwk"), (xwv, "xwv"), (xwo, "xwo"),
                      (wtf1, "wtf1"), (wtf2, "wtf2"), (gate0, "gate0"), (gate0_bias, "gate0_bias"),
                      (decay_bias, "decay_bias"), (btf1, "btf1"), (btf2, "btf2"), (wo_b, "wo_b"),
                      (cosT, "cosT"), (sinT, "sinT"), (stack_stage[0], "stack_q"), (stack_stage[1], "stack_k"),
                      (qk[:, 0:2, :], "pick_head"),
                      (block_diag, "block_diag"), (identity, "identity"),
                      (after, "after"), (upto, "upto"), (mask_stage[0], "window_mask"), (mask_stage[1], "causal_mask")]
        WEIGHTS1 = 16 * len(X1_WEIGHTS)

        def rows(ap, it, n):
            return ap[bass.ds(it * (n * P), n * P), :].rearrange("(t p) f -> p t f", p=P)

        def columns(ap, it, n):
            return ap[:, bass.ds(it * n * P, n * P)].rearrange("(k p) t -> p k t", p=P)

        def sp_load1(sp, it):
            sp.dma_start(xT[:, :, :], columns(d["xT"], it, TILES)).then_inc(in1.sem, 16)
            sp.dma_start(cT[:, :, :], columns(d["ctxT"], it, TILES)).then_inc(in1.sem, 16)
            sp.dma_start(x[:, :, :], rows(d["x"], it, TILES)).then_inc(in1.sem, 16)

        def sp_store1(sp, it):
            sp.wait_ge(*one["x2"](it, 1))
            sp.dma_start(rows(xs["x2"], it, TILES), y[:, :, :]).then_inc(stored1.sem, 16)
            sp.wait_ge(*one["x2T"](it, 1))
            sp.dma_start(columns(xsT["x2"], it, TILES), yT[:, :, :]).then_inc(stored1.sem, 16)

        def sp_phase1(sp):
            sp.sem_inc(stored1.sem, 32)
            for dst, name in X1_WEIGHTS:
                sp.dma_start(dst[tuple(slice(None) for _ in dst.shape)], d[name]).then_inc(weights_loaded.sem, 16)
            sp_load1(sp, 0)
            with sp.Fori(0, PAIRS - 1) as it:
                sp.wait_ge(*one["x1"](it, 1))
                sp.wait_ge(*one["kv"](it, 1))
                sp_load1(sp, it + 1)
                sp_store1(sp, it)
            sp_store1(sp, PAIRS - 1)
            sp.wait_ge(*stored1(PAIRS - 1, 32))

        def pe_phase1(pe):
            pe.wait_ge(weights_loaded.sem, WEIGHTS1)
            pe.wait_ge(*consts_ready(0, 1))
            with pe.Fori(0, PAIRS) as it:
                pe.wait_ge(*in1(it, 48))
                for t in range(TILES):
                    for ki in range(KT):
                        pe.matmul(PS[:, t, :], xT[:, ki, tokens(t)], wqk[:, ki, :], start=(ki == 0), stop=(ki == 1))
                    for ki in range(KT):
                        last = pe.matmul(PS[:, 4 + t, 0:DIM + 48], xT[:, ki, tokens(t)], wvg[:, ki, :],
                                         start=(ki == 0), stop=(ki == 1))
                last.then_inc(one["qkvg"].sem, 1)
                pe.wait_ge(*one["kb"](it, 1))
                pe.wait_ge(*one["logd"](it, 1))
                for s in range(2):
                    first, second = log_decay[:, 2 * s, :], log_decay[:, 2 * s + 1, :]
                    pe.matmul(PS[:, 0, 64 * s:64 * s + 32], after[:, :], first, start=True, stop=False)
                    pe.matmul(PS[:, 0, 64 * s:64 * s + 32], ones[:, :], second, start=False, stop=True)
                    last = pe.matmul(PS[:, 0, 64 * s + 32:64 * s + 64], after[:, :], second, start=True, stop=True)
                last.then_inc(one["suffix"].sem, 1)
                for t in range(TILES):
                    for cc in range(4):
                        last = pe.transpose(PS[:, 1 + t, cc * P:(cc + 1) * P], qk[:, t, cc * P:(cc + 1) * P],
                                            identity[:, :])
                last.then_inc(one["turned"].sem, 1)
                pe.wait_ge(*one["kw"](it, 1))
                for s in range(2):
                    for tt in range(2):
                        pe.matmul(PS[:, 7, 32 * s:32 * s + 32], ones[:, :], decay[:, 2 * s + tt, :],
                                  start=(tt == 0), stop=(tt == 1))
                    for fs in range(2):
                        for half in range(KT):
                            for tt in range(2):
                                last = pe.matmul(PS[:, 5 + s, (fs * 2 + half) * P:(fs * 2 + half + 1) * P],
                                                 kw[:, 2 * s + tt, fs, half * P:(half + 1) * P],
                                                 vs[:, 2 * s + tt, half * P:(half + 1) * P],
                                                 start=(tt == 0), stop=(tt == 1))
                last.then_inc(one["mem"].sem, 1)
                pe.wait_ge(*one["decay"](it, 1))
                pe.wait_ge(*one["qkT"](it, 1))
                for ki in range(KT):
                    last = pe.matmul(PS[:, 0, :], wtf1[:, ki, :], qkT[:, 2 + ki, :], start=(ki == 0), stop=(ki == 1))
                last.then_inc(one["hid"].sem, 1)
                pe.wait_ge(*one["hidden"](it, 1))
                for t in range(TILES):
                    last = pe.matmul(PS[:, 1, t * HEADS:(t + 1) * HEADS], hid[:, tokens(t)], wtf2[:, :],
                                     start=True, stop=True)
                last.then_inc(one["flux"].sem, 1)
                pe.wait_ge(*one["memory"](it, 1))
                for t in range(TILES):
                    for half in range(KT):
                        last = pe.matmul(PS[:, 2 + t, half * 2 * P:(half + 1) * 2 * P], qkT[:, half, tokens(t)],
                                         memory[:, t // 2, :, half, :],
                                         start=True, stop=True)
                last.then_inc(one["o_ps"].sem, 1)
                pe.wait_ge(*one["o"](it, 1))
                pe_turn(pe, o, 6).then_inc(one["oturned"].sem, 1)
                for blk in range(2):
                    for ki in range(KT):
                        pe.matmul(PS[:, 4 + blk, :], xwk[:, ki, blk * P:(blk + 1) * P], cT[:, ki, :],
                                  start=(ki == 0), stop=(ki == 1))
                for t in range(TILES):
                    for ki in range(KT):
                        last = pe.matmul(PS[:, 2 + t // 2, (t % 2) * DIM:(t % 2 + 1) * DIM], cT[:, ki, tokens(t)],
                                         xwv[:, ki, :], start=(ki == 0), stop=(ki == 1))
                last.then_inc(one["kv"].sem, 1)
                pe.wait_ge(*one["oT"](it, 1))
                for t in range(TILES):
                    for ki in range(KT):
                        last = pe.matmul(PS[:, t // 2, (t % 2) * DIM:(t % 2 + 1) * DIM], oT[:, ki, tokens(t)],
                                         wo[:, ki, :], start=(ki == 0), stop=(ki == 1))
                last.then_inc(one["y"].sem, 1)
                pe.wait_ge(*one["x1"](it, 1))
                pe_turn(pe, xn, 6).then_inc(one["x1turned"].sem, 1)
                pe.wait_ge(*one["x1T"](it, 1))
                for blk in range(2):
                    for ki in range(KT):
                        last = pe.matmul(PS[:, blk, :], xwq[:, ki, blk * P:(blk + 1) * P], xnT[:, ki, :],
                                         start=(ki == 0), stop=(ki == 1))
                last.then_inc(one["q"].sem, 1)
                pe_attention(pe, it, att1, window_mask)
                pe.wait_ge(*att1["normed"](it, 2))
                pe_turn(pe, o, 6).then_inc(one["oturned2"].sem, 1)
                pe.wait_ge(*one["oT2"](it, 1))
                for t in range(TILES):
                    for ki in range(KT):
                        last = pe.matmul(PS[:, t // 2, (t % 2) * DIM:(t % 2 + 1) * DIM], oT[:, ki, tokens(t)],
                                         xwo[:, ki, :], start=(ki == 0), stop=(ki == 1))
                last.then_inc(one["y2"].sem, 1)
                pe.wait_ge(*one["x2"](it, 1))
                pe_turn(pe, y, 6).then_inc(one["x2turned"].sem, 1)
                for s in range(2):
                    for half in range(KT):
                        for tt in range(2):
                            last = pe.matmul(PS[:, 4, s * 2 + half:s * 2 + half + 1],
                                             y[:, 2 * s + tt, half * P:(half + 1) * P], mean_col[:, :],
                                             start=(tt == 0), stop=(tt == 1))
                last.then_inc(one["mean"].sem, 1)
                pe.wait_ge(*one["meanT"](it, 1))
                for s in range(2):
                    for ki in range(KT):
                        last = pe.matmul(PS[0:1, 5, s * 8:s * 8 + EXPERTS0], meanT[:, s * 2 + ki:s * 2 + ki + 1],
                                         gate0[:, ki, :], start=(ki == 0), stop=(ki == 1))
                last.then_inc(one["logits"].sem, 1)
                pe.wait_ge(*one["chosen"](it, 1))
                pe.matmul(PS[:, 4, 0:4], ones[0:1, :], chosen_weight[:, :], start=True, stop=True)\
                    .then_inc(one["spread"].sem, 1)
                pe.wait_ge(*one["x2T"](it, 1))
                pe.wait_ge(*one["chosen_out"](it, 1))

        def act_phase1(act):
            act.wait_ge(weights_loaded.sem, WEIGHTS1)
            act.wait_ge(*consts_ready(0, 1))
            with act.Fori(0, PAIRS) as it:
                act.wait_ge(*one["qkvg"](it, 1))
                act.activation(big[:, :, :], PS[:, 0:4, :], ACT.Square).then_inc(one["sq"].sem, 1)
                act.wait_ge(*one["gz"](it, 1))
                act.activation(gate_exp[:, :, :], gate_sb[:, :, :], ACT.Exp, scale=-1.0).then_inc(one["gexp"].sem, 1)
                act.wait_ge(*one["sumsq"](it, 1))
                act.activation(root[:, :], sumsq[:, :], ACT.Sqrt).then_inc(one["root"].sem, 1)
                act.wait_ge(*one["sig"](it, 1))
                act.activation(log_decay[:, :, :], sig[:, :, 16:48], ACT.Ln, bias=eps6[:, :])\
                    .then_inc(one["logd"].sem, 1)
                act.wait_ge(*one["suffix"](it, 1))
                act.activation(decay[:, :, :], PS[:, 0, 0:128].rearrange("p (t h) -> p t h", t=TILES), ACT.Exp)\
                    .then_inc(one["decay"].sem, 1)
                act.wait_ge(*one["turned"](it, 1))
                act.activation(qkT[:, :, :].rearrange("p c (t j) -> p t c j", t=TILES),
                               PS[:, 1:5, :].rearrange("p t (c j) -> p t c j", c=4), ACT.Copy)\
                    .then_inc(one["qkT"].sem, 1)
                act.wait_ge(*one["hid"](it, 1))
                act.activation(hid_exp[:, :], PS[:, 0, :], ACT.Exp, bias=nbtf1[:, :], scale=-1.0)\
                    .then_inc(one["hexp"].sem, 1)
                act.wait_ge(*one["flux"](it, 1))
                act.activation(flux[:, :], PS[:, 1, 0:64], ACT.Exp, bias=nbtf2[:, :], scale=-1.0)\
                    .then_inc(one["fexp"].sem, 1)
                act.wait_ge(*one["oturned"](it, 1))
                act_turned(act, oT, 6).then_inc(one["oT"].sem, 1)
                act.wait_ge(*one["kv"](it, 1))
                for b in range(2):
                    last = act.activation(V1[:, 2 * b:2 * b + 2, :, 0:HD],
                                          PS[:, 2 + b, :].rearrange("p (t h e) -> p t h e", t=2, h=HEADS), ACT.Copy)
                last.then_inc(att1["V1"].sem, 1)
                act.wait_ge(*one["x1turned"](it, 1))
                act_turned(act, xnT, 6).then_inc(one["x1T"].sem, 1)
                act_attention(act, it, att1, 1.0)
                act.wait_ge(*one["oturned2"](it, 1))
                act_turned(act, oT, 6).then_inc(one["oT2"].sem, 1)
                act.wait_ge(*one["x2turned"](it, 1))
                act.wait_ge(*stored1(it, 0))
                act_turned(act, yT, 6).then_inc(one["x2T"].sem, 1)
                act.wait_ge(*one["top"](it, 1))
                for s in range(2):
                    act.activation(logit_exp[:, s, 0:EXPERTS0], logits8[:, s, 0:EXPERTS0], ACT.Exp,
                                   bias=neg_top[:, s:s + 1], accum_out=logit_sum[:, s:s + 1])
                    last = act.activation(logit_exp[:, s, 4:6], top8[:, s, 0:2], ACT.Exp, bias=neg_top[:, s:s + 1])
                last.then_inc(one["lexp"].sem, 1)

        def dve_phase1(dve):
            dve.wait_ge(weights_loaded.sem, WEIGHTS1)
            link(dve, dve_chain, dve.memset(V1[:, :, :, :], 0.0))
            dve.memset(V1[:, :, :, HD:HD + 1], 1.0)
            for n, dst in enumerate((stack_q, stack_k)):
                dve.tensor_copy(dst[:, :, :, :], stack_stage[n])
            dve.tensor_copy(pick_head[:, :, :].rearrange("p h k -> p (h k)"),
                            qk[:, 0:2, :].rearrange("p t f -> p (t f)"))
            dve.memset(max_split[:, :, :].bitcast(F32), 0.0)
            dve.memset(logits8[:, :, :], FAR)
            dve.tensor_scalar(nbtf1[:, :], btf1[:, :], -1.0, None, ALU.mult)
            link(dve, dve_chain, dve.tensor_scalar(nbtf2[:, :], btf2[:, :], -1.0, None, ALU.mult))
            dve.memset(eps6[:, :], 1e-6)
            dve.tensor_copy(window_mask[:, :, :], mask_stage[0])
            dve.tensor_copy(causal_mask[:, :, :], mask_stage[1])
            dve.tensor_copy(identity16[:, :], identity[:, :])
            dve.memset(mean_col[:, :], 1.0 / SEQ)
            dve.memset(minus_half[:, :], -0.5)
            dve.memset(ones[:, :], 1.0).then_inc(consts_ready.sem, 1)
            dve.wait_ge(*consts_ready(0, 1))
            with dve.Fori(0, PAIRS) as it:
                restart(dve, dve_chain)
                heads = lambda ap: ap.rearrange("p t (h e) -> p t h e", e=HD)
                spread = lambda ap: ap.unsqueeze(3).to_broadcast([P, TILES, HEADS, HD])
                dve.wait_ge(*one["qkvg"](it, 1))
                dve.tensor_tensor(gate_sb[:, :, :], PS[:, 4:8, DIM:DIM + 48],
                                  decay_bias[:, :].unsqueeze(1).to_broadcast([P, TILES, 48]),
                                  ALU.add).then_inc(one["gz"].sem, 1)
                dve.wait_ge(*one["sq"](it, 1))
                link(dve, dve_chain, dve.tensor_reduce(sumsq[:, :], big[:, :, :].rearrange("p t (h e) -> p (t h) e", e=HD),
                                                       AX.X, ALU.add))
                dve.tensor_scalar(sumsq[:, :], sumsq[:, :], 1e-24, None, ALU.max).then_inc(one["sumsq"].sem, 1)
                dve.wait_ge(*one["gexp"](it, 1))
                link(dve, dve_chain, dve.tensor_scalar(gate_exp[:, :, :], gate_exp[:, :, :], 1.0, None, ALU.add))
                dve.reciprocal(sig[:, :, :], gate_exp[:, :, :]).then_inc(one["sig"].sem, 1)
                dve.wait_ge(*one["sig"](it, 1))
                dve.tensor_tensor(heads(vs[:, :, :]), heads(PS[:, 4:8, 0:DIM]), spread(sig[:, :, 0:HEADS]), ALU.mult)
                dve.wait_ge(*one["root"](it, 1))
                link(dve, dve_chain, dve.reciprocal(inv_norm[:, :], root[:, :]))
                link(dve, dve_chain, dve.tensor_tensor(root[:, :], inv_norm[:, :], inv_norm[:, :], ALU.mult))
                link(dve, dve_chain, dve.tensor_tensor(root[:, :], root[:, :], sumsq[:, :], ALU.mult))
                link(dve, dve_chain, dve.tensor_scalar(root[:, :], root[:, :], -0.5, 1.5, ALU.mult, ALU.add))
                link(dve, dve_chain, dve.tensor_tensor(inv_norm[:, :], inv_norm[:, :], root[:, :], ALU.mult))
                link(dve, dve_chain, dve.tensor_tensor(
                    qk[:, :, :].rearrange("p t (h e) -> p (t h) e", e=HD),
                    PS[:, 0:4, :].rearrange("p t (h e) -> p (t h) e", e=HD),
                    inv_norm[:, :].unsqueeze(2).to_broadcast([P, P, HD]), ALU.mult))
                kbeta = heads(qk[:, :, DIM:2 * DIM])
                dve.tensor_tensor(kbeta, kbeta, spread(sig[:, :, 0:HEADS]), ALU.mult).then_inc(one["kb"].sem, 1)
                dve.wait_ge(*one["kb"](it, 1))
                dve.wait_ge(*one["decay"](it, 1))
                for fs in range(2):
                    last = dve.tensor_tensor(heads(kw[:, :, fs, :]), kbeta,
                                             spread(decay[:, :, fs * HEADS:(fs + 1) * HEADS]), ALU.mult)
                last.then_inc(one["kw"].sem, 1)
                dve.wait_ge(*one["mem"](it, 1))
                link(dve, dve_chain, dve.tensor_scalar(inv_decay_sum[:, :], PS[:, 7, 0:64], 1e-6, None, ALU.add))
                link(dve, dve_chain, dve.reciprocal(inv_decay_sum[:, :], inv_decay_sum[:, :]))
                for s in range(2):
                    scaled = memory[:, s, :, :, :].rearrange("p f k (h e) -> p (f k h) e", e=HD)
                    flat_memory = memory[:, s, :, :, :].rearrange("p f k e -> p (f k) e")
                    link(dve, dve_chain, dve.tensor_tensor(
                        scaled, PS[:, 5 + s, :].rearrange("p (g e) -> p g e", e=HD),
                        inv_decay_sum[:, 32 * s:32 * s + 32].unsqueeze(2).to_broadcast([P, 32, HD]), ALU.mult))
                    last = dve.tensor_tensor(flat_memory, flat_memory,
                                             block_diag[:, :].unsqueeze(1).to_broadcast([P, 4, P]), ALU.mult)
                last.then_inc(one["memory"].sem, 1)
                dve.wait_ge(*one["hexp"](it, 1))
                link(dve, dve_chain, dve.tensor_scalar(hid_exp[:, :], hid_exp[:, :], 1.0, None, ALU.add))
                link(dve, dve_chain, dve.reciprocal(hid_exp[:, :], hid_exp[:, :]))
                dve.scalar_tensor_tensor(out=hid[:, :], in0=PS[:, 0, :], scalar=btf1[:, :], in1=hid_exp[:, :],
                                         op0=ALU.add, op1=ALU.mult).then_inc(one["hidden"].sem, 1)
                dve.wait_ge(*one["fexp"](it, 1))
                link(dve, dve_chain, dve.tensor_scalar(flux[:, :], flux[:, :], 1.0, None, ALU.add))
                link(dve, dve_chain, dve.reciprocal(flux[:, :], flux[:, :]))
                link(dve, dve_chain, dve.tensor_scalar(flux[:, :], flux[:, :], 0.01, 0.99, ALU.max, ALU.min))
                flat = lambda ap: ap.rearrange("p t h -> p (t h)")
                link(dve, dve_chain, dve.tensor_scalar(flat(alpha[:, :, :]), flux[:, :], 0.3, 0.5, ALU.mult, ALU.add))
                link(dve, dve_chain, dve.tensor_scalar(flat(one_minus[:, :, :]), flat(alpha[:, :, :]), -1.0, 1.0,
                                                       ALU.mult, ALU.add))
                dve.wait_ge(*one["o_ps"](it, 1))
                for t in range(TILES):
                    for fs, (dst, w) in enumerate(((o, alpha), (rr, one_minus))):
                        last = dve.tensor_tensor(
                            dst[:, t, :].rearrange("p (k h e) -> p k h e", k=KT, e=HD),
                            PS[:, 2 + t, :].rearrange("p (k f h e) -> p k f h e", k=KT, f=2, e=HD)[:, :, fs, :, :],
                            w[:, t, :].rearrange("p (k h) -> p k h", k=KT).unsqueeze(3).to_broadcast([P, KT, 8, HD]),
                            ALU.mult)
                link(dve, dve_chain, last)
                dve.tensor_tensor(o[:, :, :], o[:, :, :], rr[:, :, :], ALU.add).then_inc(one["o"].sem, 1)

                def rope(pa, pb, scale, dst):
                    for sign, first, second, blk in ((ALU.subtract, cosT, sinT, 0), (ALU.add, sinT, cosT, 1)):
                        dve.scalar_tensor_tensor(out=rope_a[:, :], in0=pa, scalar=scale, in1=first[:, :],
                                                 op0=ALU.mult, op1=ALU.mult)
                        link(dve, dve_chain, dve.scalar_tensor_tensor(out=rope_b[:, :], in0=pb, scalar=scale,
                                                                      in1=second[:, :], op0=ALU.mult, op1=ALU.mult))
                        link(dve, dve_chain, dve.tensor_tensor(dst[:, blk, :], rope_a[:, :], rope_b[:, :], sign))

                dve.wait_ge(*one["kv"](it, 1))
                rope(PS[:, 4, :], PS[:, 5, :], 1.0, kT)
                pair2 = lambda b: PS[:, b:b + 2, :].rearrange("p b (t f) -> p (b t) f", t=2)
                dve.wait_ge(*one["y"](it, 1))
                link(dve, dve_chain, dve.tensor_tensor(rr[:, :, :], pair2(0), x[:, :, :], ALU.add))
                dve_stats(dve, rr, one["var"])
                dve.wait_ge(*one["rstd"](it, 1))
                dve_normalise(dve, xn, rr).then_inc(one["x1"].sem, 1)
                dve.wait_ge(*one["q"](it, 1))
                rope(PS[:, 0, :], PS[:, 1, :], float(HD) ** 0.5, qT)
                dve.sem_inc(att1["input"].sem, 1)
                dve_attention(dve, it, att1, 1.0)
                dve.wait_ge(*one["y2"](it, 1))
                dve.wait_ge(*one["x1b"](it, 1))
                link(dve, dve_chain, dve.tensor_tensor(rr[:, :, :], pair2(0), xb[:, :, :], ALU.add))
                dve_stats(dve, rr, one["var"])
                dve.wait_ge(*one["rstd"](it, 2))
                dve.wait_ge(*stored1(it, 0))
                dve_normalise(dve, y, rr).then_inc(one["x2"].sem, 1)
                dve.wait_ge(*one["mean"](it, 1))
                dve.tensor_copy(meanT[:, :], PS[:, 4, 0:4]).then_inc(one["meanT"].sem, 1)
                dve.wait_ge(*one["logits"](it, 1))
                link(dve, dve_chain, dve.tensor_tensor(
                    logits8[:, :, 0:EXPERTS0], PS[0:1, 5, 0:16].rearrange("p (s e) -> p s e", s=2)[:, :, 0:EXPERTS0],
                    gate0_bias[:, :].unsqueeze(1).to_broadcast([1, 2, EXPERTS0]), ALU.add))
                for s in range(2):
                    last = dve.max(top8[:, s, :], logits8[:, s, :])
                link(dve, dve_chain, last)
                dve.tensor_scalar(neg_top[:, :], top8[:, :, 0], -1.0, None, ALU.mult).then_inc(one["top"].sem, 1)
                for s in range(2):
                    last = dve.max_index(top8_index[:, s, :], top8[:, s, :], logits8[:, s, :])
                link(dve, dve_chain, last)
                dve.tensor_copy(expert_index[:, bass.ds(it * 4, 4)].rearrange("p (s e) -> p s e", s=2),
                                top8_index[:, :, 0:2])
                dve.wait_ge(*one["lexp"](it, 1))
                link(dve, dve_chain, dve.reciprocal(logit_sum[:, :], logit_sum[:, :]))
                dve.tensor_tensor(chosen_weight[:, :].rearrange("p (s e) -> p s e", s=2), logit_exp[:, :, 4:6],
                                  logit_sum[:, :].unsqueeze(2).to_broadcast([1, 2, 2]),
                                  ALU.mult).then_inc(one["chosen"].sem, 1)
                dve.wait_ge(*one["spread"](it, 1))
                dve.tensor_copy(gate_weight[:, bass.ds(it * 4, 4)], PS[:, 4, 0:4]).then_inc(one["chosen_out"].sem, 1)
                dve.wait_ge(*one["chosen_out"](it, 1))

        def pool_phase1(pool):
            pool.wait_ge(weights_loaded.sem, WEIGHTS1)
            pool.wait_ge(*consts_ready(0, 1))
            with pool.Fori(0, PAIRS) as it:
                pool_rstd(pool, it, one["var"], one["rstd"])
                pool.wait_ge(*one["x1"](it, 1))
                pool.tensor_tensor(xb[:, :, :], xn[:, :, :], wo_b[:, :].unsqueeze(1).to_broadcast([P, TILES, DIM]),
                                   ALU.add).then_inc(one["x1b"].sem, 1)
                pool_rstd(pool, it, one["var"], one["rstd"], 2)

        phase1_buffers.close()
        ctx.enter_context(phase2_buffers)
        sb2 = lambda name, shape, dt=F32: phase2_buffers.enter_context(nc.sbuf_tensor(name, shape, dt))
        hT = sb2("hT", [P, 2, FB, SEQ])
        sb2("under_stacked2", [P, STACKED - 2 * FB * SEQ])
        W_QKV, W_OUT, W_UP, W_DOWN = 2 * 768 + DIM + 4, 2 * DIM + 3 * DIM, KT * DFF + FB, FB * DIM + 3 * DIM
        w_qkv = sb2("w_qkv", [P, 2, W_QKV])
        w_out = sb2("w_out", [P, 2, W_OUT])
        w_up = sb2("w_up", [P, 2, W_UP])
        w_down = sb2("w_down", [P, 2, W_DOWN])

        in2 = signal("in2", 16)
        in2x = signal("in2x", 16)
        loaded2 = {n: signal(f"{n}_loaded", 32) for n in ("qkv", "out", "up", "down")}
        two = {n: signal(f"f_{n}", per) for n, per in (
            ("qkv", 2), ("xb", 1), ("oturned", 1), ("oT", 1), ("y", 1), ("xp", 1),
            ("xpb", 1), ("xpturned", 1), ("xpT", 1), ("h", 8), ("h_act", 4), ("h_dve", 4), ("y2", 1),
            ("x3", 1), ("x3turned", 1), ("x3T", 1), ("normed2", 1))}
        two["var"], two["rstd"] = (one[n].after(PAIRS, 3) for n in ("var", "rstd"))
        att2 = {k: s.after(PAIRS) for k, s in att1.items()}
        stored2 = stored1.after(PAIRS)
        QK_BANK, V_BANK = (2, 5), (1, 7)
        PIECES = (("qkv", w_qkv, "f_qkv"), ("out", w_out, "f_out"), ("up", w_up, "f_up"), ("down", w_down, "f_down"))

        def sp_piece(sp, it, expert, n):
            name, dst, src = PIECES[n]
            for e in range(2):
                sp.dma_start(dst[:, e, :], d[src][bass.ds(expert[e], 1), :, :].rearrange("a p n -> p (a n)"))\
                    .then_inc(loaded2[name].sem, 16)

        def sp_experts(sp, it):
            return [sp.value_load(expert_index[0:1, bass.ds(it * 2 + e, 1)], min_val=0, max_val=EXPERTS0 - 1)
                    for e in range(2)]

        def sp_store2(sp, it):
            sp.wait_ge(*two["x3"](it, 1))
            sp.dma_start(rows(xs["x3"], it, 2), y[:, 0:2, :]).then_inc(stored2.sem, 16)
            sp.wait_ge(*two["x3T"](it, 1))
            sp.dma_start(columns(xsT["x3"], it, 2), yT[:, :, 0:SEQ]).then_inc(stored2.sem, 16)

        def sp_phase2(sp):
            sp.wait_ge(*one["chosen_out"](PAIRS - 1, 1))
            sp.dma_start(xT[:, :, 0:SEQ], columns(xsT["x2"], 0, 2)).then_inc(in2.sem, 16)
            sp.dma_start(x[:, 0:2, :], rows(xs["x2"], 0, 2)).then_inc(in2x.sem, 16)
            expert = sp_experts(sp, 0)
            for n in range(4):
                sp_piece(sp, 0, expert, n)
            with sp.Fori(0, BATCH - 1) as it:
                expert = sp_experts(sp, it + 1)
                sp.wait_ge(*two["oturned"](it, 1))
                sp.dma_start(xT[:, :, 0:SEQ], columns(xsT["x2"], it + 1, 2)).then_inc(in2.sem, 16)
                sp_piece(sp, it + 1, expert, 0)
                sp.wait_ge(*two["xp"](it, 1))
                sp_piece(sp, it + 1, expert, 1)
                sp.wait_ge(*two["h_act"](it, 4))
                sp.wait_ge(*two["h_dve"](it, 4))
                sp_piece(sp, it + 1, expert, 2)
                sp.wait_ge(*two["normed2"](it, 1))
                sp_piece(sp, it + 1, expert, 3)
                sp.dma_start(x[:, 0:2, :], rows(xs["x2"], it + 1, 2)).then_inc(in2x.sem, 16)
                sp_store2(sp, it)
            sp_store2(sp, BATCH - 1)
            sp.wait_ge(*stored2(BATCH - 1, 32))

        def pe_phase2(pe):
            def project(it):
                pe.wait_ge(*in2(it, 16))
                pe.wait_ge(*loaded2["qkv"](it, 32))
                for e in range(2):
                    for blk in range(4):
                        for ki in range(KT):
                            pe.matmul(PS[:, QK_BANK[e] + blk // 2, (blk % 2) * SEQ:(blk % 2 + 1) * SEQ],
                                      w_qkv[:, e, ki * 768 + blk * P:ki * 768 + (blk + 1) * P], xT[:, ki, 0:SEQ],
                                      start=(ki == 0), stop=(ki == 1))
                    for tt in range(2):
                        for ki in range(KT):
                            last = pe.matmul(PS[:, V_BANK[e], tt * DIM:(tt + 1) * DIM], xT[:, ki, tokens(tt)],
                                             w_qkv[:, e, ki * 768 + 2 * DIM:ki * 768 + 3 * DIM],
                                             start=(ki == 0), stop=(ki == 1))
                    last.then_inc(two["qkv"].sem, 1)

            def mix(it):
                pe_attention(pe, it, att2, None)
                pe.wait_ge(*att2["normed"](it, 2))
                pe_turn(pe, o, 6).then_inc(two["oturned"].sem, 1)
                pe.wait_ge(*loaded2["out"](it, 32))
                pe.wait_ge(*two["oT"](it, 1))
                for t in range(TILES):
                    for ki in range(KT):
                        last = pe.matmul(PS[:, t // 2, (t % 2) * DIM:(t % 2 + 1) * DIM], oT[:, ki, tokens(t)],
                                         w_out[:, t // 2, ki * DIM:(ki + 1) * DIM], start=(ki == 0), stop=(ki == 1))
                last.then_inc(two["y"].sem, 1)
                pe.wait_ge(*two["xp"](it, 1))
                pe_turn(pe, xn, 6).then_inc(two["xpturned"].sem, 1)
                pe.wait_ge(*loaded2["up"](it, 32))
                pe.wait_ge(*two["xpT"](it, 1))
                for e in range(2):
                    for blk in range(FB):
                        for ki in range(KT):
                            last = pe.matmul(PS[:, 4 * e + blk // 2, (blk % 2) * SEQ:(blk % 2 + 1) * SEQ],
                                             w_up[:, e, ki * DFF + blk * P:ki * DFF + (blk + 1) * P],
                                             xnT[:, ki, e * SEQ:(e + 1) * SEQ], start=(ki == 0), stop=(ki == 1))
                        if blk % 2:
                            last.then_inc(two["h"].sem, 1)
                pe.wait_ge(*loaded2["down"](it, 32))
                for e in range(2):
                    pe.wait_ge(*two["h_act"](it, 2 * (e + 1)))
                    pe.wait_ge(*two["h_dve"](it, 2 * (e + 1)))
                    for tt in range(2):
                        for ki in range(FB):
                            last = pe.matmul(PS[:, 4 * e, tt * DIM:(tt + 1) * DIM], hT[:, e, ki, tokens(tt)],
                                             w_down[:, e, ki * DIM:(ki + 1) * DIM], start=(ki == 0), stop=(ki == FB - 1))
                last.then_inc(two["y2"].sem, 1)

            def turn(it):
                pe.wait_ge(*two["x3"](it, 1))
                pe_turn(pe, y, 0, 2).then_inc(two["x3turned"].sem, 1)

            project(0)
            with pe.Fori(0, BATCH - 1) as it:
                mix(it)
                project(it + 1)
                turn(it)
            mix(BATCH - 1)
            turn(BATCH - 1)

        def act_phase2(act):
            def project(it):
                bias0 = 2 * 768 + DIM
                for e in range(2):
                    act.wait_ge(*two["qkv"](it, e + 1))
                    for dst, n in ((qT, 0), (kT, 1)):
                        for blk in range(KT):
                            col = bias0 + 2 * n + blk
                            last = act.activation(dst[:, blk, e * SEQ:(e + 1) * SEQ],
                                                  PS[:, QK_BANK[e] + n, blk * SEQ:(blk + 1) * SEQ], ACT.Identity,
                                                  bias=w_qkv[:, e, col:col + 1])
                last.then_inc(att2["input"].sem, 1)

            def mix(it):
                act_attention(act, it, att2, float(HD) ** -0.5)
                act.wait_ge(*two["oturned"](it, 1))
                act_turned(act, oT, 6).then_inc(two["oT"].sem, 1)
                act.wait_ge(*two["xpturned"](it, 1))
                act_turned(act, xnT, 6).then_inc(two["xpT"].sem, 1)
                for b in range(0, 8, 2):
                    act.wait_ge(*two["h"](it, b + 1))
                    for j in range(2):
                        e, blk = b // 4, 2 * (b % 4) + j
                        last = act.activation(hT[:, e, blk, :], PS[:, b, j * SEQ:(j + 1) * SEQ], ACT.Relu,
                                              bias=w_up[:, e, KT * DFF + blk:KT * DFF + blk + 1])
                    last.then_inc(two["h_act"].sem, 1)

            def turned(it):
                act.wait_ge(*two["x3turned"](it, 1))
                act.wait_ge(*stored2(it, 0))
                act_turned(act, yT, 0, 2).then_inc(two["x3T"].sem, 1)

            project(0)
            with act.Fori(0, BATCH - 1) as it:
                mix(it)
                project(it + 1)
                turned(it)
            mix(BATCH - 1)
            turned(BATCH - 1)

        def dve_phase2(dve):
            with dve.Fori(0, BATCH) as it:
                restart(dve, dve_chain)

                def evacuate_values():
                    for e in range(2):
                        for tt in range(2):
                            last = dve.tensor_tensor(
                                V1[:, 2 * e + tt, :, 0:HD],
                                PS[:, V_BANK[e], tt * DIM:(tt + 1) * DIM].rearrange("p (h e) -> p h e", h=HEADS),
                                w_qkv[:, e, 2 * 768:2 * 768 + DIM].rearrange("p (h e) -> p h e", h=HEADS), ALU.add)
                    last.then_inc(att2["V1"].sem, 1)

                dve_attention(dve, it, att2, float(HD) ** -0.5, evacuate_values)
                halves = lambda ap, e: ap[:, 2 * e:2 * e + 2, :]
                row = lambda w, e, start: w[:, e, start:start + DIM].unsqueeze(1).to_broadcast([P, 2, DIM])

                def scale_shift(w, start):
                    for e in range(2):
                        last = dve.tensor_tensor(halves(xn, e), halves(xn, e), row(w, e, start), ALU.mult)
                    link(dve, dve_chain, last)
                    for e in range(2):
                        last = dve.tensor_tensor(halves(xn, e), halves(xn, e), row(w, e, start + DIM), ALU.add)
                    return last

                dve.wait_ge(*two["y"](it, 1))
                dve.wait_ge(*two["xb"](it, 1))
                link(dve, dve_chain, dve.tensor_tensor(
                    rr[:, :, :], PS[:, 0:2, :].rearrange("p b (t f) -> p (b t) f", t=2), xb[:, :, :], ALU.add))
                dve_stats(dve, rr, two["var"])
                dve.wait_ge(*two["rstd"](it, 1))
                link(dve, dve_chain, dve_normalise(dve, xn, rr))
                scale_shift(w_out, 3 * DIM).then_inc(two["xp"].sem, 1)
                for b in range(1, 8, 2):
                    dve.wait_ge(*two["h"](it, b + 1))
                    for j in range(2):
                        e, blk = b // 4, 2 * (b % 4) + j
                        last = dve.tensor_scalar(hT[:, e, blk, :], PS[:, b, j * SEQ:(j + 1) * SEQ],
                                                 w_up[:, e, KT * DFF + blk:KT * DFF + blk + 1], 0.0, ALU.add, ALU.max)
                    last.then_inc(two["h_dve"].sem, 1)
                dve.wait_ge(*two["y2"](it, 1))
                dve.wait_ge(*two["xpb"](it, 1))
                for e in range(2):
                    last = dve.tensor_tensor(halves(rr, e), PS[:, 4 * e, :].rearrange("p (t f) -> p t f", t=2),
                                             halves(xb, e), ALU.add)
                link(dve, dve_chain, last)
                dve_stats(dve, rr, two["var"])
                dve.wait_ge(*two["rstd"](it, 2))
                link(dve, dve_chain, dve_normalise(dve, xn, rr))
                link(dve, dve_chain, scale_shift(w_down, FB * DIM + DIM))
                flat = lambda ap: ap.rearrange("p t f -> p (t f)")
                link(dve, dve_chain, dve.scalar_tensor_tensor(
                    out=flat(halves(rr, 0)), in0=flat(halves(xn, 0)), scalar=gate_weight[:, bass.ds(it * 2, 1)],
                    in1=flat(x[:, 0:2, :]), op0=ALU.mult, op1=ALU.add))
                dve.scalar_tensor_tensor(
                    out=flat(halves(rr, 0)), in0=flat(halves(xn, 1)), scalar=gate_weight[:, bass.ds(it * 2 + 1, 1)],
                    in1=flat(halves(rr, 0)), op0=ALU.mult, op1=ALU.add).then_inc(two["normed2"].sem, 1)
                dve.wait_ge(*two["normed2"](it, 1))
                dve_stats(dve, rr, two["var"], 2)
                dve.wait_ge(*two["rstd"](it, 3))
                dve.wait_ge(*stored2(it, 0))
                dve_normalise(dve, y, rr, 2).then_inc(two["x3"].sem, 1)

        def pool_phase2(pool):
            with pool.Fori(0, BATCH) as it:
                pool.wait_ge(*in2x(it, 16))
                pool.wait_ge(*loaded2["out"](it, 32))
                for e in range(2):
                    last = pool.tensor_tensor(xb[:, 2 * e:2 * e + 2, :], x[:, 0:2, :],
                                              w_out[:, e, 2 * DIM:3 * DIM].unsqueeze(1).to_broadcast([P, 2, DIM]), ALU.add)
                last.then_inc(two["xb"].sem, 1)
                pool_rstd(pool, it, two["var"], two["rstd"], 1)
                pool.wait_ge(*two["xp"](it, 1))
                pool.wait_ge(*loaded2["down"](it, 32))
                for e in range(2):
                    last = pool.tensor_tensor(xb[:, 2 * e:2 * e + 2, :], xn[:, 2 * e:2 * e + 2, :],
                                              w_down[:, e, FB * DIM:FB * DIM + DIM].unsqueeze(1).to_broadcast([P, 2, DIM]),
                                              ALU.add)
                last.then_inc(two["xpb"].sem, 1)
                pool_rstd(pool, it, two["var"], two["rstd"], 2)
                pool_rstd(pool, it, two["var"], two["rstd"], 3, 2)

        phase2_buffers.close()
        attention_shared.close()
        phase3_buffers = ExitStack()
        ctx.enter_context(phase3_buffers)
        sb3 = lambda name, shape, dt=F32: phase3_buffers.enter_context(nc.sbuf_tensor(name, shape, dt))
        NH, DH = 4, 64
        SLOT_HEADS = (0, 2, 1, 3)
        GROUPS = 4
        c = sb3("c", [P, TILES, DIM])
        head_rows = sb3("head_rows", [2 * NH, NH, P])
        head_rows_r = sb3("head_rows_r", [2 * NH, NH, P], F32R)
        aw = sb3("aw", [P, KT, 3 * DIM])
        mgate = sb3("mgate", [P, 3 * KT, 2 * NH])
        mgate_bias = sb3("mgate_bias", [P, 2 * NH])
        outnorm = sb3("outnorm", [P, DIM])
        gate1 = sb3("gate1", [P, KT, EXPERTS1])
        gate1_bias = sb3("gate1_bias", [P, EXPERTS1])
        av = sb3("av", [P, TILES, DIM])
        aprob = sb3("aprob", [P, TILES, SEQ])
        aprobT = sb3("aprobT", [P, 2, 3 * P])
        neg_max3 = sb3("neg_max3", [P, TILES])
        row_sum = sb3("row_sum", [P, TILES])
        gates = sb3("gates", [P, TILES, 2 * NH])
        abs_f = sb3("abs_f", [P, TILES, NH])
        min_f = sb3("min_f", [P, TILES, NH])
        log_f = sb3("log_f", [P, TILES, NH])
        cum = sb3("cum", [P, TILES, NH])
        source = sb3("source", [P, TILES, NH])
        source_split = sb3("source_split", [P, TILES, 2 * NH], F32R)
        sourceT = sb3("sourceT", [2 * NH, TOK], F32R)
        neg_run = sb3("neg_run", [P, TILES, NH])
        Dm = sb3("Dm", [P, 2, NH, SEQ])
        Cm = sb3("Cm", [P, 2, NH, SEQ])
        CT = sb3("CT", [P, 2, NH, SEQ])
        row_C = sb3("row_C", [P, TILES, NH])
        floor = sb3("floor", [P, TILES, NH])
        hm = sb3("hm", [P, TILES, DIM])
        hsq = sb3("hsq", [P, TILES, DIM])
        hmean = sb3("hmean", [P, TILES * NH])
        hvar = sb3("hvar", [P, TILES * NH])
        score = sb3("score", [P, TILES, EXPERTS1])
        choice = sb3("choice", [P, TILES, EXPERTS1])
        group8 = sb3("group8", [P, TILES, GROUPS, 8])
        group10 = sb3("group10", [P, TILES, 10])
        group_top = sb3("group_top", [P, TILES, 8])
        group_want = sb3("group_want", [P, TILES, 8])
        group_hit = sb3("group_hit", [P, TILES, 10])
        expert_top = sb3("expert_top", [P, TILES, 8])
        route = sb3("route", [P, TILES, ALL_EXPERTS])
        route_sum = sb3("route_sum", [P, TILES])

        W3 = [(head_rows, "head_rows"), (aw, "aw"), (mgate, "mgate"), (mgate_bias, "mgate_bias"), (outnorm, "outnorm"), (gate1, "gate1"),
              (gate1_bias, "gate1_bias")]
        in3 = in1.after(PAIRS, 64)
        three = {n: signal(f"l1_{n}", per) for n, per in (
            ("qkv", 1), ("k", 1), ("v", 1), ("scores", 4), ("max", 4), ("exp", 4), ("turned", 2), ("probT", 2),
            ("out", 1), ("x4", 1), ("x4turned", 1), ("x4T", 1),
            ("gates", 1), ("abs", 1), ("fexp", 1), ("flog", 1), ("logf", 1), ("cum", 1), ("source", 1),
            ("sourceturned", 1), ("sourceT", 1), ("ab", 4), ("run", 4), ("D", 4), ("C", 4), ("Cturned", 4), ("CT", 4),
            ("h", 4), ("hout", 4), ("floor", 1), ("fl", 1), ("hc", 1), ("hsq", 1), ("hvar", 1), ("hrstd", 1),
            ("x5", 1), ("x5turned", 1), ("x5T", 1), ("logits", 1), ("lexp", 1), ("route", 1))}
        three["var"], three["rstd"] = (two[n].after(BATCH, 2) for n in ("var", "rstd"))
        stored3 = stored2.after(BATCH, 48)

        def sp_load3(sp, it):
            sp.dma_start(xT[:, :, :], columns(xsT["x3"], it, TILES)).then_inc(in3.sem, 16)
            sp.dma_start(x[:, :, :], rows(xs["x3"], it, TILES)).then_inc(in3.sem, 16)
            sp.dma_start(cT[:, :, :], columns(d["ctxT"], it, TILES)).then_inc(in3.sem, 16)
            sp.dma_start(c[:, :, :], rows(d["ctx"], it, TILES)).then_inc(in3.sem, 16)

        def sp_store3(sp, it):
            sp.wait_ge(*three["x5"](it, 1))
            sp.dma_start(rows(xs["x5"], it, TILES), y[:, :, :]).then_inc(stored3.sem, 16)
            sp.wait_ge(*three["x5T"](it, 1))
            sp.dma_start(columns(xsT["x5"], it, TILES), yT[:, :, :]).then_inc(stored3.sem, 16)
            sp.wait_ge(*three["route"](it, 1))
            sp.dma_start(rows(route_dram, it, TILES), route[:, :, :]).then_inc(stored3.sem, 16)

        def sp_phase3(sp):
            for dst, name in W3:
                sp.dma_start(dst[tuple(slice(None) for _ in dst.shape)], d[name]).then_inc(weights_loaded.sem, 16)
            sp_load3(sp, 0)
            with sp.Fori(0, PAIRS - 1) as it:
                sp.wait_ge(*three["h"](it, 4))
                sp_load3(sp, it + 1)
                sp_store3(sp, it)
            sp_store3(sp, PAIRS - 1)
            sp.wait_ge(*stored3(PAIRS - 1, 48))

        def width(t):
            return (t % 2 + 1) * P

        def pe_phase3(pe):
            pe.wait_ge(weights_loaded.sem, WEIGHTS1 + 16 * len(W3))
            pe.wait_ge(*consts_ready(0, 2))
            with pe.Fori(0, PAIRS) as it:
                pe.wait_ge(*in3(it, 64))
                for blk in range(4):
                    for ki in range(KT):
                        pe.matmul(PS[:, blk, :], aw[:, ki, blk * P:(blk + 1) * P], xT[:, ki, :],
                                  start=(ki == 0), stop=(ki == 1))
                for t in range(TILES):
                    for ki in range(KT):
                        last = pe.matmul(PS[:, 4 + t // 2, (t % 2) * DIM:(t % 2 + 1) * DIM], xT[:, ki, tokens(t)],
                                         aw[:, ki, 2 * DIM:3 * DIM], start=(ki == 0), stop=(ki == 1))
                last.then_inc(three["qkv"].sem, 1)
                pe.wait_ge(*three["k"](it, 1))
                for t in range(TILES):
                    s, w = t // 2, width(t)
                    pe.matmul(PS[:, t, 0:w], identity16[:, :], causal_mask[:, t % 2, 0:w], start=True, stop=False)
                    for ki in range(KT):
                        last = pe.matmul(PS[:, t, 0:w], qT[:, ki, tokens(t)], kT[:, ki, s * SEQ:s * SEQ + w],
                                         start=False, stop=(ki == 1))
                    last.then_inc(three["scores"].sem, 1)
                pe.wait_ge(*three["v"](it, 1))
                for s in range(2):
                    pe.wait_ge(*three["exp"](it, 2 * s + 2))
                    for slot, (qt, kt) in enumerate(((0, 0), (1, 0), (1, 1))):
                        last = pe.transpose(PS[:, 4 + s, slot * P:(slot + 1) * P],
                                            aprob[:, 2 * s + qt, kt * P:(kt + 1) * P], identity[:, :])
                    last.then_inc(three["turned"].sem, 1)
                for s in range(2):
                    pe.wait_ge(*three["probT"](it, s + 1))
                    for slot, (qt, kt) in enumerate(((0, 0), (1, 0), (1, 1))):
                        last = pe.matmul(PS[:, 6 + s, qt * DIM:(qt + 1) * DIM], aprobT[:, s, slot * P:(slot + 1) * P],
                                         av[:, 2 * s + kt, :], start=(kt == 0), stop=(kt == qt))
                last.then_inc(three["out"].sem, 1)
                def gates(first, blocks):
                    for t in range(TILES):
                        for blk in blocks:
                            lhs = (xnT if blk < KT else cT)[:, blk % KT, tokens(t)]
                            last = pe.matmul(PS[:, 2, first + t * 2 * NH:first + (t + 1) * 2 * NH], lhs, mgate[:, blk, :],
                                             start=(blk == blocks[0]), stop=(blk == blocks[-1]))
                    return last

                gates(TILES * 2 * NH, range(KT, 3 * KT))
                pe.wait_ge(*three["x4"](it, 1))
                pe_turn(pe, xn, 0).then_inc(three["x4turned"].sem, 1)
                pe.wait_ge(*three["x4T"](it, 1))
                gates(0, range(KT)).then_inc(three["gates"].sem, 1)
                pe.wait_ge(*three["logf"](it, 1))
                for s in range(2):
                    pe.matmul(PS[:, 3, 2 * s * NH:(2 * s + 1) * NH], upto[:, :], log_f[:, 2 * s, :],
                              start=True, stop=True)
                    pe.matmul(PS[:, 3, (2 * s + 1) * NH:(2 * s + 2) * NH], ones[:, :], log_f[:, 2 * s, :],
                              start=True, stop=False)
                    last = pe.matmul(PS[:, 3, (2 * s + 1) * NH:(2 * s + 2) * NH], upto[:, :], log_f[:, 2 * s + 1, :],
                                     start=False, stop=True)
                last.then_inc(three["cum"].sem, 1)
                pe.wait_ge(*three["source"](it, 1))
                for t in range(TILES):
                    last = pe.transpose(PS[0:2 * NH, 4, tokens(t)], source_split[:, t, :].bitcast(F32), identity[:, :])
                last.then_inc(three["sourceturned"].sem, 1)
                pe.wait_ge(*three["sourceT"](it, 1))
                def mix_scores(t):
                    s, w, base = t // 2, width(t), 4 * (t % 2)
                    if t >= 2:
                        pe.wait_ge(*three["hout"](it, t - 1))
                    for slot, h in enumerate(SLOT_HEADS):
                        bank, col = base + slot // 2, (slot % 2) * SEQ
                        pe.matmul(PS[:, bank, col:col + w], identity16[:, :], causal_mask[:, t % 2, 0:w],
                                  start=True, stop=False)
                        pe.matmul(PS[:, bank, col:col + w], head_rows_r[:, h, :], sourceT[:, s * SEQ:s * SEQ + w],
                                  start=False, stop=True)
                    for slot, h in enumerate(SLOT_HEADS):
                        bank, col, r = base + 2 + slot // 2, (slot % 2) * SEQ, DH * (h % 2)
                        last = pe.matmul(PS[:, bank, col:col + w], xnT[r:r + DH, h // 2, tokens(t)],
                                         cT[r:r + DH, h // 2, s * SEQ:s * SEQ + w], start=True, stop=True)
                    last.then_inc(three["ab"].sem, 1)

                def mix_values(t):
                    s, base = t // 2, 4 * (t % 2)
                    pe.wait_ge(*three["C"](it, t + 1))
                    for slot in range(NH):
                        for kt in range(t % 2 + 1):
                            col = (slot % 2) * SEQ + kt * P
                            last = pe.transpose(PS[:, base + slot // 2, col:col + P],
                                                Cm[:, t % 2, slot, kt * P:(kt + 1) * P], identity[:, :])
                    last.then_inc(three["Cturned"].sem, 1)
                    pe.wait_ge(*three["CT"](it, t + 1))
                    for slot, h in enumerate(SLOT_HEADS):
                        for kt in range(t % 2 + 1):
                            last = pe.matmul(PS[:, base + 2, h * DH:(h + 1) * DH], CT[:, t % 2, slot, kt * P:(kt + 1) * P],
                                             c[:, 2 * s + kt, h * DH:(h + 1) * DH], start=(kt == 0), stop=(kt == t % 2))
                    last.then_inc(three["h"].sem, 1)

                mix_scores(0)
                for t in range(TILES):
                    if t + 1 < TILES:
                        mix_scores(t + 1)
                    mix_values(t)
                pe.wait_ge(*three["x5"](it, 1))
                pe_turn(pe, y, 0).then_inc(three["x5turned"].sem, 1)
                pe.wait_ge(*three["x5T"](it, 1))
                for t in range(TILES):
                    for ki in range(KT):
                        last = pe.matmul(PS[:, 4, t * EXPERTS1:(t + 1) * EXPERTS1], yT[:, ki, tokens(t)],
                                         gate1[:, ki, :], start=(ki == 0), stop=(ki == 1))
                last.then_inc(three["logits"].sem, 1)
                pe.wait_ge(*three["lexp"](it, 1))

        def act_phase3(act):
            with act.Fori(0, PAIRS) as it:
                act.wait_ge(*three["qkv"](it, 1))
                act.activation(qT[:, :, :], PS[:, 0:2, :], ACT.Copy, scale=float(DIM) ** -0.5)
                act.activation(kT[:, :, :], PS[:, 2:4, :], ACT.Copy).then_inc(three["k"].sem, 1)
                for t in range(TILES):
                    act.wait_ge(*three["max"](it, t + 1))
                    act.activation(aprob[:, t, 0:width(t)], PS[:, t, 0:width(t)], ACT.Exp, bias=neg_max3[:, t:t + 1],
                                   accum_out=row_sum[:, t:t + 1]).then_inc(three["exp"].sem, 1)
                for s in range(2):
                    act.wait_ge(*three["turned"](it, s + 1))
                    act.activation(aprobT[:, s, :], PS[:, 4 + s, 0:3 * P], ACT.Copy).then_inc(three["probT"].sem, 1)
                act.wait_ge(*three["x4turned"](it, 1))
                act_turned(act, xnT, 0).then_inc(three["x4T"].sem, 1)
                act.wait_ge(*three["abs"](it, 1))
                act.activation(abs_f[:, :, :], abs_f[:, :, :], ACT.Exp, scale=-1.0).then_inc(three["fexp"].sem, 1)
                act.wait_ge(*three["fexp"](it, 1))
                act.activation(abs_f[:, :, :], abs_f[:, :, :], ACT.Ln, bias=1.0).then_inc(three["flog"].sem, 1)
                act.wait_ge(*three["sourceturned"](it, 1))
                act.activation(sourceT[:, :], PS[0:2 * NH, 4, :], ACT.Copy).then_inc(three["sourceT"].sem, 1)

                def mix_exp(t):
                    act.wait_ge(*three["run"](it, t + 1))
                    if t >= 2:
                        act.wait_ge(*three["C"](it, t - 1))
                    for slot, h in enumerate(SLOT_HEADS):
                        src = PS[:, 4 * (t % 2) + slot // 2, (slot % 2) * SEQ:(slot % 2) * SEQ + width(t)]
                        last = act.activation(Dm[:, t % 2, slot, 0:width(t)], src, ACT.Exp, bias=neg_run[:, t, h:h + 1])
                    last.then_inc(three["D"].sem, 1)

                mix_exp(0)
                for t in range(TILES):
                    if t + 1 < TILES:
                        mix_exp(t + 1)
                    act.wait_ge(*three["Cturned"](it, t + 1))
                    base = 4 * (t % 2)
                    act.activation(CT[:, t % 2, :, 0:width(t)],
                                   PS[:, base:base + 2, :].rearrange("p b (h k) -> p (b h) k", h=2)[:, :, 0:width(t)],
                                   ACT.Copy).then_inc(three["CT"].sem, 1)
                act.wait_ge(*three["floor"](it, 1))
                act.activation(floor[:, :, :], floor[:, :, :], ACT.Exp).then_inc(three["fl"].sem, 1)
                act.wait_ge(*three["hc"](it, 1))
                act.activation(hsq[:, :, :], hm[:, :, :], ACT.Square).then_inc(three["hsq"].sem, 1)
                act.wait_ge(*three["x5turned"](it, 1))
                act.wait_ge(*stored3(it, 0))
                act_turned(act, yT, 0).then_inc(three["x5T"].sem, 1)
                act.wait_ge(*three["logits"](it, 1))
                act.activation(score[:, :, :], PS[:, 4, 0:TILES * EXPERTS1].rearrange("p (t e) -> p t e", t=TILES),
                               ACT.Exp, scale=-1.0).then_inc(three["lexp"].sem, 1)

        def dve_phase3(dve):
            dve.wait_ge(weights_loaded.sem, WEIGHTS1 + 16 * len(W3))
            restart(dve, dve_chain)
            dve.tensor_copy(head_rows_r[:, :, :], head_rows[:, :, :]).then_inc(consts_ready.sem, 1)
            dve.memset(group10[:, :, :], FAR)
            dve.memset(group_want[:, :, :], FAR)
            link(dve, dve_chain, dve.memset(route[:, :, EXPERTS1:ALL_EXPERTS], 1.0))
            with dve.Fori(0, PAIRS) as it:
                restart(dve, dve_chain)

                def chained(ins):
                    link(dve, dve_chain, ins)

                dve.wait_ge(*three["qkv"](it, 1))
                dve.tensor_copy(av[:, :, :], PS[:, 4:6, :].rearrange("p b (t f) -> p (b t) f", t=2))\
                    .then_inc(three["v"].sem, 1)
                for t in range(TILES):
                    dve.wait_ge(*three["scores"](it, t + 1))
                    dve.tensor_reduce(neg_max3[:, t:t + 1], PS[:, t, 0:width(t)], AX.X, ALU.max, negate=True)\
                        .then_inc(three["max"].sem, 1)
                dve.wait_ge(*three["exp"](it, 4))
                chained(dve.reciprocal(row_sum[:, :], row_sum[:, :]))
                dve.wait_ge(*three["out"](it, 1))
                for t in range(TILES):
                    last = dve.scalar_tensor_tensor(out=rr[:, t, :], in0=PS[:, 6 + t // 2, (t % 2) * DIM:(t % 2 + 1) * DIM],
                                                    scalar=row_sum[:, t:t + 1], in1=x[:, t, :],
                                                    op0=ALU.mult, op1=ALU.add)
                chained(last)
                dve_stats(dve, rr, three["var"])
                dve.wait_ge(*three["rstd"](it, 1))
                dve_normalise(dve, xn, rr).then_inc(three["x4"].sem, 1)
                dve.wait_ge(*three["gates"](it, 1))
                chained(dve.tensor_tensor(gates[:, :, :], PS[:, 2, 0:TILES * 2 * NH].rearrange("p (t g) -> p t g", t=TILES),
                                          mgate_bias[:, :].unsqueeze(1).to_broadcast([P, TILES, 2 * NH]), ALU.add))
                chained(dve.tensor_tensor(gates[:, :, :], PS[:, 2, TILES * 2 * NH:2 * TILES * 2 * NH]
                                          .rearrange("p (t g) -> p t g", t=TILES), gates[:, :, :], ALU.add))
                forget = gates[:, :, NH:2 * NH]
                dve.scalar_tensor_tensor(out=abs_f[:, :, :], in0=forget, scalar=-1.0, in1=forget,
                                         op0=ALU.mult, op1=ALU.max).then_inc(three["abs"].sem, 1)
                chained(dve.tensor_scalar(min_f[:, :, :], forget, 0.0, None, ALU.min))
                dve.wait_ge(*three["flog"](it, 1))
                dve.tensor_tensor(log_f[:, :, :], min_f[:, :, :], abs_f[:, :, :], ALU.subtract)\
                    .then_inc(three["logf"].sem, 1)
                dve.wait_ge(*three["cum"](it, 1))
                chained(dve.tensor_copy(cum[:, :, :], PS[:, 3, 0:TILES * NH].rearrange("p (t g) -> p t g", t=TILES)))
                chained(dve.tensor_tensor(source[:, :, :], gates[:, :, 0:NH], cum[:, :, :], ALU.subtract))
                chained(dve.tensor_copy(source_split[:, :, 0:NH], source[:, :, :]))
                dve.tensor_tensor(source_split[:, :, NH:], source[:, :, :], source_split[:, :, 0:NH].bitcast(F32),
                                  ALU.subtract).then_inc(three["source"].sem, 1)

                by_slot = lambda ap: ap.rearrange("p (b h) -> p h b", h=2)

                def mix_max(t):
                    dve.wait_ge(*three["ab"](it, t + 1))
                    base = 4 * (t % 2)
                    src = PS[:, base:base + 2, :].rearrange("p b (h k) -> p b h k", h=2)[:, :, :, 0:width(t)]
                    dve.tensor_reduce(by_slot(neg_run[:, t, :]), src, AX.X, ALU.max, negate=True).then_inc(three["run"].sem, 1)

                def mix_c(t):
                    dve.wait_ge(*three["D"](it, t + 1))
                    if t >= 2:
                        dve.wait_ge(*three["Cturned"](it, t - 1))
                    base = 4 * (t % 2) + 2
                    src = PS[:, base:base + 2, :].rearrange("p b (h k) -> p (b h) k", h=2)[:, :, 0:width(t)]
                    dst = Cm[:, t % 2, :, 0:width(t)]
                    dve.scalar_tensor_tensor(out=dst, in0=src, scalar=float(DH) ** -0.5, in1=Dm[:, t % 2, :, 0:width(t)],
                                             op0=ALU.mult, op1=ALU.mult).then_inc(three["C"].sem, 1)
                    dve.wait_ge(*three["C"](it, t + 1))
                    chained(dve.tensor_reduce(by_slot(row_C[:, t, :]), dst.rearrange("p (b h) k -> p b h k", b=2),
                                              AX.X, ALU.add))

                mix_max(0)
                mix_c(0)
                for t in range(TILES):
                    if t + 1 < TILES:
                        mix_max(t + 1)
                        mix_c(t + 1)
                    dve.wait_ge(*three["h"](it, t + 1))
                    dve.tensor_copy(hm[:, t, :], PS[:, 4 * (t % 2) + 2, 0:DIM]).then_inc(three["hout"].sem, 1)
                flat = lambda ap: ap.rearrange("p t h -> p (t h)")
                dve.tensor_tensor(floor[:, :, :], neg_run[:, :, :], cum[:, :, :], ALU.subtract)\
                    .then_inc(three["floor"].sem, 1)
                chained(dve.scalar_tensor_tensor(out=flat(row_C[:, :, :]), in0=flat(row_C[:, :, :]), scalar=-1.0,
                                                 in1=flat(row_C[:, :, :]), op0=ALU.mult, op1=ALU.max))
                dve.wait_ge(*three["fl"](it, 1))
                chained(dve.tensor_tensor(row_C[:, :, :], row_C[:, :, :], floor[:, :, :], ALU.max))
                chained(dve.tensor_scalar(row_C[:, :, :], row_C[:, :, :], 1e-6, None, ALU.add))
                chained(dve.reciprocal(row_C[:, :, :], row_C[:, :, :]))
                per_head = hm[:, :, :].rearrange("p t (h e) -> p (t h) e", h=NH)
                spread = lambda ap: ap.unsqueeze(2).to_broadcast([P, TILES * NH, DH])
                dve.wait_ge(*three["hout"](it, 4))
                chained(dve.tensor_tensor(per_head, per_head, spread(flat(row_C[:, :, :])), ALU.mult))
                chained(dve.tensor_reduce(hmean[:, :], per_head, AX.X, ALU.add))
                chained(dve.tensor_scalar(hmean[:, :], hmean[:, :], 1.0 / DH, None, ALU.mult))
                dve.tensor_tensor(per_head, per_head, spread(hmean[:, :]), ALU.subtract).then_inc(three["hc"].sem, 1)
                dve.wait_ge(*three["hsq"](it, 1))
                chained(dve.tensor_reduce(hvar[:, :], hsq[:, :, :].rearrange("p t (h e) -> p (t h) e", h=NH), AX.X, ALU.add))
                dve.tensor_scalar(hvar[:, :], hvar[:, :], 1.0 / DH, 1e-5, ALU.mult, ALU.add).then_inc(three["hvar"].sem, 1)
                dve.wait_ge(*three["hrstd"](it, 1))
                chained(dve.tensor_tensor(per_head, per_head, spread(hvar[:, :]), ALU.mult))
                chained(dve.tensor_tensor(hm[:, :, :], hm[:, :, :],
                                          outnorm[:, :].unsqueeze(1).to_broadcast([P, TILES, DIM]), ALU.mult))
                chained(dve.tensor_tensor(rr[:, :, :], hm[:, :, :], xn[:, :, :], ALU.add))
                dve_stats(dve, rr, three["var"])
                dve.wait_ge(*three["rstd"](it, 2))
                dve.wait_ge(*stored3(it, 0))
                dve_normalise(dve, y, rr).then_inc(three["x5"].sem, 1)
                dve.wait_ge(*three["lexp"](it, 1))
                chained(dve.tensor_scalar(score[:, :, :], score[:, :, :], 1.0, None, ALU.add))
                chained(dve.reciprocal(score[:, :, :], score[:, :, :]))
                chained(dve.tensor_tensor(choice[:, :, :], score[:, :, :],
                                          gate1_bias[:, :].unsqueeze(1).to_broadcast([P, TILES, EXPERTS1]), ALU.add))
                for t in range(TILES):
                    for g in range(GROUPS):
                        last = dve.max(group8[:, t, g, :], choice[:, t, 8 * g:8 * g + 8])
                chained(last)
                chained(dve.tensor_tensor(group10[:, :, 0:GROUPS], group8[:, :, :, 0], group8[:, :, :, 1], ALU.add))
                for t in range(TILES):
                    last = dve.max(group_top[:, t, :], group10[:, t, :])
                chained(last)
                chained(dve.tensor_copy(group_want[:, :, 0:2], group_top[:, :, 0:2]))
                for t in range(TILES):
                    last = dve.match_replace(group_hit[:, t, :], group_want[:, t, :], group10[:, t, :], -FAR)
                chained(last)
                chained(dve.tensor_scalar(group_hit[:, :, :], group_hit[:, :, :], 1e38, None, ALU.is_ge))
                by_group = lambda ap: ap.rearrange("p t (g e) -> p t g e", g=GROUPS)
                chained(dve.tensor_tensor(by_group(choice[:, :, :]), by_group(choice[:, :, :]),
                                          group_hit[:, :, 0:GROUPS].unsqueeze(3).to_broadcast([P, TILES, GROUPS, 8]),
                                          ALU.mult))
                chained(dve.tensor_scalar(choice[:, :, :], choice[:, :, :], 0.0, None, ALU.add))
                for t in range(TILES):
                    last = dve.max(expert_top[:, t, :], choice[:, t, :])
                chained(last)
                for t in range(TILES):
                    last = dve.match_replace(choice[:, t, :], expert_top[:, t, :], choice[:, t, :], -FAR)
                chained(last)
                chained(dve.tensor_scalar(choice[:, :, :], choice[:, :, :], 1e38, None, ALU.is_ge))
                chained(dve.tensor_tensor(score[:, :, :], score[:, :, :], choice[:, :, :], ALU.mult))
                chained(dve.tensor_reduce(route_sum[:, :], score[:, :, :], AX.X, ALU.add))
                chained(dve.tensor_scalar(route_sum[:, :], route_sum[:, :], 1e-20, None, ALU.add))
                chained(dve.reciprocal(route_sum[:, :], route_sum[:, :]))
                chained(dve.tensor_scalar(route_sum[:, :], route_sum[:, :], 2.5, None, ALU.mult))
                dve.tensor_tensor(route[:, :, 0:EXPERTS1], score[:, :, :],
                                  route_sum[:, :].unsqueeze(2).to_broadcast([P, TILES, EXPERTS1]), ALU.mult)\
                    .then_inc(three["route"].sem, 1)
                dve.wait_ge(*three["route"](it, 1))

        def pool_phase3(pool):
            with pool.Fori(0, PAIRS) as it:
                pool_rstd(pool, it, three["var"], three["rstd"], 1)
                pool.wait_ge(*three["hvar"](it, 1))
                pool.tensor_tensor(hvar[:, :], hvar[:, :], minus_half[:, 0:TILES * NH], ALU.pow)\
                    .then_inc(three["hrstd"].sem, 1)
                pool_rstd(pool, it, three["var"], three["rstd"], 2)

        phase3_buffers.close()
        sb4 = lambda name, shape, dt=F32: ctx.enter_context(nc.sbuf_tensor(name, shape, dt))
        NT = BATCH * SEQ // P
        NG = NT // TILES
        W_EXPERT = 2 * KT * INNER + DIM
        SLOTS = 4
        x_high, x_low = (sb4(n, [P, KT, NT * P], F32R) for n in ("x_high", "x_low"))
        acc = sb4("acc", [P, NT, DIM])
        route4 = sb4("route4", [P, NT, ALL_EXPERTS])
        w_expert = sb4("w_expert", [P, 2, W_EXPERT])
        w_high, w_low = (sb4(n, [P, 2, W_EXPERT], F32R) for n in ("w_high", "w_low"))
        silu_g = sb4("silu_g", [P, 2, TOK])
        hidden_t = sb4("hidden_t", [P, 2, TOK])
        h_high, h_low = (sb4(n, [P, SLOTS, TOK], F32R) for n in ("h_high", "h_low"))

        in4 = in3.after(PAIRS, 16)
        group_loaded = [signal(f"group_loaded{j}", 32) for j in range(2)]
        expert_loaded = [signal(f"expert_loaded{j}", 16) for j in range(2)]
        x_split = {n: signal(f"x_{n}", 1) for n in ("high", "low")}
        w_split = {n: signal(f"w_{n}", 2) for n in ("high", "low")}
        STEPS = 2 * NG
        ITERATIONS = ALL_EXPERTS // 2
        BEHIND = 2
        four = {n: signal(f"e_{n}", STEPS, base) for n, base in
                (("gu", 0), ("silu", 0), ("hidden", 2), ("high", 0), ("low", 0), ("down", 0), ("added", 2))}
        four_ln = {n: three[n].after(PAIRS, 1) for n in ("var", "rstd")}
        four_ln["out"] = signal("z_out", 1)
        stored4 = stored3.after(PAIRS, 16)
        group_slot = (xT, cT)

        def expert_loop(eng, body):
            body(0, True, False)
            with eng.Fori(1, ITERATIONS - 1) as it:
                body(it, False, False)
            body(ITERATIONS - 1, False, True)

        def sp_phase4(sp):
            sp.wait_ge(*three["route"](PAIRS - 1, 1))
            load = lambda e, j: sp.dma_start(
                w_expert[:, j, :], d["experts"][bass.ds(e, 1), :, :].rearrange("a p n -> p (a n)"))\
                .then_inc(expert_loaded[j].sem, 16)
            load(0, 0)
            for g in range(NG):
                if g >= 2:
                    sp.wait_ge(*x_split["low"](0, g - 1))
                sp.dma_start(group_slot[g % 2][:, :, :], columns(xsT["x5"], g, TILES))\
                    .then_inc(group_loaded[g % 2].sem, 16)
                sp.dma_start(acc[:, g * TILES:(g + 1) * TILES, :], rows(xs["x5"], g, TILES))\
                    .then_inc(group_loaded[g % 2].sem, 16)
                if g == 0:
                    sp.dma_start(route4[:, :, :], route_dram.rearrange("(t p) e -> p t e", p=P)).then_inc(in4.sem, 16)
                    load(1, 1)
            with sp.Fori(0, ITERATIONS - 1) as it:
                for j in range(2):
                    sp.wait_ge(*w_split["high"](it, j + 1))
                    sp.wait_ge(*w_split["low"](it, j + 1))
                    load((it + 1) * 2 + j, j)
            with sp.Fori(0, NG) as g:
                sp.wait_ge(*four_ln["out"](g, 1))
                sp.dma_start(rows(out, g, TILES), y[:, :, :]).then_inc(stored4.sem, 16)
            sp.wait_ge(*stored4(NG - 1, 16))

        def pe_phase4(pe):
            def body(it, first, final):
                def up(n):
                    j, g = n // NG, n % NG
                    if first and n < NG:
                        pe.wait_ge(*x_split["low"](0, n + 1))
                    if g == 0:
                        pe.wait_ge(*w_split["high"](it, j + 1))
                        pe.wait_ge(*w_split["low"](it, j + 1))
                    pe.wait_ge(*four["hidden"](it, n - 1))
                    for m in range(2):
                        for ki in range(KT):
                            col = (ki * 2 + m) * INNER
                            for k, (w, x_half) in enumerate(((w_high, x_high), (w_high, x_low), (w_low, x_high))):
                                last = pe.matmul(PS[:, 2 * (n % 2) + m, :], w[:, j, col:col + INNER],
                                                 x_half[:, ki, g * TOK:(g + 1) * TOK],
                                                 start=(ki == 0 and k == 0), stop=(ki == 1 and k == 2))
                    last.then_inc(four["gu"].sem, 1)

                def down(n):
                    j = n % STEPS // NG
                    pe.wait_ge(*four["low"](it, n + 1))
                    pe.wait_ge(*four["added"](it, n - 1))
                    for t in range(TILES):
                        for k, (h_half, w) in enumerate(((h_high, w_high), (h_high, w_low), (h_low, w_high))):
                            last = pe.matmul(PS[:, 4 + 2 * (n % 2) + t // 2, (t % 2) * DIM:(t % 2 + 1) * DIM],
                                             h_half[:, n % SLOTS, tokens(t)], w[:, j, 2 * KT * INNER:],
                                             start=(k == 0), stop=(k == 2))
                    last.then_inc(four["down"].sem, 1)

                for n in range(STEPS):
                    up(n)
                    if n >= BEHIND or not first:
                        down(n - BEHIND)
                if final:
                    for n in range(STEPS - BEHIND, STEPS):
                        down(n)

            expert_loop(pe, body)

        def split_expert_at(n):
            return {3: (0, 1), NG + 3: (1, 0)}.get(n)

        def act_phase4(act):
            def group_high(g):
                act.wait_ge(*group_loaded[g % 2](g // 2, 32))
                act.activation(x_high[:, :, g * TOK:(g + 1) * TOK], group_slot[g % 2][:, :, :], ACT.Copy)\
                    .then_inc(x_split["high"].sem, 1)

            def expert_high(it, j):
                act.wait_ge(*expert_loaded[j](it, 16))
                act.activation(w_high[:, j, :], w_expert[:, j, :], ACT.Copy).then_inc(w_split["high"].sem, 1)

            def body(it, first, final):
                for n in range(STEPS):
                    if first and n + 2 < NG:
                        group_high(n + 2)
                    act.wait_ge(*four["gu"](it, n + 1))
                    act.wait_ge(*four["hidden"](it, n - 1))
                    act.activation(silu_g[:, n % 2, :], PS[:, 2 * (n % 2), :], ACT.Silu).then_inc(four["silu"].sem, 1)
                    act.wait_ge(*four["hidden"](it, n + 1))
                    act.activation(h_high[:, n % SLOTS, :], hidden_t[:, n % 2, :], ACT.Copy).then_inc(four["high"].sem, 1)
                    want = split_expert_at(n)
                    if want and not (final and want[0]):
                        act.wait_ge(*four["down"](it, NG * want[0] + 1 - want[0]))
                        expert_high(it + want[0], want[1])

            expert_high(0, 0)
            group_high(0)
            group_high(1)
            expert_loop(act, body)

        def dve_phase4(dve):
            def group_low(g):
                dve.wait_ge(*x_split["high"](0, g + 1))
                dve.tensor_tensor(x_low[:, :, g * TOK:(g + 1) * TOK], group_slot[g % 2][:, :, :],
                                  x_high[:, :, g * TOK:(g + 1) * TOK].bitcast(F32), ALU.subtract)\
                    .then_inc(x_split["low"].sem, 1)

            def body(it, first, final):
                def hidden(n):
                    dve.wait_ge(*four["silu"](it, n + 1))
                    if n >= SLOTS or not first:
                        dve.wait_ge(*four["down"](it, n - SLOTS + 1))
                    if n >= 2 or not first:
                        dve.wait_ge(*four["low"](it, n - 1))
                    dve.tensor_tensor(hidden_t[:, n % 2, :], silu_g[:, n % 2, :], PS[:, 2 * (n % 2) + 1, :], ALU.mult)\
                        .then_inc(four["hidden"].sem, 1)

                def add(n):
                    j, g = n % STEPS // NG, n % NG
                    column = it * 2 + j - (2 if n < 0 else 0)
                    dve.wait_ge(*four["down"](it, n + 1))
                    for t in range(TILES):
                        tile = TILES * g + t
                        last = dve.scalar_tensor_tensor(
                            out=acc[:, tile, :], in0=PS[:, 4 + 2 * (n % 2) + t // 2, (t % 2) * DIM:(t % 2 + 1) * DIM],
                            scalar=route4[:, tile, bass.ds(column, 1)], in1=acc[:, tile, :],
                            op0=ALU.mult, op1=ALU.add)
                    last.then_inc(four["added"].sem, 1)

                for n in range(STEPS):
                    if first and n + 2 < NG:
                        group_low(n + 2)
                    hidden(n)
                    if n >= BEHIND or not first:
                        add(n - BEHIND)
                if final:
                    for n in range(STEPS - BEHIND, STEPS):
                        add(n)

            group_low(0)
            group_low(1)
            dve.wait_ge(*in4(0, 16))
            dve.sem_inc(four["hidden"].sem, 2)
            dve.sem_inc(four["added"].sem, 2)
            expert_loop(dve, body)
            dve.wait_ge(*four["added"](ITERATIONS - 1, STEPS))
            with dve.Fori(0, NG) as g:
                restart(dve, dve_chain)
                link(dve, dve_chain, dve.tensor_copy(rr[:, :, :], acc[:, bass.ds(g * TILES, TILES), :]))
                dve_stats(dve, rr, four_ln["var"])
                dve.wait_ge(*four_ln["rstd"](g, 1))
                dve.wait_ge(*stored4(g, 0))
                dve_normalise(dve, y, rr).then_inc(four_ln["out"].sem, 1)
                dve.wait_ge(*four_ln["out"](g, 1))

        def pool_phase4(pool):
            def expert_low(it, j):
                pool.wait_ge(*w_split["high"](it, j + 1))
                pool.tensor_tensor(w_low[:, j, :], w_expert[:, j, :], w_high[:, j, :].bitcast(F32), ALU.subtract)\
                    .then_inc(w_split["low"].sem, 1)

            def body(it, first, final):
                for n in range(STEPS):
                    pool.wait_ge(*four["high"](it, n + 1))
                    pool.tensor_tensor(h_low[:, n % SLOTS, :], hidden_t[:, n % 2, :], h_high[:, n % SLOTS, :].bitcast(F32),
                                       ALU.subtract).then_inc(four["low"].sem, 1)
                    want = split_expert_at(n)
                    if want and not (final and want[0]):
                        expert_low(it + want[0], want[1])

            expert_low(0, 0)
            expert_loop(pool, body)
            with pool.Fori(0, NG) as g:
                pool_rstd(pool, g, four_ln["var"], four_ln["rstd"])

        block = ctx.enter_context(nc.Block())

        @block.sync
        def _(sp):
            sp_phase1(sp)
            sp_phase2(sp)
            sp_phase3(sp)
            sp_phase4(sp)

        @block.tensor
        def _(pe):
            pe_phase1(pe)
            pe_phase2(pe)
            pe_phase3(pe)
            pe_phase4(pe)

        @block.scalar
        def _(act):
            act_phase1(act)
            act_phase2(act)
            act_phase3(act)
            act_phase4(act)

        @block.vector
        def _(dve):
            dve_phase1(dve)
            dve_phase2(dve)
            dve_phase3(dve)
            dve_phase4(dve)

        @block.gpsimd
        def _(pool):
            pool_phase1(pool)
            pool_phase2(pool)
            pool_phase3(pool)
            pool_phase4(pool)


def more_layout(f, h, np):
    E = "L0_ffn_"
    g = lambda n: f[E + n]
    qkv, outp, up, down = [], [], [], []
    for e in range(EXPERTS0):
        b = g("in_proj_b")[e]
        qkv.append(np.concatenate([_rows(g("in_proj_w")[e].T).reshape(128, -1), _spread(b[512:768]),
                                   _column(b[0:512])], 1))
        outp.append(np.concatenate([_rows(g("out_proj_w")[e].T).reshape(128, -1), _spread(g("out_proj_b")[e]),
                                    _spread(g("ln1_w")[e]), _spread(g("ln1_b")[e])], 1))
        up.append(np.concatenate([_rows(g("lin1_w")[e].T).reshape(128, -1), _column(g("lin1_b")[e])], 1))
        down.append(np.concatenate([_rows(g("lin2_w")[e].T).reshape(128, -1), _spread(g("lin2_b")[e]),
                                    _spread(g("ln2_w")[e]), _spread(g("ln2_b")[e])], 1))
    for n, v in (("f_qkv", qkv), ("f_out", outp), ("f_up", up), ("f_down", down)):
        h[n] = np.stack(v)
    h["aw"] = _rows(f["L1_attn_W_qkv"])
    M = "L1_xattn_"
    h["mgate"] = _rows(np.concatenate([f[M + "igate_kernel"], f[M + "fgate_kernel"]], 1))
    h["mgate_bias"] = _spread(np.concatenate([f[M + "igate_bias"], f[M + "fgate_bias"]]))
    h["outnorm"] = _spread(f[M + "outnorm_scale"])
    h["gate1"] = _rows(f["L1_ffn_gate_w"].T)
    h["gate1_bias"] = _spread(f["L1_ffn_gate_bias"])
    F = "L1_ffn_"
    gate = np.concatenate([f[F + "expert_gate"], f[F + "shared_gate"].reshape(2, INNER, DIM)])
    up1 = np.concatenate([f[F + "expert_up"], f[F + "shared_up"].reshape(2, INNER, DIM)])
    down1 = np.concatenate([f[F + "expert_down"], f[F + "shared_down"].reshape(DIM, 2, INNER).transpose(1, 0, 2)])
    both = np.concatenate([gate.transpose(0, 2, 1).reshape(-1, KT, 128, INNER),
                           up1.transpose(0, 2, 1).reshape(-1, KT, 128, INNER)], 3)
    both = both.transpose(0, 2, 1, 3).reshape(-1, 128, KT * 2 * INNER)
    h["experts"] = np.concatenate([both, down1.transpose(0, 2, 1)], 2)


def _rows(w, rows=128):
    import numpy as np
    return np.ascontiguousarray(w.reshape(w.shape[0] // rows, rows, w.shape[1]).transpose(1, 0, 2))


def _spread(v):
    import numpy as np
    return np.ascontiguousarray(np.broadcast_to(np.asarray(v).reshape(1, -1), (128, np.asarray(v).size)))


def _column(v):
    import numpy as np
    return np.ascontiguousarray(np.asarray(v).reshape(-1, 128).T)


def layout(a):
    import numpy as np
    f = {k: np.asarray(v) for k, v in a.items()}
    P = 128
    h = {}
    h["x"] = f["x"].reshape(-1, DIM)
    h["xT"] = np.ascontiguousarray(h["x"].T)
    h["ctx"] = f["ctx_1024"].reshape(-1, DIM)
    h["ctxT"] = np.ascontiguousarray(h["ctx"].T)
    L = "L0_attn_"
    h["wqk"] = _rows(np.concatenate([f[L + "Wq"], f[L + "Wk"]], 1))
    h["wvg"] = _rows(np.concatenate([f[L + "Wv"], f[L + "Wb"], f[L + "Wfd"], f[L + "Wsd"]], 1))
    h["decay_bias"] = _spread(np.concatenate([np.zeros(16, np.float32), f[L + "bfd"], f[L + "bsd"]]))
    h["wo"] = _rows(f[L + "Wo"])
    w1 = np.zeros((P, KT, P), np.float32)
    w2 = np.zeros((P, HEADS), np.float32)
    for n in range(HEADS):
        w1[16 * (n % 8):16 * (n % 8) + 16, n // 8, 8 * n:8 * n + 8] = f[L + "Wtf1"]
        w2[8 * n:8 * n + 8, n:n + 1] = f[L + "Wtf2"]
    h["wtf1"], h["wtf2"] = w1, w2
    h["btf1"] = np.ascontiguousarray(np.tile(f[L + "btf1"], HEADS).reshape(P, 1))
    h["btf2"] = _spread(f[L + "btf2"])
    X = "L0_xattn_"
    for n, k in (("xwq", "wq"), ("xwk", "wk"), ("xwv", "wv"), ("xwo", "wo_w")):
        h[n] = _rows(f[X + k].T)
    h["wo_b"] = _spread(f[X + "wo_b"])
    h["gate0"] = _rows(f["L0_ffn_gate_w"].T)
    h["gate0_bias"] = f["L0_ffn_gate_b"].reshape(1, -1)
    half = DIM // 2
    inv_freq = (1.0 / np.float32(10000.0) ** (np.arange(half, dtype=np.float32) / half)).astype(np.float32)
    angle = (np.arange(SEQ, dtype=np.float32)[:, None] * inv_freq[None, :]).astype(np.float32).T
    h["cosT"] = np.ascontiguousarray(np.tile(np.cos(angle), (1, 2)).astype(np.float32))
    h["sinT"] = np.ascontiguousarray(np.tile(np.sin(angle), (1, 2)).astype(np.float32))
    row = np.arange(P)
    for name, halves in (("stack_q", (0, 1, 0)), ("stack_k", (0, 0, 1))):
        place = np.zeros((P, 2, 4, P), np.float32)
        for g in range(4):
            for j in range(2):
                for n, part in enumerate(halves):
                    for e in range(HD):
                        place[32 * g + HD * j + e, part, g, 64 * j + HD * n + e] = 1.0
        h[name] = place
    pick = np.zeros((P, BATCH_UNITS, P), np.float32)
    for n in range(BATCH_UNITS):
        pick[64 * (n % 2) + n, n] = pick[64 * (n % 2) + BATCH_UNITS + n, n] = 1.0
    h["pick_head"] = pick.reshape(P, 2, 2 * DIM)
    h["block_diag"] = (row[:, None] // HD == row[None, :] // HD).astype(np.float32)
    heads = np.zeros((8, 4, P), np.float32)
    for n in range(4):
        heads[n, n, :] = heads[4 + n, n, :] = 1.0
    h["head_rows"] = heads
    h["identity"] = np.eye(P, dtype=np.float32)
    h["after"] = (row[:, None] > row[None, :]).astype(np.float32)
    h["upto"] = (row[:, None] <= row[None, :]).astype(np.float32)
    q = (np.arange(2)[:, None] * P + row[None, :])[:, :, None]
    k = np.arange(SEQ)[None, None, :]
    window = np.where(np.abs(k - q) <= WINDOW, 0.0, MASKED)
    causal = np.where(k <= q, 0.0, MASKED)
    for n, m in (("window_mask", window), ("causal_mask", causal)):
        h[n] = np.ascontiguousarray(m.transpose(1, 0, 2).astype(np.float32))
    more_layout(f, h, np)
    return h


def kernel(**inputs):
    import numpy as np
    import concourse.bacc as bacc
    from concourse import mybir as mb
    from concourse.bass_utils import run_bass_kernel_spmd

    arrays = {n: np.ascontiguousarray(v) for n, v in layout(inputs).items()}
    nc = bacc.Bacc("TRN2", target_bir_lowering=False, num_devices=1)
    d = {n: nc.dram_tensor(f"in_{n}", v.shape, mb.dt.from_np(v.dtype), kind="ExternalInput").ap()
         for n, v in arrays.items()}
    out = nc.dram_tensor("out", (BATCH * SEQ, DIM), F32, kind="ExternalOutput").ap()
    build(nc, d, out)
    r = run_bass_kernel_spmd(nc, [{f"in_{n}": v for n, v in arrays.items()}], core_ids=[0])
    return r.results[0]["out"].reshape(BATCH, SEQ, DIM)
```

```python
from contextlib import ExitStack

import concourse.bass as bass
from concourse import mybir

F32 = mybir.dt.float32
BF16 = mybir.dt.bfloat16
U32 = mybir.dt.uint32
F32R = mybir.dt.float32r
ALU = mybir.AluOpType
ACT = mybir.ActivationFunctionType
AX = mybir.AxisListType

P = 128
BATCH, SEQ, DIM = 16, 256, 256
HEADS, HD = 16, 16
KT = DIM // P
PAIRS = BATCH // 2
TILES = 4
TOK = TILES * P
WINDOW = 64
EXPERTS0, DFF = 4, 1024
FB = DFF // P
EXPERTS1, INNER = 32, 128
ALL_EXPERTS = EXPERTS1 + 2
LN_EPS = 1e-5
MASKED = -1e30
FAR = -3e38
UNITS = 2 * HEADS
QUADS = UNITS // 4
BATCH_UNITS = 8
BATCHES = UNITS // BATCH_UNITS
LAG = 11
PROBS = 6
BLOCKS = HEADS // 2


class Signal:

    def __init__(self, ctx, nc, name, per, base=0):
        self.sem = ctx.enter_context(nc.semaphore(name))
        self.per = per
        self.base = base

    def __call__(self, it, k):
        return self.sem, it * self.per + (self.base + k)

    def after(self, iterations, per=None):
        later = Signal.__new__(Signal)
        later.sem, later.per, later.base = self.sem, self.per if per is None else per, self.base + iterations * self.per
        return later


def build(nc, d, out):
    with ExitStack() as ctx:
        def sb(name, shape, dt=F32):
            return ctx.enter_context(nc.sbuf_tensor(name, shape, dt))

        def signal(name, per, base=0):
            return Signal(ctx, nc, name, per, base)

        PS = ctx.enter_context(nc.psum_tensor("PS", [P, 8, 512], F32))
        xs = {n: nc.dram_tensor(f"scratch_{n}", (32 * P, DIM), F32).ap() for n in ("x2", "x3", "x5")}
        xsT = {n: nc.dram_tensor(f"scratch_{n}T", (DIM, 32 * P), F32).ap() for n in ("x2", "x3", "x5")}
        route_dram = nc.dram_tensor("scratch_route", (32 * P, ALL_EXPERTS), F32).ap()

        identity = sb("identity", [P, P])
        identity16 = sb("identity16", [P, P], BF16)
        ones = sb("ones", [P, P])
        after = sb("after", [P, P])
        upto = sb("upto", [P, P])
        minus_half = sb("minus_half", [P, TILES * 4])
        mean_col = sb("mean_col", [P, 1])
        eps6 = sb("eps6", [P, 1])
        window_mask = sb("window_mask", [P, 2, SEQ], BF16)
        causal_mask = sb("causal_mask", [P, 2, SEQ], BF16)
        block_diag = sb("block_diag", [P, P])
        expert_index = sb("expert_index", [1, 2 * BATCH + 4], U32)
        gate_weight = sb("gate_weight", [P, 2 * BATCH + 4])

        x = sb("x", [P, TILES, DIM])
        xT = sb("xT", [P, KT, TOK])
        cT = sb("cT", [P, KT, TOK])
        qT = sb("qT", [P, KT, TOK])
        kT = sb("kT", [P, KT, TOK])
        o = sb("o", [P, TILES, DIM])
        oT = sb("oT", [P, KT, TOK])
        rr = sb("rr", [P, TILES, DIM])
        xn = sb("xn", [P, TILES, DIM])
        xnT = sb("xnT", [P, KT, TOK])
        xb = sb("xb", [P, TILES, DIM])
        y = sb("y", [P, TILES, DIM])
        yT = sb("yT", [P, KT, TOK])
        stats = sb("stats", [P, TILES, 6])
        mv = sb("mv", [P, TILES, 2])
        var_eps = sb("var_eps", [P, TILES])
        rstd = sb("rstd", [P, TILES])

        attention_shared = ExitStack()
        sba = lambda name, shape, dt=F32: attention_shared.enter_context(nc.sbuf_tensor(name, shape, dt))
        q_high, q_low, k_high, k_low = (sba(n, [P, KT, TOK], F32R) for n in ("q_high", "q_low", "k_high", "k_low"))
        stack_q = sba("stack_q", [P, 2, 4, P], F32R)
        stack_k = sba("stack_k", [P, 2, 4, P], F32R)
        pick_head = sba("pick_head", [P, BATCH_UNITS, P], F32R)
        V1 = sba("V1", [P, TILES, HEADS, 32])
        prob = sba("prob", [P, PROBS, 2, SEQ])
        neg_max = sba("neg_max", [P, 2, HEADS])
        max_split = sba("max_split", [P, 2, P], F32R)
        maxT = sba("maxT", [P, 2, SEQ], F32R)
        outT = sba("outT", [P, 4, SEQ])
        inv_sum = sba("inv_sum", [P, 2, 2, HEADS])

        consts_ready = signal("consts_ready", 1)
        dve_chain = ctx.enter_context(nc.semaphore("dve_chain"))
        pool_chain = ctx.enter_context(nc.semaphore("pool_chain"))

        links = {}

        def link(eng, chain, ins):
            links[eng] = links.get(eng, 0) + 1
            ins.then_inc(chain, 1)
            eng.wait_ge(chain, links[eng])

        def restart(eng, chain):
            eng.sem_clear(chain)
            links[eng] = 0

        def tokens(t):
            return slice(t * P, (t + 1) * P)

        def attention_signals():
            return {k: signal(f"att_{k}", n) for k, n in
                    (("input", 1), ("V1", 1), ("high", KT), ("low", KT), ("stacked", 2 * BLOCKS), ("q", BLOCKS), ("k", BLOCKS),
                     ("scores", UNITS), ("max", UNITS), ("maxsplit", BATCHES), ("maxturned", BATCHES), ("maxT", BATCHES),
                     ("scoresT", UNITS), ("exp", UNITS), ("pv", QUADS), ("outT", 2), ("outturned", 2), ("normed", 2),
                     ("oturned", 2), ("oT", 2))}

        def stack_bank(n):
            return 2 + (n + 4) % 5

        def pe_attention(pe, it, a, mask, project_out):
            def stack(g):
                if g % 4 == 0:
                    pe.wait_ge(*a["low"](it, g // 4 + 1))
                for n in (2 * g, 2 * g + 1):
                    if n >= 5:
                        pe.wait_ge(*a[("q", "k")[(n - 5) % 2]](it, (n - 5) // 2 + 1))
                    high, low, place = ((q_high, q_low, stack_q), (k_high, k_low, stack_k))[n % 2]
                    bank = stack_bank(n)
                    pe.matmul(PS[:, bank, :], place[:, 0, g % 4, :], high[:, g // 4, :], start=True, stop=False)
                    pe.matmul(PS[:, bank, :], place[:, 1, g % 4, :], low[:, g // 4, :], start=False, stop=True)\
                        .then_inc(a["stacked"].sem, 1)

            def scores(n):
                s, h = n // HEADS, n % HEADS
                g, r = h // 2, 64 * (h % 2)
                if n >= 2:
                    pe.wait_ge(*a["max"](it, n - 1))
                if mask is not None:
                    pe.matmul(PS[:, h % 2, :], identity16[:, :], mask[:, :, :], start=True, stop=False)
                for qt in range(2):
                    last = pe.matmul(PS[:, h % 2, qt * SEQ:(qt + 1) * SEQ],
                                     stacked_q[r:r + 64, g, s * SEQ + qt * P:s * SEQ + (qt + 1) * P],
                                     stacked_k[r:r + 64, g, s * SEQ:(s + 1) * SEQ], start=(mask is None),
                                     stop=(mask is None or qt == 1))
                last.then_inc(a["scores"].sem, 1)

            def scores_t(n):
                s, h = n // HEADS, n % HEADS
                g, r = h // 2, 64 * (h % 2)
                bank, slot = 2 + h % 2, n // BATCH_UNITS % 2
                if n >= 2:
                    pe.wait_ge(*a["exp"](it, n - 1))
                if mask is not None:
                    pe.matmul(PS[:, bank, :], identity16[:, :], mask[:, :, :], start=True, stop=False)
                pe.matmul(PS[:, bank, :].rearrange("p (k q) -> p k q", k=2), pick_head[:, n % BATCH_UNITS, :],
                          maxT[:, slot, :].unsqueeze(1).to_broadcast([P, 2, SEQ]), start=(mask is None), stop=False)
                for kt in range(2):
                    last = pe.matmul(PS[:, bank, kt * SEQ:(kt + 1) * SEQ],
                                     stacked_k[r:r + 64, g, s * SEQ + kt * P:s * SEQ + (kt + 1) * P],
                                     stacked_q[r:r + 64, g, s * SEQ:(s + 1) * SEQ], start=False, stop=(kt == 1))
                last.then_inc(a["scoresT"].sem, 1)

            def values(quad):
                pe.wait_ge(*a["exp"](it, 4 * quad + 4))
                for kt in range(2):
                    for n in range(4 * quad, 4 * quad + 4):
                        s, h = n // HEADS, n % HEADS
                        last = pe.matmul(PS[32 * (h % 4):32 * (h % 4) + 32, 4 + 2 * s + h // 8,
                                            (h // 4 % 2) * SEQ:(h // 4 % 2 + 1) * SEQ],
                                         V1[:, 2 * s + kt, h, :], prob[:, n % PROBS, kt, :], start=(kt == 0), stop=(kt == 1))
                last.then_inc(a["pv"].sem, 1)

            def turn_max(b):
                pe.wait_ge(*a["maxsplit"](it, b + 1))
                for qt in range(2):
                    last = pe.transpose(PS[:, 7, qt * P:(qt + 1) * P], max_split[:, qt, :].bitcast(F32), identity[:, :])
                last.then_inc(a["maxturned"].sem, 1)

            def turn_out(s):
                pe.wait_ge(*a["outT"](it, s + 1))
                for qt in range(2):
                    for g in range(4):
                        last = pe.transpose(PS[:, 4 + 2 * s + qt, g * P:(g + 1) * P],
                                            outT[:, g, qt * P:(qt + 1) * P], identity[:, :])
                last.then_inc(a["outturned"].sem, 1)

            def turn_normed(s):
                pe.wait_ge(*a["normed"](it, s + 1))
                pe_turn(pe, o, 4 + s, 2, 2 * s).then_inc(a["oturned"].sem, 1)

            stack(0)
            stack(1)
            pe.wait_ge(*a["V1"](it, 1))
            for n in range(UNITS + LAG):
                if n % 2 == 0 and n // 2 + 2 < BLOCKS:
                    stack(n // 2 + 2)
                if n % 2 == 0 and n // 2 < BLOCKS:
                    pe.wait_ge(*a["k"](it, n // 2 + 1))
                if n < UNITS:
                    scores(n)
                if n % BATCH_UNITS == 1 and 1 < n < UNITS or n == UNITS + 2:
                    turn_max(n // BATCH_UNITS - 1)
                t = n - LAG
                if t >= 0:
                    if t % BATCH_UNITS == 0:
                        pe.wait_ge(*a["maxT"](it, t // BATCH_UNITS + 1))
                    scores_t(t)
                    if t >= 5 and t % 4 == 1:
                        values(t // 4 - 1)
                    if t == HEADS + 6:
                        turn_out(0)
                    if t == HEADS + 12:
                        turn_normed(0)
            values(QUADS - 1)
            pe.wait_ge(*a["oT"](it, 1))
            project_out(0)
            turn_out(1)
            turn_normed(1)
            pe.wait_ge(*a["oT"](it, 2))
            project_out(1)

        def act_high(act, it, a, q_scale):
            act.wait_ge(*a["input"](it, 1))
            for ki in range(KT):
                act.activation(q_high[:, ki, :], qT[:, ki, :], ACT.Copy, scale=q_scale)
                act.activation(k_high[:, ki, :], kT[:, ki, :], ACT.Copy).then_inc(a["high"].sem, 1)

        def act_attention(act, it, a):
            for n in range(2 * BLOCKS):
                act.wait_ge(*a["stacked"](it, n + 1))
                dst, done = ((stacked_q, "q"), (stacked_k, "k"))[n % 2]
                act.activation(dst[:, n // 2, :], PS[:, stack_bank(n), :], ACT.Copy).then_inc(a[done].sem, 1)
            for n in range(UNITS):
                act.wait_ge(*a["scoresT"](it, n + 1))
                if n >= PROBS:
                    act.wait_ge(*a["pv"](it, (n - PROBS) // 4 + 1))
                act.activation(prob[:, n % PROBS, :, :].rearrange("p k q -> p (k q)"), PS[:, 2 + n % 2, :], ACT.Exp)\
                    .then_inc(a["exp"].sem, 1)
                if n == HEADS + 6:
                    act.wait_ge(*a["pv"](it, QUADS // 2))
                    act.activation(outT[:, :, :].rearrange("p (k a) q -> p k (a q)", a=2), PS[:, 4:6, :], ACT.Copy)\
                        .then_inc(a["outT"].sem, 1)
                if n == HEADS + 14:
                    act.wait_ge(*a["oturned"](it, 1))
                    act_turned(act, oT, 4, 2, 0).then_inc(a["oT"].sem, 1)
            act.wait_ge(*a["pv"](it, QUADS))
            act.wait_ge(*a["outturned"](it, 1))
            act.activation(outT[:, :, :].rearrange("p (k a) q -> p k (a q)", a=2), PS[:, 6:8, :], ACT.Copy)\
                .then_inc(a["outT"].sem, 1)
            act.wait_ge(*a["oturned"](it, 2))
            act_turned(act, oT, 5, 2, 2).then_inc(a["oT"].sem, 1)

        def dve_attention(dve, it, a, q_scale, evacuate_values=None, between=None):
            for ki in range(KT):
                dve.wait_ge(*a["high"](it, ki + 1))
                dve.scalar_tensor_tensor(out=q_low[:, ki, :], in0=qT[:, ki, :], scalar=q_scale,
                                         in1=q_high[:, ki, :].bitcast(F32), op0=ALU.mult, op1=ALU.subtract)
                dve.tensor_tensor(k_low[:, ki, :], kT[:, ki, :], k_high[:, ki, :].bitcast(F32), ALU.subtract)\
                    .then_inc(a["low"].sem, 1)

            def copy_max(b):
                dve.wait_ge(*a["maxturned"](it, b + 1))
                if b >= 2:
                    dve.wait_ge(*a["scoresT"](it, (b - 1) * BATCH_UNITS))
                dve.tensor_copy(maxT[:, b % 2, :], PS[:, 7, 0:SEQ]).then_inc(a["maxT"].sem, 1)

            if evacuate_values is not None:
                evacuate_values()
            for n in range(UNITS):
                h = n % HEADS
                dve.wait_ge(*a["scores"](it, n + 1))
                dve.tensor_reduce(neg_max[:, :, h], PS[:, h % 2, :].rearrange("p (q k) -> p q k", q=2),
                                  AX.X, ALU.max, negate=True).then_inc(a["max"].sem, 1)
                b = n // BATCH_UNITS
                if n % BATCH_UNITS == BATCH_UNITS - 1:
                    dve.wait_ge(*a["max"](it, n + 1))
                    split = max_split[:, :, :].rearrange("p q (w r) -> p q w r", w=2)
                    twice = neg_max[:, :, h + 1 - BATCH_UNITS:h + 1].unsqueeze(2).to_broadcast([P, 2, 2, BATCH_UNITS])
                    high = split[:, :, :, 0:BATCH_UNITS]
                    link(dve, dve_chain, dve.tensor_copy(high, twice))
                    dve.tensor_tensor(split[:, :, :, BATCH_UNITS:2 * BATCH_UNITS], twice, high.bitcast(F32), ALU.subtract)\
                        .then_inc(a["maxsplit"].sem, 1)
                if n % BATCH_UNITS == 1 and b > 0:
                    copy_max(b - 1)
            copy_max(BATCHES - 1)
            for s in range(2):
                dve.wait_ge(*a["outturned"](it, s + 1))
                heads = PS[:, 4 + 2 * s:6 + 2 * s, :].rearrange("p q (h e) -> p q h e", e=32)
                link(dve, dve_chain, dve.reciprocal(inv_sum[:, s, :, :], heads[:, :, :, HD]))
                dve.tensor_tensor(o[:, 2 * s:2 * s + 2, :].rearrange("p q (h e) -> p q h e", e=HD), heads[:, :, :, 0:HD],
                                  inv_sum[:, s, :, :].unsqueeze(3).to_broadcast([P, 2, HEADS, HD]), ALU.mult)\
                    .then_inc(a["normed"].sem, 1)
                if s == 0 and between is not None:
                    between()

        def pe_turn(pe, src, bank, tiles=TILES, first=0):
            for t in range(tiles):
                for ki in range(KT):
                    last = pe.transpose(PS[:, bank + t // 2, ((t % 2) * 2 + ki) * P:((t % 2) * 2 + ki + 1) * P],
                                        src[:, first + t, ki * P:(ki + 1) * P], identity[:, :])
            return last

        def act_turned(act, dst, bank, tiles=TILES, first=0):
            for b in range(tiles // 2):
                last = act.activation(
                    dst[:, :, (first + 2 * b) * P:(first + 2 * b + 2) * P].rearrange("p k (t j) -> p t k j", t=2),
                    PS[:, bank + b, :].rearrange("p (t k j) -> p t k j", t=2, k=2), ACT.Copy)
            return last

        def dve_stats(dve, src, ready, tiles=TILES, first=0):
            for t in range(first, first + tiles):
                ins = dve.bn_stats(stats[:, t, :], src[:, t, :])
            link(dve, dve_chain, ins)
            for t in range(first, first + tiles):
                ins = dve.bn_aggr(mv[:, t, :], stats[:, t, :])
            link(dve, dve_chain, ins)
            dve.tensor_scalar(var_eps[:, first:first + tiles], mv[:, first:first + tiles, 1], LN_EPS, None, ALU.add).then_inc(ready.sem, 1)

        def dve_normalise(dve, dst, src, tiles=TILES, first=0):
            for t in range(first, first + tiles):
                ins = dve.tensor_scalar(dst[:, t, :], src[:, t, :], mv[:, t, 0:1], rstd[:, t:t + 1],
                                        ALU.subtract, ALU.mult)
            return ins

        def pool_rstd(pool, it, var_ready, rstd_ready, k=1, tiles=TILES, first=0):
            pool.wait_ge(*var_ready(it, k))
            pool.tensor_tensor(rstd[:, first:first + tiles], var_eps[:, first:first + tiles], minus_half[:, 0:tiles], ALU.pow).then_inc(rstd_ready.sem, 1)

        attention_buffers, phase1_buffers, phase2_buffers = ExitStack(), ExitStack(), ExitStack()
        stacked_q, stacked_k = (attention_buffers.enter_context(nc.sbuf_tensor(n, [P, BLOCKS, TOK], F32R))
                                for n in ("stacked_q", "stacked_k"))
        attention_buffers.close()
        STACKED = 2 * BLOCKS * TOK
        sb1 = lambda name, shape, dt=F32: phase1_buffers.enter_context(nc.sbuf_tensor(name, shape, dt))
        big = sb1("big", [P, TILES, 512])
        kw = big[:, :, :].rearrange("p t (f d) -> p t f d", f=2)
        qk = sb1("qk", [P, TILES, 512])
        vs = sb1("vs", [P, TILES, DIM])
        qkT = sb1("qkT", [P, 4, TOK])
        sb1("under_stacked1", [P, STACKED - TILES * (512 + 512 + DIM) - 4 * TOK])
        wqk = sb1("wqk", [P, KT, 2 * DIM])
        wvg = sb1("wvg", [P, KT, DIM + 48])
        wo = sb1("wo", [P, KT, DIM])
        xwq, xwk, xwv, xwo = (sb1(f"x{n}", [P, KT, DIM]) for n in ("wq", "wk", "wv", "wo"))
        wtf1 = sb1("wtf1", [P, KT, P])
        wtf2 = sb1("wtf2", [P, HEADS])
        gate0 = sb1("gate0", [P, KT, EXPERTS0])
        gate0_bias = sb1("gate0_bias", [1, EXPERTS0])
        decay_bias = sb1("decay_bias", [P, 48])
        btf1 = sb1("btf1", [P, 1])
        btf2 = sb1("btf2", [P, 1])
        nbtf1 = sb1("nbtf1", [P, 1])
        nbtf2 = sb1("nbtf2", [P, 1])
        wo_b = sb1("wo_b", [P, DIM])
        cosT = sb1("cosT", [P, TOK])
        sinT = sb1("sinT", [P, TOK])
        gate_sb = sb1("gate_sb", [P, TILES, 48])
        gate_exp = sb1("gate_exp", [P, TILES, 48])
        sig = sb1("sig", [P, TILES, 48])
        log_decay = sb1("log_decay", [P, TILES, 32])
        decay = sb1("decay", [P, TILES, 32])
        sumsq = sb1("sumsq", [P, P])
        root = sb1("root", [P, P])
        inv_norm = sb1("inv_norm", [P, P])
        inv_decay_sum = sb1("inv_decay_sum", [P, 64])
        memory = sb1("memory", [P, 2, 2, KT, P])
        hid_exp = sb1("hid_exp", [P, TOK])
        hid = sb1("hid", [P, TOK])
        flux = sb1("flux", [P, TILES * HEADS])
        alpha = sb1("alpha", [P, TILES, HEADS])
        one_minus = sb1("one_minus", [P, TILES, HEADS])
        rope_a = sb1("rope_a", [P, TOK])
        rope_b = sb1("rope_b", [P, TOK])
        meanT = sb1("meanT", [P, 4])
        logits8 = sb1("logits8", [1, 2, 8])
        top8 = sb1("top8", [1, 2, 8])
        top8_index = sb1("top8_index", [1, 2, 8], U32)
        neg_top = sb1("neg_top", [1, 2])
        logit_exp = sb1("logit_exp", [1, 2, 6])
        logit_sum = sb1("logit_sum", [1, 2])
        chosen_weight = sb1("chosen_weight", [1, 4])

        weights_loaded = signal("weights_loaded", 0)
        in1 = signal("in1", 48)
        one = {n: signal(f"l0_{n}", 2 if n in ("var", "rstd", "y2") else 1) for n in (
            "qk", "vg", "sq", "gz", "gexp", "sumsq", "root", "sig", "kb", "logd", "suffix", "decay", "turned", "qkT",
            "kw", "mem", "memory", "hid", "hexp", "hidden", "flux", "fexp", "o_ps", "o", "oturned", "oT", "y",
            "var", "rstd", "x1", "x1turned", "x1T", "k", "v", "q",
            "y2", "x1b", "x2", "x2turned", "x2T", "mean", "meanT",
            "logits", "top", "lexp", "chosen", "spread", "chosen_out")}
        att1 = attention_signals()
        stored1 = signal("stored1", 32, base=32)

        mask_stage = [big[:, n, :].rearrange("p (t k) -> p t k", t=2) for n in range(2)]
        stack_stage = [qkT[:, 2 * n:2 * n + 2, :].rearrange("p n (g r) -> p n g r", g=4) for n in range(2)]
        X1_WEIGHTS = [(wqk, "wqk"), (wvg, "wvg"), (wo, "wo"), (xwq, "xwq"), (xwk, "xwk"), (xwv, "xwv"), (xwo, "xwo"),
                      (wtf1, "wtf1"), (wtf2, "wtf2"), (gate0, "gate0"), (gate0_bias, "gate0_bias"),
                      (decay_bias, "decay_bias"), (btf1, "btf1"), (btf2, "btf2"), (wo_b, "wo_b"),
                      (cosT, "cosT"), (sinT, "sinT"), (stack_stage[0], "stack_q"), (stack_stage[1], "stack_k"),
                      (qk[:, 0:2, :], "pick_head"),
                      (block_diag, "block_diag"), (identity, "identity"),
                      (after, "after"), (upto, "upto"), (mask_stage[0], "window_mask"), (mask_stage[1], "causal_mask")]
        WEIGHTS1 = 16 * len(X1_WEIGHTS)

        def rows(ap, it, n):
            return ap[bass.ds(it * (n * P), n * P), :].rearrange("(t p) f -> p t f", p=P)

        def columns(ap, it, n):
            return ap[:, bass.ds(it * n * P, n * P)].rearrange("(k p) t -> p k t", p=P)

        def sp_load1(sp, it):
            sp.dma_start(xT[:, :, :], columns(d["xT"], it, TILES)).then_inc(in1.sem, 16)
            sp.dma_start(cT[:, :, :], columns(d["ctxT"], it, TILES)).then_inc(in1.sem, 16)
            sp.dma_start(x[:, :, :], rows(d["x"], it, TILES)).then_inc(in1.sem, 16)

        def sp_store1(sp, it):
            sp.wait_ge(*one["x2"](it, 1))
            sp.dma_start(rows(xs["x2"], it, TILES), y[:, :, :]).then_inc(stored1.sem, 16)
            sp.wait_ge(*one["x2T"](it, 1))
            sp.dma_start(columns(xsT["x2"], it, TILES), yT[:, :, :]).then_inc(stored1.sem, 16)

        def sp_phase1(sp):
            sp.sem_inc(stored1.sem, 32)
            for dst, name in X1_WEIGHTS:
                sp.dma_start(dst[tuple(slice(None) for _ in dst.shape)], d[name]).then_inc(weights_loaded.sem, 16)
            sp_load1(sp, 0)
            with sp.Fori(0, PAIRS - 1) as it:
                sp.wait_ge(*one["x1"](it, 1))
                sp.wait_ge(*one["v"](it, 1))
                sp_load1(sp, it + 1)
                sp_store1(sp, it)
            sp_store1(sp, PAIRS - 1)
            sp.wait_ge(*stored1(PAIRS - 1, 32))

        def pe_phase1(pe):
            pe.wait_ge(weights_loaded.sem, WEIGHTS1)
            pe.wait_ge(*consts_ready(0, 1))

            def project_qk(it):
                pe.wait_ge(*in1(it, 48))
                for t in range(TILES):
                    for ki in range(KT):
                        last = pe.matmul(PS[:, t, :], xT[:, ki, tokens(t)], wqk[:, ki, :],
                                         start=(ki == 0), stop=(ki == 1))
                last.then_inc(one["qk"].sem, 1)

            def mix(it, final):
                for t in range(TILES):
                    for ki in range(KT):
                        last = pe.matmul(PS[:, 4 + t, 0:DIM + 48], xT[:, ki, tokens(t)], wvg[:, ki, :],
                                         start=(ki == 0), stop=(ki == 1))
                last.then_inc(one["vg"].sem, 1)
                pe.wait_ge(*one["kb"](it, 1))
                pe.wait_ge(*one["logd"](it, 1))
                for s in range(2):
                    first, second = log_decay[:, 2 * s, :], log_decay[:, 2 * s + 1, :]
                    pe.matmul(PS[:, 0, 64 * s:64 * s + 32], after[:, :], first, start=True, stop=False)
                    pe.matmul(PS[:, 0, 64 * s:64 * s + 32], ones[:, :], second, start=False, stop=True)
                    last = pe.matmul(PS[:, 0, 64 * s + 32:64 * s + 64], after[:, :], second, start=True, stop=True)
                last.then_inc(one["suffix"].sem, 1)
                for t in range(TILES):
                    for cc in range(4):
                        last = pe.transpose(PS[:, 1 + t, cc * P:(cc + 1) * P], qk[:, t, cc * P:(cc + 1) * P],
                                            identity[:, :])
                last.then_inc(one["turned"].sem, 1)
                pe.wait_ge(*one["kw"](it, 1))
                for s in range(2):
                    for tt in range(2):
                        pe.matmul(PS[:, 7, 32 * s:32 * s + 32], ones[:, :], decay[:, 2 * s + tt, :],
                                  start=(tt == 0), stop=(tt == 1))
                    for fs in range(2):
                        for half in range(KT):
                            for tt in range(2):
                                last = pe.matmul(PS[:, 5 + s, (fs * 2 + half) * P:(fs * 2 + half + 1) * P],
                                                 kw[:, 2 * s + tt, fs, half * P:(half + 1) * P],
                                                 vs[:, 2 * s + tt, half * P:(half + 1) * P],
                                                 start=(tt == 0), stop=(tt == 1))
                last.then_inc(one["mem"].sem, 1)
                pe.wait_ge(*one["decay"](it, 1))
                pe.wait_ge(*one["qkT"](it, 1))
                for ki in range(KT):
                    last = pe.matmul(PS[:, 0, :], wtf1[:, ki, :], qkT[:, 2 + ki, :], start=(ki == 0), stop=(ki == 1))
                last.then_inc(one["hid"].sem, 1)
                for blk in range(2):
                    for ki in range(KT):
                        last = pe.matmul(PS[:, 2 + blk, :], xwk[:, ki, blk * P:(blk + 1) * P], cT[:, ki, :],
                                         start=(ki == 0), stop=(ki == 1))
                last.then_inc(one["k"].sem, 1)
                pe.wait_ge(*one["hidden"](it, 1))
                for t in range(TILES):
                    last = pe.matmul(PS[:, 0, t * HEADS:(t + 1) * HEADS], hid[:, tokens(t)], wtf2[:, :],
                                     start=True, stop=True)
                last.then_inc(one["flux"].sem, 1)
                pe.wait_ge(*one["memory"](it, 1))
                for t in range(TILES):
                    for half in range(KT):
                        last = pe.matmul(PS[:, 4 + t, half * 2 * P:(half + 1) * 2 * P], qkT[:, half, tokens(t)],
                                         memory[:, t // 2, :, half, :],
                                         start=True, stop=True)
                last.then_inc(one["o_ps"].sem, 1)
                pe.wait_ge(*one["o"](it, 1))
                pe_turn(pe, o, 6).then_inc(one["oturned"].sem, 1)
                for t in range(TILES):
                    for ki in range(KT):
                        last = pe.matmul(PS[:, 4 + t // 2, (t % 2) * DIM:(t % 2 + 1) * DIM], cT[:, ki, tokens(t)],
                                         xwv[:, ki, :], start=(ki == 0), stop=(ki == 1))
                last.then_inc(one["v"].sem, 1)
                pe.wait_ge(*one["oT"](it, 1))
                for t in range(TILES):
                    for ki in range(KT):
                        last = pe.matmul(PS[:, t // 2, (t % 2) * DIM:(t % 2 + 1) * DIM], oT[:, ki, tokens(t)],
                                         wo[:, ki, :], start=(ki == 0), stop=(ki == 1))
                last.then_inc(one["y"].sem, 1)
                pe.wait_ge(*one["x1"](it, 1))
                pe_turn(pe, xn, 6).then_inc(one["x1turned"].sem, 1)
                pe.wait_ge(*one["x1T"](it, 1))
                for blk in range(2):
                    for ki in range(KT):
                        last = pe.matmul(PS[:, blk, :], xwq[:, ki, blk * P:(blk + 1) * P], xnT[:, ki, :],
                                         start=(ki == 0), stop=(ki == 1))
                last.then_inc(one["q"].sem, 1)

                def project_out(s):
                    for t in range(2 * s, 2 * s + 2):
                        for ki in range(KT):
                            last = pe.matmul(PS[:, 4 + s, (t % 2) * DIM:(t % 2 + 1) * DIM], oT[:, ki, tokens(t)],
                                             xwo[:, ki, :], start=(ki == 0), stop=(ki == 1))
                    last.then_inc(one["y2"].sem, 1)

                pe_attention(pe, it, att1, window_mask, project_out)
                if not final:
                    project_qk(it + 1)
                pe.wait_ge(*one["x2"](it, 1))
                pe_turn(pe, y, 6).then_inc(one["x2turned"].sem, 1)
                for s in range(2):
                    for half in range(KT):
                        for tt in range(2):
                            last = pe.matmul(PS[:, 4, s * 2 + half:s * 2 + half + 1],
                                             y[:, 2 * s + tt, half * P:(half + 1) * P], mean_col[:, :],
                                             start=(tt == 0), stop=(tt == 1))
                last.then_inc(one["mean"].sem, 1)
                pe.wait_ge(*one["meanT"](it, 1))
                for s in range(2):
                    for ki in range(KT):
                        last = pe.matmul(PS[0:1, 5, s * 8:s * 8 + EXPERTS0], meanT[:, s * 2 + ki:s * 2 + ki + 1],
                                         gate0[:, ki, :], start=(ki == 0), stop=(ki == 1))
                last.then_inc(one["logits"].sem, 1)
                pe.wait_ge(*one["chosen"](it, 1))
                pe.matmul(PS[:, 4, 0:4], ones[0:1, :], chosen_weight[:, :], start=True, stop=True)\
                    .then_inc(one["spread"].sem, 1)
                pe.wait_ge(*one["x2T"](it, 1))
                pe.wait_ge(*one["chosen_out"](it, 1))

            project_qk(0)
            with pe.Fori(0, PAIRS - 1) as it:
                mix(it, False)
            mix(PAIRS - 1, True)

        def act_phase1(act):
            act.wait_ge(weights_loaded.sem, WEIGHTS1)
            act.wait_ge(*consts_ready(0, 1))
            with act.Fori(0, PAIRS) as it:
                act.wait_ge(*one["qk"](it, 1))
                act.activation(big[:, :, :], PS[:, 0:4, :], ACT.Square).then_inc(one["sq"].sem, 1)
                act.wait_ge(*one["sumsq"](it, 1))
                act.activation(root[:, :], sumsq[:, :], ACT.Sqrt).then_inc(one["root"].sem, 1)
                act.wait_ge(*one["gz"](it, 1))
                act.activation(gate_exp[:, :, :], gate_sb[:, :, :], ACT.Exp, scale=-1.0).then_inc(one["gexp"].sem, 1)
                act.wait_ge(*one["sig"](it, 1))
                act.activation(log_decay[:, :, :], sig[:, :, 16:48], ACT.Ln, bias=eps6[:, :])\
                    .then_inc(one["logd"].sem, 1)
                act.wait_ge(*one["suffix"](it, 1))
                act.activation(decay[:, :, :], PS[:, 0, 0:128].rearrange("p (t h) -> p t h", t=TILES), ACT.Exp)\
                    .then_inc(one["decay"].sem, 1)
                act.wait_ge(*one["turned"](it, 1))
                act.activation(qkT[:, :, :].rearrange("p c (t j) -> p t c j", t=TILES),
                               PS[:, 1:5, :].rearrange("p t (c j) -> p t c j", c=4), ACT.Copy)\
                    .then_inc(one["qkT"].sem, 1)
                act.wait_ge(*one["hid"](it, 1))
                act.activation(hid_exp[:, :], PS[:, 0, :], ACT.Exp, bias=nbtf1[:, :], scale=-1.0)\
                    .then_inc(one["hexp"].sem, 1)
                act.wait_ge(*one["flux"](it, 1))
                act.activation(flux[:, :], PS[:, 0, 0:64], ACT.Exp, bias=nbtf2[:, :], scale=-1.0)\
                    .then_inc(one["fexp"].sem, 1)
                act.wait_ge(*one["oturned"](it, 1))
                act_turned(act, oT, 6).then_inc(one["oT"].sem, 1)
                act.wait_ge(*one["v"](it, 1))
                for b in range(2):
                    last = act.activation(V1[:, 2 * b:2 * b + 2, :, 0:HD],
                                          PS[:, 4 + b, :].rearrange("p (t h e) -> p t h e", t=2, h=HEADS), ACT.Copy)
                last.then_inc(att1["V1"].sem, 1)
                act.wait_ge(*one["x1turned"](it, 1))
                act_turned(act, xnT, 6).then_inc(one["x1T"].sem, 1)
                act_high(act, it, att1, 1.0)
                act_attention(act, it, att1)
                act.wait_ge(*one["x2turned"](it, 1))
                act.wait_ge(*stored1(it, 0))
                act_turned(act, yT, 6).then_inc(one["x2T"].sem, 1)
                act.wait_ge(*one["top"](it, 1))
                for s in range(2):
                    act.activation(logit_exp[:, s, 0:EXPERTS0], logits8[:, s, 0:EXPERTS0], ACT.Exp,
                                   bias=neg_top[:, s:s + 1], accum_out=logit_sum[:, s:s + 1])
                    last = act.activation(logit_exp[:, s, 4:6], top8[:, s, 0:2], ACT.Exp, bias=neg_top[:, s:s + 1])
                last.then_inc(one["lexp"].sem, 1)

        def dve_phase1(dve):
            dve.wait_ge(weights_loaded.sem, WEIGHTS1)
            link(dve, dve_chain, dve.memset(V1[:, :, :, :], 0.0))
            dve.memset(V1[:, :, :, HD:HD + 1], 1.0)
            for n, dst in enumerate((stack_q, stack_k)):
                dve.tensor_copy(dst[:, :, :, :], stack_stage[n])
            dve.tensor_copy(pick_head[:, :, :].rearrange("p h k -> p (h k)"),
                            qk[:, 0:2, :].rearrange("p t f -> p (t f)"))
            dve.memset(max_split[:, :, :].bitcast(F32), 0.0)
            dve.memset(logits8[:, :, :], FAR)
            dve.tensor_scalar(nbtf1[:, :], btf1[:, :], -1.0, None, ALU.mult)
            link(dve, dve_chain, dve.tensor_scalar(nbtf2[:, :], btf2[:, :], -1.0, None, ALU.mult))
            dve.memset(eps6[:, :], 1e-6)
            dve.tensor_copy(window_mask[:, :, :], mask_stage[0])
            dve.tensor_copy(causal_mask[:, :, :], mask_stage[1])
            dve.tensor_copy(identity16[:, :], identity[:, :])
            dve.memset(mean_col[:, :], 1.0 / SEQ)
            dve.memset(minus_half[:, :], -0.5)
            dve.memset(ones[:, :], 1.0).then_inc(consts_ready.sem, 1)
            dve.wait_ge(*consts_ready(0, 1))
            with dve.Fori(0, PAIRS) as it:
                restart(dve, dve_chain)
                heads = lambda ap: ap.rearrange("p t (h e) -> p t h e", e=HD)
                spread = lambda ap: ap.unsqueeze(3).to_broadcast([P, TILES, HEADS, HD])
                dve.wait_ge(*one["sq"](it, 1))
                link(dve, dve_chain, dve.tensor_reduce(sumsq[:, :], big[:, :, :].rearrange("p t (h e) -> p (t h) e", e=HD),
                                                       AX.X, ALU.add))
                dve.tensor_scalar(sumsq[:, :], sumsq[:, :], 1e-24, None, ALU.max).then_inc(one["sumsq"].sem, 1)
                dve.wait_ge(*one["root"](it, 1))
                link(dve, dve_chain, dve.reciprocal(inv_norm[:, :], root[:, :]))
                link(dve, dve_chain, dve.tensor_tensor(root[:, :], inv_norm[:, :], inv_norm[:, :], ALU.mult))
                link(dve, dve_chain, dve.tensor_tensor(root[:, :], root[:, :], sumsq[:, :], ALU.mult))
                link(dve, dve_chain, dve.tensor_scalar(root[:, :], root[:, :], -0.5, 1.5, ALU.mult, ALU.add))
                link(dve, dve_chain, dve.tensor_tensor(inv_norm[:, :], inv_norm[:, :], root[:, :], ALU.mult))
                link(dve, dve_chain, dve.tensor_tensor(
                    qk[:, :, :].rearrange("p t (h e) -> p (t h) e", e=HD),
                    PS[:, 0:4, :].rearrange("p t (h e) -> p (t h) e", e=HD),
                    inv_norm[:, :].unsqueeze(2).to_broadcast([P, P, HD]), ALU.mult))
                dve.wait_ge(*one["vg"](it, 1))
                dve.tensor_tensor(gate_sb[:, :, :], PS[:, 4:8, DIM:DIM + 48],
                                  decay_bias[:, :].unsqueeze(1).to_broadcast([P, TILES, 48]),
                                  ALU.add).then_inc(one["gz"].sem, 1)
                dve.wait_ge(*one["gexp"](it, 1))
                link(dve, dve_chain, dve.tensor_scalar(gate_exp[:, :, :], gate_exp[:, :, :], 1.0, None, ALU.add))
                dve.reciprocal(sig[:, :, :], gate_exp[:, :, :]).then_inc(one["sig"].sem, 1)
                dve.wait_ge(*one["sig"](it, 1))
                dve.tensor_tensor(heads(vs[:, :, :]), heads(PS[:, 4:8, 0:DIM]), spread(sig[:, :, 0:HEADS]), ALU.mult)
                kbeta = heads(qk[:, :, DIM:2 * DIM])
                dve.tensor_tensor(kbeta, kbeta, spread(sig[:, :, 0:HEADS]), ALU.mult).then_inc(one["kb"].sem, 1)
                dve.wait_ge(*one["kb"](it, 1))
                dve.wait_ge(*one["decay"](it, 1))
                for fs in range(2):
                    last = dve.tensor_tensor(heads(kw[:, :, fs, :]), kbeta,
                                             spread(decay[:, :, fs * HEADS:(fs + 1) * HEADS]), ALU.mult)
                last.then_inc(one["kw"].sem, 1)
                dve.wait_ge(*one["mem"](it, 1))
                link(dve, dve_chain, dve.tensor_scalar(inv_decay_sum[:, :], PS[:, 7, 0:64], 1e-6, None, ALU.add))
                link(dve, dve_chain, dve.reciprocal(inv_decay_sum[:, :], inv_decay_sum[:, :]))
                for s in range(2):
                    scaled = memory[:, s, :, :, :].rearrange("p f k (h e) -> p (f k h) e", e=HD)
                    flat_memory = memory[:, s, :, :, :].rearrange("p f k e -> p (f k) e")
                    link(dve, dve_chain, dve.tensor_tensor(
                        scaled, PS[:, 5 + s, :].rearrange("p (g e) -> p g e", e=HD),
                        inv_decay_sum[:, 32 * s:32 * s + 32].unsqueeze(2).to_broadcast([P, 32, HD]), ALU.mult))
                    last = dve.tensor_tensor(flat_memory, flat_memory,
                                             block_diag[:, :].unsqueeze(1).to_broadcast([P, 4, P]), ALU.mult)
                last.then_inc(one["memory"].sem, 1)
                dve.wait_ge(*one["hexp"](it, 1))
                link(dve, dve_chain, dve.tensor_scalar(hid_exp[:, :], hid_exp[:, :], 1.0, None, ALU.add))
                link(dve, dve_chain, dve.reciprocal(hid_exp[:, :], hid_exp[:, :]))
                dve.scalar_tensor_tensor(out=hid[:, :], in0=PS[:, 0, :], scalar=btf1[:, :], in1=hid_exp[:, :],
                                         op0=ALU.add, op1=ALU.mult).then_inc(one["hidden"].sem, 1)
                def rope(pa, pb, scale, dst):
                    for sign, first, second, blk in ((ALU.subtract, cosT, sinT, 0), (ALU.add, sinT, cosT, 1)):
                        dve.scalar_tensor_tensor(out=rope_a[:, :], in0=pa, scalar=scale, in1=first[:, :],
                                                 op0=ALU.mult, op1=ALU.mult)
                        link(dve, dve_chain, dve.scalar_tensor_tensor(out=rope_b[:, :], in0=pb, scalar=scale,
                                                                      in1=second[:, :], op0=ALU.mult, op1=ALU.mult))
                        link(dve, dve_chain, dve.tensor_tensor(dst[:, blk, :], rope_a[:, :], rope_b[:, :], sign))

                dve.wait_ge(*one["k"](it, 1))
                rope(PS[:, 2, :], PS[:, 3, :], 1.0, kT)
                dve.wait_ge(*one["fexp"](it, 1))
                link(dve, dve_chain, dve.tensor_scalar(flux[:, :], flux[:, :], 1.0, None, ALU.add))
                link(dve, dve_chain, dve.reciprocal(flux[:, :], flux[:, :]))
                link(dve, dve_chain, dve.tensor_scalar(flux[:, :], flux[:, :], 0.01, 0.99, ALU.max, ALU.min))
                flat = lambda ap: ap.rearrange("p t h -> p (t h)")
                link(dve, dve_chain, dve.tensor_scalar(flat(alpha[:, :, :]), flux[:, :], 0.3, 0.5, ALU.mult, ALU.add))
                link(dve, dve_chain, dve.tensor_scalar(flat(one_minus[:, :, :]), flat(alpha[:, :, :]), -1.0, 1.0,
                                                       ALU.mult, ALU.add))
                dve.wait_ge(*one["o_ps"](it, 1))
                for t in range(TILES):
                    for fs, (dst, w) in enumerate(((o, alpha), (rr, one_minus))):
                        last = dve.tensor_tensor(
                            dst[:, t, :].rearrange("p (k h e) -> p k h e", k=KT, e=HD),
                            PS[:, 4 + t, :].rearrange("p (k f h e) -> p k f h e", k=KT, f=2, e=HD)[:, :, fs, :, :],
                            w[:, t, :].rearrange("p (k h) -> p k h", k=KT).unsqueeze(3).to_broadcast([P, KT, 8, HD]),
                            ALU.mult)
                link(dve, dve_chain, last)
                dve.tensor_tensor(o[:, :, :], o[:, :, :], rr[:, :, :], ALU.add).then_inc(one["o"].sem, 1)

                pair2 = lambda b: PS[:, b:b + 2, :].rearrange("p b (t f) -> p (b t) f", t=2)
                dve.wait_ge(*one["y"](it, 1))
                link(dve, dve_chain, dve.tensor_tensor(rr[:, :, :], pair2(0), x[:, :, :], ALU.add))
                dve_stats(dve, rr, one["var"])
                dve.wait_ge(*one["rstd"](it, 1))
                dve_normalise(dve, xn, rr).then_inc(one["x1"].sem, 1)
                dve.wait_ge(*one["q"](it, 1))
                rope(PS[:, 0, :], PS[:, 1, :], float(HD) ** 0.5, qT)
                dve.sem_inc(att1["input"].sem, 1)
                dve_attention(dve, it, att1, 1.0)
                dve.wait_ge(*one["y2"](it, 2))
                dve.wait_ge(*one["x1b"](it, 1))
                link(dve, dve_chain, dve.tensor_tensor(rr[:, :, :], pair2(4), xb[:, :, :], ALU.add))
                dve_stats(dve, rr, one["var"])
                dve.wait_ge(*one["rstd"](it, 2))
                dve.wait_ge(*stored1(it, 0))
                dve_normalise(dve, y, rr).then_inc(one["x2"].sem, 1)
                dve.wait_ge(*one["mean"](it, 1))
                dve.tensor_copy(meanT[:, :], PS[:, 4, 0:4]).then_inc(one["meanT"].sem, 1)
                dve.wait_ge(*one["logits"](it, 1))
                link(dve, dve_chain, dve.tensor_tensor(
                    logits8[:, :, 0:EXPERTS0], PS[0:1, 5, 0:16].rearrange("p (s e) -> p s e", s=2)[:, :, 0:EXPERTS0],
                    gate0_bias[:, :].unsqueeze(1).to_broadcast([1, 2, EXPERTS0]), ALU.add))
                for s in range(2):
                    last = dve.max(top8[:, s, :], logits8[:, s, :])
                link(dve, dve_chain, last)
                dve.tensor_scalar(neg_top[:, :], top8[:, :, 0], -1.0, None, ALU.mult).then_inc(one["top"].sem, 1)
                for s in range(2):
                    last = dve.max_index(top8_index[:, s, :], top8[:, s, :], logits8[:, s, :])
                link(dve, dve_chain, last)
                dve.tensor_copy(expert_index[:, bass.ds(it * 4, 4)].rearrange("p (s e) -> p s e", s=2),
                                top8_index[:, :, 0:2])
                dve.wait_ge(*one["lexp"](it, 1))
                link(dve, dve_chain, dve.reciprocal(logit_sum[:, :], logit_sum[:, :]))
                dve.tensor_tensor(chosen_weight[:, :].rearrange("p (s e) -> p s e", s=2), logit_exp[:, :, 4:6],
                                  logit_sum[:, :].unsqueeze(2).to_broadcast([1, 2, 2]),
                                  ALU.mult).then_inc(one["chosen"].sem, 1)
                dve.wait_ge(*one["spread"](it, 1))
                dve.tensor_copy(gate_weight[:, bass.ds(it * 4, 4)], PS[:, 4, 0:4]).then_inc(one["chosen_out"].sem, 1)
                dve.wait_ge(*one["chosen_out"](it, 1))

        def pool_phase1(pool):
            pool.wait_ge(weights_loaded.sem, WEIGHTS1)
            pool.wait_ge(*consts_ready(0, 1))
            with pool.Fori(0, PAIRS) as it:
                pool_rstd(pool, it, one["var"], one["rstd"])
                pool.wait_ge(*one["x1"](it, 1))
                pool.tensor_tensor(xb[:, :, :], xn[:, :, :], wo_b[:, :].unsqueeze(1).to_broadcast([P, TILES, DIM]),
                                   ALU.add).then_inc(one["x1b"].sem, 1)
                pool_rstd(pool, it, one["var"], one["rstd"], 2)

        phase1_buffers.close()
        ctx.enter_context(phase2_buffers)
        sb2 = lambda name, shape, dt=F32: phase2_buffers.enter_context(nc.sbuf_tensor(name, shape, dt))
        hT = sb2("hT", [P, 2, FB, SEQ])
        sb2("under_stacked2", [P, STACKED - 2 * FB * SEQ])
        W_QKV, W_OUT, W_UP, W_DOWN = 2 * 768 + DIM + 4, 2 * DIM + 3 * DIM, KT * DFF + FB, FB * DIM + 3 * DIM
        w_qkv = sb2("w_qkv", [P, 2, W_QKV])
        w_out = sb2("w_out", [P, 2, W_OUT])
        w_up = sb2("w_up", [P, 2, W_UP])
        w_down = sb2("w_down", [P, 2, W_DOWN])

        in2 = signal("in2", 16)
        in2x = signal("in2x", 16)
        loaded2 = {n: signal(f"{n}_loaded", 32) for n in ("qkv", "out", "up", "down")}
        two = {n: signal(f"f_{n}", per) for n, per in (
            ("qk", 2), ("v", 1), ("xb", 1), ("y", 2), ("xp", 2),
            ("xpb", 2), ("xpturned", 2), ("xpT", 2), ("h", 8), ("h_act", 4), ("h_dve", 4), ("y2", 2),
            ("x3", 1), ("x3turned", 1), ("x3T", 1), ("normed2", 1))}
        two["var"], two["rstd"] = (one[n].after(PAIRS, 5) for n in ("var", "rstd"))
        att2 = {k: s.after(PAIRS) for k, s in att1.items()}
        stored2 = stored1.after(PAIRS)
        QK_BANK, V_BANK = (2, 5), (1, 7)
        PIECES = (("qkv", w_qkv, "f_qkv"), ("out", w_out, "f_out"), ("up", w_up, "f_up"), ("down", w_down, "f_down"))

        def sp_piece(sp, it, expert, n):
            name, dst, src = PIECES[n]
            for e in range(2):
                sp.dma_start(dst[:, e, :], d[src][bass.ds(expert[e], 1), :, :].rearrange("a p n -> p (a n)"))\
                    .then_inc(loaded2[name].sem, 16)

        def sp_experts(sp, it):
            return [sp.value_load(expert_index[0:1, bass.ds(it * 2 + e, 1)], min_val=0, max_val=EXPERTS0 - 1)
                    for e in range(2)]

        def sp_store2(sp, it):
            sp.wait_ge(*two["x3"](it, 1))
            sp.dma_start(rows(xs["x3"], it, 2), y[:, 0:2, :]).then_inc(stored2.sem, 16)
            sp.wait_ge(*two["x3T"](it, 1))
            sp.dma_start(columns(xsT["x3"], it, 2), yT[:, :, 0:SEQ]).then_inc(stored2.sem, 16)

        def sp_phase2(sp):
            sp.wait_ge(*one["chosen_out"](PAIRS - 1, 1))
            sp.dma_start(xT[:, :, 0:SEQ], columns(xsT["x2"], 0, 2)).then_inc(in2.sem, 16)
            sp.dma_start(x[:, 0:2, :], rows(xs["x2"], 0, 2)).then_inc(in2x.sem, 16)
            expert = sp_experts(sp, 0)
            for n in range(4):
                sp_piece(sp, 0, expert, n)
            with sp.Fori(0, BATCH - 1) as it:
                expert = sp_experts(sp, it + 1)
                sp.wait_ge(*two["y"](it, 1))
                sp.dma_start(xT[:, :, 0:SEQ], columns(xsT["x2"], it + 1, 2)).then_inc(in2.sem, 16)
                sp_piece(sp, it + 1, expert, 0)
                sp.wait_ge(*two["xp"](it, 2))
                sp_piece(sp, it + 1, expert, 1)
                sp.wait_ge(*two["h_act"](it, 4))
                sp.wait_ge(*two["h_dve"](it, 4))
                sp_piece(sp, it + 1, expert, 2)
                sp.wait_ge(*two["normed2"](it, 1))
                sp_piece(sp, it + 1, expert, 3)
                sp.dma_start(x[:, 0:2, :], rows(xs["x2"], it + 1, 2)).then_inc(in2x.sem, 16)
                sp_store2(sp, it)
            sp_store2(sp, BATCH - 1)
            sp.wait_ge(*stored2(BATCH - 1, 32))

        def pe_phase2(pe):
            def project(it):
                pe.wait_ge(*in2(it, 16))
                pe.wait_ge(*loaded2["qkv"](it, 32))
                for e in range(2):
                    for blk in range(4):
                        for ki in range(KT):
                            last = pe.matmul(PS[:, QK_BANK[e] + blk // 2, (blk % 2) * SEQ:(blk % 2 + 1) * SEQ],
                                      w_qkv[:, e, ki * 768 + blk * P:ki * 768 + (blk + 1) * P], xT[:, ki, 0:SEQ],
                                      start=(ki == 0), stop=(ki == 1))
                    last.then_inc(two["qk"].sem, 1)
                for e in range(2):
                    for tt in range(2):
                        for ki in range(KT):
                            last = pe.matmul(PS[:, V_BANK[e], tt * DIM:(tt + 1) * DIM], xT[:, ki, tokens(tt)],
                                             w_qkv[:, e, ki * 768 + 2 * DIM:ki * 768 + 3 * DIM],
                                             start=(ki == 0), stop=(ki == 1))
                last.then_inc(two["v"].sem, 1)

            def mix(it):
                def project_out(e):
                    if e == 0:
                        pe.wait_ge(*loaded2["out"](it, 32))
                    for t in range(2 * e, 2 * e + 2):
                        for ki in range(KT):
                            last = pe.matmul(PS[:, 4 + e, (t % 2) * DIM:(t % 2 + 1) * DIM], oT[:, ki, tokens(t)],
                                             w_out[:, e, ki * DIM:(ki + 1) * DIM], start=(ki == 0), stop=(ki == 1))
                    last.then_inc(two["y"].sem, 1)

                pe_attention(pe, it, att2, None, project_out)
                pe.wait_ge(*loaded2["up"](it, 32))
                for e in range(2):
                    pe.wait_ge(*two["xp"](it, e + 1))
                    pe_turn(pe, xn, 6 + e, 2, 2 * e).then_inc(two["xpturned"].sem, 1)
                    pe.wait_ge(*two["xpT"](it, e + 1))
                    for blk in range(FB):
                        for ki in range(KT):
                            last = pe.matmul(PS[:, 4 * e + blk // 2, (blk % 2) * SEQ:(blk % 2 + 1) * SEQ],
                                             w_up[:, e, ki * DFF + blk * P:ki * DFF + (blk + 1) * P],
                                             xnT[:, ki, e * SEQ:(e + 1) * SEQ], start=(ki == 0), stop=(ki == 1))
                        if blk % 2:
                            last.then_inc(two["h"].sem, 1)
                pe.wait_ge(*loaded2["down"](it, 32))
                for e in range(2):
                    pe.wait_ge(*two["h_act"](it, 2 * (e + 1)))
                    pe.wait_ge(*two["h_dve"](it, 2 * (e + 1)))
                    for tt in range(2):
                        for ki in range(FB):
                            last = pe.matmul(PS[:, 4 * e, tt * DIM:(tt + 1) * DIM], hT[:, e, ki, tokens(tt)],
                                             w_down[:, e, ki * DIM:(ki + 1) * DIM], start=(ki == 0), stop=(ki == FB - 1))
                    last.then_inc(two["y2"].sem, 1)

            def turn(it):
                pe.wait_ge(*two["x3"](it, 1))
                pe_turn(pe, y, 0, 2).then_inc(two["x3turned"].sem, 1)

            project(0)
            with pe.Fori(0, BATCH - 1) as it:
                mix(it)
                project(it + 1)
                turn(it)
            mix(BATCH - 1)
            turn(BATCH - 1)

        def act_phase2(act):
            def project(it):
                bias0 = 2 * 768 + DIM
                for e in range(2):
                    act.wait_ge(*two["qk"](it, e + 1))
                    for dst, n in ((qT, 0), (kT, 1)):
                        for blk in range(KT):
                            col = bias0 + 2 * n + blk
                            last = act.activation(dst[:, blk, e * SEQ:(e + 1) * SEQ],
                                                  PS[:, QK_BANK[e] + n, blk * SEQ:(blk + 1) * SEQ], ACT.Identity,
                                                  bias=w_qkv[:, e, col:col + 1])
                last.then_inc(att2["input"].sem, 1)
                act_high(act, it, att2, float(HD) ** -0.5)

            def mix(it):
                act_attention(act, it, att2)
                for b in range(0, 8, 2):
                    if b % 4 == 0:
                        e = b // 4
                        act.wait_ge(*two["xpturned"](it, e + 1))
                        act_turned(act, xnT, 6 + e, 2, 2 * e).then_inc(two["xpT"].sem, 1)
                    act.wait_ge(*two["h"](it, b + 1))
                    for j in range(2):
                        e, blk = b // 4, 2 * (b % 4) + j
                        last = act.activation(hT[:, e, blk, :], PS[:, b, j * SEQ:(j + 1) * SEQ], ACT.Relu,
                                              bias=w_up[:, e, KT * DFF + blk:KT * DFF + blk + 1])
                    last.then_inc(two["h_act"].sem, 1)

            def turned(it):
                act.wait_ge(*two["x3turned"](it, 1))
                act.wait_ge(*stored2(it, 0))
                act_turned(act, yT, 0, 2).then_inc(two["x3T"].sem, 1)

            project(0)
            with act.Fori(0, BATCH - 1) as it:
                mix(it)
                project(it + 1)
                turned(it)
            mix(BATCH - 1)
            turned(BATCH - 1)

        def dve_phase2(dve):
            with dve.Fori(0, BATCH) as it:
                restart(dve, dve_chain)

                def evacuate_values():
                    dve.wait_ge(*two["v"](it, 1))
                    for e in range(2):
                        for tt in range(2):
                            last = dve.tensor_tensor(
                                V1[:, 2 * e + tt, :, 0:HD],
                                PS[:, V_BANK[e], tt * DIM:(tt + 1) * DIM].rearrange("p (h e) -> p h e", h=HEADS),
                                w_qkv[:, e, 2 * 768:2 * 768 + DIM].rearrange("p (h e) -> p h e", h=HEADS), ALU.add)
                    last.then_inc(att2["V1"].sem, 1)

                halves = lambda ap, e: ap[:, 2 * e:2 * e + 2, :]
                row = lambda w, e, start: w[:, e, start:start + DIM].unsqueeze(1).to_broadcast([P, 2, DIM])

                def residual(e, bank):
                    link(dve, dve_chain, dve.tensor_tensor(
                        halves(rr, e), PS[:, bank, :].rearrange("p (t f) -> p t f", t=2), halves(xb, e), ALU.add))
                    dve_stats(dve, rr, two["var"], 2, 2 * e)

                def norm(e, k, w, start):
                    dve.wait_ge(*two["rstd"](it, k))
                    link(dve, dve_chain, dve_normalise(dve, xn, rr, 2, 2 * e))
                    link(dve, dve_chain, dve.tensor_tensor(halves(xn, e), halves(xn, e), row(w, e, start), ALU.mult))
                    return dve.tensor_tensor(halves(xn, e), halves(xn, e), row(w, e, start + DIM), ALU.add)

                def first_residual():
                    dve.wait_ge(*two["y"](it, 1))
                    dve.wait_ge(*two["xb"](it, 1))
                    residual(0, 4)

                dve_attention(dve, it, att2, float(HD) ** -0.5, evacuate_values, first_residual)
                norm(0, 1, w_out, 3 * DIM).then_inc(two["xp"].sem, 1)
                dve.wait_ge(*two["y"](it, 2))
                residual(1, 5)
                norm(1, 2, w_out, 3 * DIM).then_inc(two["xp"].sem, 1)
                for b in range(1, 8, 2):
                    dve.wait_ge(*two["h"](it, b + 1))
                    for j in range(2):
                        e, blk = b // 4, 2 * (b % 4) + j
                        last = dve.tensor_scalar(hT[:, e, blk, :], PS[:, b, j * SEQ:(j + 1) * SEQ],
                                                 w_up[:, e, KT * DFF + blk:KT * DFF + blk + 1], 0.0, ALU.add, ALU.max)
                    last.then_inc(two["h_dve"].sem, 1)
                for e in range(2):
                    dve.wait_ge(*two["y2"](it, e + 1))
                    dve.wait_ge(*two["xpb"](it, e + 1))
                    residual(e, 4 * e)
                    link(dve, dve_chain, norm(e, 3 + e, w_down, FB * DIM + DIM))
                flat = lambda ap: ap.rearrange("p t f -> p (t f)")
                link(dve, dve_chain, dve.scalar_tensor_tensor(
                    out=flat(halves(rr, 0)), in0=flat(halves(xn, 0)), scalar=gate_weight[:, bass.ds(it * 2, 1)],
                    in1=flat(x[:, 0:2, :]), op0=ALU.mult, op1=ALU.add))
                dve.scalar_tensor_tensor(
                    out=flat(halves(rr, 0)), in0=flat(halves(xn, 1)), scalar=gate_weight[:, bass.ds(it * 2 + 1, 1)],
                    in1=flat(halves(rr, 0)), op0=ALU.mult, op1=ALU.add).then_inc(two["normed2"].sem, 1)
                dve.wait_ge(*two["normed2"](it, 1))
                dve_stats(dve, rr, two["var"], 2)
                dve.wait_ge(*two["rstd"](it, 5))
                dve.wait_ge(*stored2(it, 0))
                dve_normalise(dve, y, rr, 2).then_inc(two["x3"].sem, 1)

        def pool_phase2(pool):
            with pool.Fori(0, BATCH) as it:
                pool.wait_ge(*in2x(it, 16))
                pool.wait_ge(*loaded2["out"](it, 32))
                for e in range(2):
                    last = pool.tensor_tensor(xb[:, 2 * e:2 * e + 2, :], x[:, 0:2, :],
                                              w_out[:, e, 2 * DIM:3 * DIM].unsqueeze(1).to_broadcast([P, 2, DIM]), ALU.add)
                last.then_inc(two["xb"].sem, 1)
                for e in range(2):
                    pool_rstd(pool, it, two["var"], two["rstd"], 1 + e, 2, 2 * e)
                pool.wait_ge(*loaded2["down"](it, 32))
                for e in range(2):
                    pool.wait_ge(*two["xp"](it, e + 1))
                    pool.tensor_tensor(xb[:, 2 * e:2 * e + 2, :], xn[:, 2 * e:2 * e + 2, :],
                                       w_down[:, e, FB * DIM:FB * DIM + DIM].unsqueeze(1).to_broadcast([P, 2, DIM]),
                                       ALU.add).then_inc(two["xpb"].sem, 1)
                for e in range(2):
                    pool_rstd(pool, it, two["var"], two["rstd"], 3 + e, 2, 2 * e)
                pool_rstd(pool, it, two["var"], two["rstd"], 5, 2)

        phase2_buffers.close()
        attention_shared.close()
        phase3_buffers = ExitStack()
        ctx.enter_context(phase3_buffers)
        sb3 = lambda name, shape, dt=F32: phase3_buffers.enter_context(nc.sbuf_tensor(name, shape, dt))
        NH, DH = 4, 64
        SLOT_HEADS = (0, 2, 1, 3)
        GROUPS = 4
        c = sb3("c", [P, TILES, DIM])
        head_rows = sb3("head_rows", [2 * NH, NH, P])
        head_rows_r = sb3("head_rows_r", [2 * NH, NH, P], F32R)
        aw = sb3("aw", [P, KT, 3 * DIM])
        mgate = sb3("mgate", [P, 3 * KT, 2 * NH])
        mgate_bias = sb3("mgate_bias", [P, 2 * NH])
        outnorm = sb3("outnorm", [P, DIM])
        gate1 = sb3("gate1", [P, KT, EXPERTS1])
        gate1_bias = sb3("gate1_bias", [P, EXPERTS1])
        av = sb3("av", [P, TILES, DIM])
        aprob = sb3("aprob", [P, TILES, SEQ])
        aprobT = sb3("aprobT", [P, 2, 3 * P])
        neg_max3 = sb3("neg_max3", [P, TILES])
        row_sum = sb3("row_sum", [P, TILES])
        gates = sb3("gates", [P, TILES, 2 * NH])
        abs_f = sb3("abs_f", [P, TILES, NH])
        min_f = sb3("min_f", [P, TILES, NH])
        log_f = sb3("log_f", [P, TILES, NH])
        cum = sb3("cum", [P, TILES, NH])
        source = sb3("source", [P, TILES, NH])
        source_split = sb3("source_split", [P, TILES, 2 * NH], F32R)
        sourceT = sb3("sourceT", [2 * NH, TOK], F32R)
        neg_run = sb3("neg_run", [P, TILES, NH])
        Dm = sb3("Dm", [P, 2, NH, SEQ])
        Cm = sb3("Cm", [P, 2, NH, SEQ])
        CT = sb3("CT", [P, 2, NH, SEQ])
        row_C = sb3("row_C", [P, TILES, NH])
        floor = sb3("floor", [P, TILES, NH])
        hm = sb3("hm", [P, TILES, DIM])
        hsq = sb3("hsq", [P, TILES, DIM])
        hmean = sb3("hmean", [P, TILES * NH])
        hvar = sb3("hvar", [P, TILES * NH])
        score = sb3("score", [P, TILES, EXPERTS1])
        choice = sb3("choice", [P, TILES, EXPERTS1])
        group8 = sb3("group8", [P, TILES, GROUPS, 8])
        group10 = sb3("group10", [P, TILES, 10])
        group_top = sb3("group_top", [P, TILES, 8])
        group_want = sb3("group_want", [P, TILES, 8])
        group_hit = sb3("group_hit", [P, TILES, 10])
        expert_top = sb3("expert_top", [P, TILES, 8])
        route = sb3("route", [P, TILES, ALL_EXPERTS])
        route_sum = sb3("route_sum", [P, TILES])

        W3 = [(head_rows, "head_rows"), (aw, "aw"), (mgate, "mgate"), (mgate_bias, "mgate_bias"), (outnorm, "outnorm"), (gate1, "gate1"),
              (gate1_bias, "gate1_bias")]
        in3 = in1.after(PAIRS, 64)
        three = {n: signal(f"l1_{n}", per) for n, per in (
            ("qkv", 1), ("k", 1), ("v", 1), ("scores", 4), ("max", 4), ("exp", 4), ("turned", 2), ("probT", 2),
            ("out", 1), ("x4", 1), ("x4turned", 1), ("x4T", 1),
            ("gates", 1), ("abs", 1), ("fexp", 1), ("flog", 1), ("logf", 1), ("cum", 1), ("source", 1),
            ("sourceturned", 1), ("sourceT", 1), ("ab", 4), ("run", 4), ("D", 4), ("C", 4), ("Cturned", 4), ("CT", 4),
            ("h", 4), ("hout", 4), ("floor", 2), ("fl", 2), ("hc", 2), ("hsq", 2), ("hvar", 2), ("hrstd", 2),
            ("x5", 2), ("x5turned", 1), ("x5T", 1), ("logits", 1), ("lexp", 1), ("route", 1))}
        three["var"], three["rstd"] = (two[n].after(BATCH, 3) for n in ("var", "rstd"))
        stored3 = stored2.after(BATCH, 48)

        def sp_load3(sp, it):
            sp.dma_start(xT[:, :, :], columns(xsT["x3"], it, TILES)).then_inc(in3.sem, 16)
            sp.dma_start(x[:, :, :], rows(xs["x3"], it, TILES)).then_inc(in3.sem, 16)
            sp.dma_start(cT[:, :, :], columns(d["ctxT"], it, TILES)).then_inc(in3.sem, 16)
            sp.dma_start(c[:, :, :], rows(d["ctx"], it, TILES)).then_inc(in3.sem, 16)

        def sp_store3(sp, it):
            sp.wait_ge(*three["x5"](it, 2))
            sp.dma_start(rows(xs["x5"], it, TILES), y[:, :, :]).then_inc(stored3.sem, 16)
            sp.wait_ge(*three["x5T"](it, 1))
            sp.dma_start(columns(xsT["x5"], it, TILES), yT[:, :, :]).then_inc(stored3.sem, 16)
            sp.wait_ge(*three["route"](it, 1))
            sp.dma_start(rows(route_dram, it, TILES), route[:, :, :]).then_inc(stored3.sem, 16)

        def sp_phase3(sp):
            for dst, name in W3:
                sp.dma_start(dst[tuple(slice(None) for _ in dst.shape)], d[name]).then_inc(weights_loaded.sem, 16)
            sp_load3(sp, 0)
            with sp.Fori(0, PAIRS - 1) as it:
                sp.wait_ge(*three["h"](it, 4))
                sp_load3(sp, it + 1)
                sp_store3(sp, it)
            sp_store3(sp, PAIRS - 1)
            sp.wait_ge(*stored3(PAIRS - 1, 48))

        def width(t):
            return (t % 2 + 1) * P

        def pe_phase3(pe):
            pe.wait_ge(weights_loaded.sem, WEIGHTS1 + 16 * len(W3))
            pe.wait_ge(*consts_ready(0, 2))
            with pe.Fori(0, PAIRS) as it:
                pe.wait_ge(*in3(it, 64))
                for blk in range(4):
                    for ki in range(KT):
                        pe.matmul(PS[:, blk, :], aw[:, ki, blk * P:(blk + 1) * P], xT[:, ki, :],
                                  start=(ki == 0), stop=(ki == 1))
                for t in range(TILES):
                    for ki in range(KT):
                        last = pe.matmul(PS[:, 4 + t // 2, (t % 2) * DIM:(t % 2 + 1) * DIM], xT[:, ki, tokens(t)],
                                         aw[:, ki, 2 * DIM:3 * DIM], start=(ki == 0), stop=(ki == 1))
                last.then_inc(three["qkv"].sem, 1)
                pe.wait_ge(*three["k"](it, 1))
                for t in range(TILES):
                    s, w = t // 2, width(t)
                    pe.matmul(PS[:, t, 0:w], identity16[:, :], causal_mask[:, t % 2, 0:w], start=True, stop=False)
                    for ki in range(KT):
                        last = pe.matmul(PS[:, t, 0:w], qT[:, ki, tokens(t)], kT[:, ki, s * SEQ:s * SEQ + w],
                                         start=False, stop=(ki == 1))
                    last.then_inc(three["scores"].sem, 1)
                pe.wait_ge(*three["v"](it, 1))
                for s in range(2):
                    pe.wait_ge(*three["exp"](it, 2 * s + 2))
                    for slot, (qt, kt) in enumerate(((0, 0), (1, 0), (1, 1))):
                        last = pe.transpose(PS[:, 4 + s, slot * P:(slot + 1) * P],
                                            aprob[:, 2 * s + qt, kt * P:(kt + 1) * P], identity[:, :])
                    last.then_inc(three["turned"].sem, 1)
                for s in range(2):
                    pe.wait_ge(*three["probT"](it, s + 1))
                    for slot, (qt, kt) in enumerate(((0, 0), (1, 0), (1, 1))):
                        last = pe.matmul(PS[:, 6 + s, qt * DIM:(qt + 1) * DIM], aprobT[:, s, slot * P:(slot + 1) * P],
                                         av[:, 2 * s + kt, :], start=(kt == 0), stop=(kt == qt))
                last.then_inc(three["out"].sem, 1)
                def gates(first, blocks):
                    for t in range(TILES):
                        for blk in blocks:
                            lhs = (xnT if blk < KT else cT)[:, blk % KT, tokens(t)]
                            last = pe.matmul(PS[:, 2, first + t * 2 * NH:first + (t + 1) * 2 * NH], lhs, mgate[:, blk, :],
                                             start=(blk == blocks[0]), stop=(blk == blocks[-1]))
                    return last

                gates(TILES * 2 * NH, range(KT, 3 * KT))
                pe.wait_ge(*three["x4"](it, 1))
                pe_turn(pe, xn, 0).then_inc(three["x4turned"].sem, 1)
                pe.wait_ge(*three["x4T"](it, 1))
                gates(0, range(KT)).then_inc(three["gates"].sem, 1)
                pe.wait_ge(*three["logf"](it, 1))
                for s in range(2):
                    pe.matmul(PS[:, 3, 2 * s * NH:(2 * s + 1) * NH], upto[:, :], log_f[:, 2 * s, :],
                              start=True, stop=True)
                    pe.matmul(PS[:, 3, (2 * s + 1) * NH:(2 * s + 2) * NH], ones[:, :], log_f[:, 2 * s, :],
                              start=True, stop=False)
                    last = pe.matmul(PS[:, 3, (2 * s + 1) * NH:(2 * s + 2) * NH], upto[:, :], log_f[:, 2 * s + 1, :],
                                     start=False, stop=True)
                last.then_inc(three["cum"].sem, 1)
                pe.wait_ge(*three["source"](it, 1))
                for t in range(TILES):
                    last = pe.transpose(PS[0:2 * NH, 4, tokens(t)], source_split[:, t, :].bitcast(F32), identity[:, :])
                last.then_inc(three["sourceturned"].sem, 1)
                pe.wait_ge(*three["sourceT"](it, 1))
                def mix_scores(t):
                    s, w, base = t // 2, width(t), 4 * (t % 2)
                    if t >= 2:
                        pe.wait_ge(*three["hout"](it, t - 1))
                    for slot, h in enumerate(SLOT_HEADS):
                        bank, col = base + slot // 2, (slot % 2) * SEQ
                        pe.matmul(PS[:, bank, col:col + w], identity16[:, :], causal_mask[:, t % 2, 0:w],
                                  start=True, stop=False)
                        pe.matmul(PS[:, bank, col:col + w], head_rows_r[:, h, :], sourceT[:, s * SEQ:s * SEQ + w],
                                  start=False, stop=True)
                    for slot, h in enumerate(SLOT_HEADS):
                        bank, col, r = base + 2 + slot // 2, (slot % 2) * SEQ, DH * (h % 2)
                        last = pe.matmul(PS[:, bank, col:col + w], xnT[r:r + DH, h // 2, tokens(t)],
                                         cT[r:r + DH, h // 2, s * SEQ:s * SEQ + w], start=True, stop=True)
                    last.then_inc(three["ab"].sem, 1)

                def mix_values(t):
                    s, base = t // 2, 4 * (t % 2)
                    pe.wait_ge(*three["C"](it, t + 1))
                    for slot in range(NH):
                        for kt in range(t % 2 + 1):
                            col = (slot % 2) * SEQ + kt * P
                            last = pe.transpose(PS[:, base + slot // 2, col:col + P],
                                                Cm[:, t % 2, slot, kt * P:(kt + 1) * P], identity[:, :])
                    last.then_inc(three["Cturned"].sem, 1)
                    pe.wait_ge(*three["CT"](it, t + 1))
                    for slot, h in enumerate(SLOT_HEADS):
                        for kt in range(t % 2 + 1):
                            last = pe.matmul(PS[:, base + 2, h * DH:(h + 1) * DH], CT[:, t % 2, slot, kt * P:(kt + 1) * P],
                                             c[:, 2 * s + kt, h * DH:(h + 1) * DH], start=(kt == 0), stop=(kt == t % 2))
                    last.then_inc(three["h"].sem, 1)

                mix_scores(0)
                for t in range(TILES):
                    if t + 1 < TILES:
                        mix_scores(t + 1)
                    mix_values(t)
                pe.wait_ge(*three["x5"](it, 1))
                pe_turn(pe, y, 0, 2, 0)
                pe.wait_ge(*three["x5"](it, 2))
                pe_turn(pe, y, 1, 2, 2).then_inc(three["x5turned"].sem, 1)
                pe.wait_ge(*three["x5T"](it, 1))
                for t in range(TILES):
                    for ki in range(KT):
                        last = pe.matmul(PS[:, 4, t * EXPERTS1:(t + 1) * EXPERTS1], yT[:, ki, tokens(t)],
                                         gate1[:, ki, :], start=(ki == 0), stop=(ki == 1))
                last.then_inc(three["logits"].sem, 1)
                pe.wait_ge(*three["lexp"](it, 1))

        def act_phase3(act):
            with act.Fori(0, PAIRS) as it:
                act.wait_ge(*three["qkv"](it, 1))
                act.activation(qT[:, :, :], PS[:, 0:2, :], ACT.Copy, scale=float(DIM) ** -0.5)
                act.activation(kT[:, :, :], PS[:, 2:4, :], ACT.Copy).then_inc(three["k"].sem, 1)
                for t in range(TILES):
                    act.wait_ge(*three["max"](it, t + 1))
                    act.activation(aprob[:, t, 0:width(t)], PS[:, t, 0:width(t)], ACT.Exp, bias=neg_max3[:, t:t + 1],
                                   accum_out=row_sum[:, t:t + 1]).then_inc(three["exp"].sem, 1)
                for s in range(2):
                    act.wait_ge(*three["turned"](it, s + 1))
                    act.activation(aprobT[:, s, :], PS[:, 4 + s, 0:3 * P], ACT.Copy).then_inc(three["probT"].sem, 1)
                act.wait_ge(*three["x4turned"](it, 1))
                act_turned(act, xnT, 0).then_inc(three["x4T"].sem, 1)
                act.wait_ge(*three["abs"](it, 1))
                act.activation(abs_f[:, :, :], abs_f[:, :, :], ACT.Exp, scale=-1.0).then_inc(three["fexp"].sem, 1)
                act.wait_ge(*three["fexp"](it, 1))
                act.activation(abs_f[:, :, :], abs_f[:, :, :], ACT.Ln, bias=1.0).then_inc(three["flog"].sem, 1)
                act.wait_ge(*three["sourceturned"](it, 1))
                act.activation(sourceT[:, :], PS[0:2 * NH, 4, :], ACT.Copy).then_inc(three["sourceT"].sem, 1)

                def mix_exp(t):
                    act.wait_ge(*three["run"](it, t + 1))
                    if t >= 2:
                        act.wait_ge(*three["C"](it, t - 1))
                    for slot, h in enumerate(SLOT_HEADS):
                        src = PS[:, 4 * (t % 2) + slot // 2, (slot % 2) * SEQ:(slot % 2) * SEQ + width(t)]
                        last = act.activation(Dm[:, t % 2, slot, 0:width(t)], src, ACT.Exp, bias=neg_run[:, t, h:h + 1])
                    last.then_inc(three["D"].sem, 1)

                def finish(s):
                    pair = slice(2 * s, 2 * s + 2)
                    act.wait_ge(*three["floor"](it, s + 1))
                    act.activation(floor[:, pair, :], floor[:, pair, :], ACT.Exp).then_inc(three["fl"].sem, 1)
                    act.wait_ge(*three["hc"](it, s + 1))
                    act.activation(hsq[:, pair, :], hm[:, pair, :], ACT.Square).then_inc(three["hsq"].sem, 1)

                mix_exp(0)
                for t in range(TILES):
                    if t + 1 < TILES:
                        mix_exp(t + 1)
                    act.wait_ge(*three["Cturned"](it, t + 1))
                    base = 4 * (t % 2)
                    act.activation(CT[:, t % 2, :, 0:width(t)],
                                   PS[:, base:base + 2, :].rearrange("p b (h k) -> p (b h) k", h=2)[:, :, 0:width(t)],
                                   ACT.Copy).then_inc(three["CT"].sem, 1)
                    if t == 1:
                        finish(0)
                finish(1)
                act.wait_ge(*three["x5turned"](it, 1))
                act.wait_ge(*stored3(it, 0))
                act_turned(act, yT, 0).then_inc(three["x5T"].sem, 1)
                act.wait_ge(*three["logits"](it, 1))
                act.activation(score[:, :, :], PS[:, 4, 0:TILES * EXPERTS1].rearrange("p (t e) -> p t e", t=TILES),
                               ACT.Exp, scale=-1.0).then_inc(three["lexp"].sem, 1)

        def dve_phase3(dve):
            dve.wait_ge(weights_loaded.sem, WEIGHTS1 + 16 * len(W3))
            restart(dve, dve_chain)
            dve.tensor_copy(head_rows_r[:, :, :], head_rows[:, :, :]).then_inc(consts_ready.sem, 1)
            dve.memset(group10[:, :, :], FAR)
            dve.memset(group_want[:, :, :], FAR)
            link(dve, dve_chain, dve.memset(route[:, :, EXPERTS1:ALL_EXPERTS], 1.0))
            with dve.Fori(0, PAIRS) as it:
                restart(dve, dve_chain)

                def chained(ins):
                    link(dve, dve_chain, ins)

                dve.wait_ge(*three["qkv"](it, 1))
                dve.tensor_copy(av[:, :, :], PS[:, 4:6, :].rearrange("p b (t f) -> p (b t) f", t=2))\
                    .then_inc(three["v"].sem, 1)
                for t in range(TILES):
                    dve.wait_ge(*three["scores"](it, t + 1))
                    dve.tensor_reduce(neg_max3[:, t:t + 1], PS[:, t, 0:width(t)], AX.X, ALU.max, negate=True)\
                        .then_inc(three["max"].sem, 1)
                dve.wait_ge(*three["exp"](it, 4))
                chained(dve.reciprocal(row_sum[:, :], row_sum[:, :]))
                dve.wait_ge(*three["out"](it, 1))
                for t in range(TILES):
                    last = dve.scalar_tensor_tensor(out=rr[:, t, :], in0=PS[:, 6 + t // 2, (t % 2) * DIM:(t % 2 + 1) * DIM],
                                                    scalar=row_sum[:, t:t + 1], in1=x[:, t, :],
                                                    op0=ALU.mult, op1=ALU.add)
                chained(last)
                dve_stats(dve, rr, three["var"])
                dve.wait_ge(*three["rstd"](it, 1))
                dve_normalise(dve, xn, rr).then_inc(three["x4"].sem, 1)
                dve.wait_ge(*three["gates"](it, 1))
                chained(dve.tensor_tensor(gates[:, :, :], PS[:, 2, 0:TILES * 2 * NH].rearrange("p (t g) -> p t g", t=TILES),
                                          mgate_bias[:, :].unsqueeze(1).to_broadcast([P, TILES, 2 * NH]), ALU.add))
                chained(dve.tensor_tensor(gates[:, :, :], PS[:, 2, TILES * 2 * NH:2 * TILES * 2 * NH]
                                          .rearrange("p (t g) -> p t g", t=TILES), gates[:, :, :], ALU.add))
                forget = gates[:, :, NH:2 * NH]
                dve.scalar_tensor_tensor(out=abs_f[:, :, :], in0=forget, scalar=-1.0, in1=forget,
                                         op0=ALU.mult, op1=ALU.max).then_inc(three["abs"].sem, 1)
                chained(dve.tensor_scalar(min_f[:, :, :], forget, 0.0, None, ALU.min))
                dve.wait_ge(*three["flog"](it, 1))
                dve.tensor_tensor(log_f[:, :, :], min_f[:, :, :], abs_f[:, :, :], ALU.subtract)\
                    .then_inc(three["logf"].sem, 1)
                dve.wait_ge(*three["cum"](it, 1))
                chained(dve.tensor_copy(cum[:, :, :], PS[:, 3, 0:TILES * NH].rearrange("p (t g) -> p t g", t=TILES)))
                chained(dve.tensor_tensor(source[:, :, :], gates[:, :, 0:NH], cum[:, :, :], ALU.subtract))
                chained(dve.tensor_copy(source_split[:, :, 0:NH], source[:, :, :]))
                dve.tensor_tensor(source_split[:, :, NH:], source[:, :, :], source_split[:, :, 0:NH].bitcast(F32),
                                  ALU.subtract).then_inc(three["source"].sem, 1)

                by_slot = lambda ap: ap.rearrange("p (b h) -> p h b", h=2)

                def mix_max(t):
                    dve.wait_ge(*three["ab"](it, t + 1))
                    base = 4 * (t % 2)
                    src = PS[:, base:base + 2, :].rearrange("p b (h k) -> p b h k", h=2)[:, :, :, 0:width(t)]
                    dve.tensor_reduce(by_slot(neg_run[:, t, :]), src, AX.X, ALU.max, negate=True).then_inc(three["run"].sem, 1)

                def mix_c(t):
                    dve.wait_ge(*three["D"](it, t + 1))
                    if t >= 2:
                        dve.wait_ge(*three["Cturned"](it, t - 1))
                    base = 4 * (t % 2) + 2
                    src = PS[:, base:base + 2, :].rearrange("p b (h k) -> p (b h) k", h=2)[:, :, 0:width(t)]
                    dst = Cm[:, t % 2, :, 0:width(t)]
                    dve.scalar_tensor_tensor(out=dst, in0=src, scalar=float(DH) ** -0.5, in1=Dm[:, t % 2, :, 0:width(t)],
                                             op0=ALU.mult, op1=ALU.mult).then_inc(three["C"].sem, 1)
                    dve.wait_ge(*three["C"](it, t + 1))
                    chained(dve.tensor_reduce(by_slot(row_C[:, t, :]), dst.rearrange("p (b h) k -> p b h k", b=2),
                                              AX.X, ALU.add))

                by_head = lambda ap, s: ap[:, 2 * s:2 * s + 2, :].rearrange("p t (h e) -> p (t h) e", h=NH)
                spread = lambda ap: ap.unsqueeze(2).to_broadcast([P, 2 * NH, DH])

                def normaliser(s):
                    pair = slice(2 * s, 2 * s + 2)
                    flat = lambda ap: ap.rearrange("p t h -> p (t h)")
                    row, low_limit = row_C[:, pair, :], floor[:, pair, :]
                    dve.tensor_tensor(low_limit, neg_run[:, pair, :], cum[:, pair, :], ALU.subtract)\
                        .then_inc(three["floor"].sem, 1)
                    chained(dve.scalar_tensor_tensor(out=flat(row), in0=flat(row), scalar=-1.0,
                                                     in1=flat(row), op0=ALU.mult, op1=ALU.max))
                    dve.wait_ge(*three["fl"](it, s + 1))
                    chained(dve.tensor_tensor(row, row, low_limit, ALU.max))
                    chained(dve.tensor_scalar(row, row, 1e-6, None, ALU.add))
                    chained(dve.reciprocal(row, row))
                    per_head = by_head(hm, s)
                    mean = hmean[:, 2 * s * NH:(2 * s + 2) * NH]
                    dve.wait_ge(*three["hout"](it, 2 * s + 2))
                    chained(dve.tensor_tensor(per_head, per_head, spread(flat(row)), ALU.mult))
                    chained(dve.tensor_reduce(mean, per_head, AX.X, ALU.add))
                    chained(dve.tensor_scalar(mean, mean, 1.0 / DH, None, ALU.mult))
                    dve.tensor_tensor(per_head, per_head, spread(mean), ALU.subtract).then_inc(three["hc"].sem, 1)

                def finish(s):
                    pair = slice(2 * s, 2 * s + 2)
                    per_head = by_head(hm, s)
                    var = hvar[:, 2 * s * NH:(2 * s + 2) * NH]
                    dve.wait_ge(*three["hsq"](it, s + 1))
                    chained(dve.tensor_reduce(var, by_head(hsq, s), AX.X, ALU.add))
                    dve.tensor_scalar(var, var, 1.0 / DH, 1e-5, ALU.mult, ALU.add).then_inc(three["hvar"].sem, 1)
                    dve.wait_ge(*three["hrstd"](it, s + 1))
                    chained(dve.tensor_tensor(per_head, per_head, spread(var), ALU.mult))
                    chained(dve.tensor_tensor(hm[:, pair, :], hm[:, pair, :],
                                              outnorm[:, :].unsqueeze(1).to_broadcast([P, 2, DIM]), ALU.mult))
                    chained(dve.tensor_tensor(rr[:, pair, :], hm[:, pair, :], xn[:, pair, :], ALU.add))
                    dve_stats(dve, rr, three["var"], 2, 2 * s)
                    dve.wait_ge(*three["rstd"](it, s + 2))
                    if s == 0:
                        dve.wait_ge(*stored3(it, 0))
                    dve_normalise(dve, y, rr, 2, 2 * s).then_inc(three["x5"].sem, 1)

                mix_max(0)
                mix_c(0)
                for t in range(TILES):
                    if t + 1 < TILES:
                        mix_max(t + 1)
                        mix_c(t + 1)
                    if t == 2:
                        finish(0)
                    dve.wait_ge(*three["h"](it, t + 1))
                    dve.tensor_copy(hm[:, t, :], PS[:, 4 * (t % 2) + 2, 0:DIM]).then_inc(three["hout"].sem, 1)
                    if t == 1:
                        normaliser(0)
                normaliser(1)
                finish(1)
                dve.wait_ge(*three["lexp"](it, 1))
                chained(dve.tensor_scalar(score[:, :, :], score[:, :, :], 1.0, None, ALU.add))
                chained(dve.reciprocal(score[:, :, :], score[:, :, :]))
                chained(dve.tensor_tensor(choice[:, :, :], score[:, :, :],
                                          gate1_bias[:, :].unsqueeze(1).to_broadcast([P, TILES, EXPERTS1]), ALU.add))
                for t in range(TILES):
                    for g in range(GROUPS):
                        last = dve.max(group8[:, t, g, :], choice[:, t, 8 * g:8 * g + 8])
                chained(last)
                chained(dve.tensor_tensor(group10[:, :, 0:GROUPS], group8[:, :, :, 0], group8[:, :, :, 1], ALU.add))
                for t in range(TILES):
                    last = dve.max(group_top[:, t, :], group10[:, t, :])
                chained(last)
                chained(dve.tensor_copy(group_want[:, :, 0:2], group_top[:, :, 0:2]))
                for t in range(TILES):
                    last = dve.match_replace(group_hit[:, t, :], group_want[:, t, :], group10[:, t, :], -FAR)
                chained(last)
                chained(dve.tensor_scalar(group_hit[:, :, :], group_hit[:, :, :], 1e38, None, ALU.is_ge))
                by_group = lambda ap: ap.rearrange("p t (g e) -> p t g e", g=GROUPS)
                chained(dve.tensor_tensor(by_group(choice[:, :, :]), by_group(choice[:, :, :]),
                                          group_hit[:, :, 0:GROUPS].unsqueeze(3).to_broadcast([P, TILES, GROUPS, 8]),
                                          ALU.mult))
                chained(dve.tensor_scalar(choice[:, :, :], choice[:, :, :], 0.0, None, ALU.add))
                for t in range(TILES):
                    last = dve.max(expert_top[:, t, :], choice[:, t, :])
                chained(last)
                for t in range(TILES):
                    last = dve.match_replace(choice[:, t, :], expert_top[:, t, :], choice[:, t, :], -FAR)
                chained(last)
                chained(dve.tensor_scalar(choice[:, :, :], choice[:, :, :], 1e38, None, ALU.is_ge))
                chained(dve.tensor_tensor(score[:, :, :], score[:, :, :], choice[:, :, :], ALU.mult))
                chained(dve.tensor_reduce(route_sum[:, :], score[:, :, :], AX.X, ALU.add))
                chained(dve.tensor_scalar(route_sum[:, :], route_sum[:, :], 1e-20, None, ALU.add))
                chained(dve.reciprocal(route_sum[:, :], route_sum[:, :]))
                chained(dve.tensor_scalar(route_sum[:, :], route_sum[:, :], 2.5, None, ALU.mult))
                dve.tensor_tensor(route[:, :, 0:EXPERTS1], score[:, :, :],
                                  route_sum[:, :].unsqueeze(2).to_broadcast([P, TILES, EXPERTS1]), ALU.mult)\
                    .then_inc(three["route"].sem, 1)
                dve.wait_ge(*three["route"](it, 1))

        def pool_phase3(pool):
            with pool.Fori(0, PAIRS) as it:
                pool_rstd(pool, it, three["var"], three["rstd"], 1)
                for s in range(2):
                    pool.wait_ge(*three["hvar"](it, s + 1))
                    var = hvar[:, 2 * s * NH:(2 * s + 2) * NH]
                    pool.tensor_tensor(var, var, minus_half[:, 0:2 * NH], ALU.pow).then_inc(three["hrstd"].sem, 1)
                    pool_rstd(pool, it, three["var"], three["rstd"], s + 2, 2, 2 * s)

        phase3_buffers.close()
        sb4 = lambda name, shape, dt=F32: ctx.enter_context(nc.sbuf_tensor(name, shape, dt))
        NT = BATCH * SEQ // P
        NG = NT // TILES
        W_EXPERT = 2 * KT * INNER + DIM
        SLOTS = 4
        x_high, x_low = (sb4(n, [P, KT, NT * P], F32R) for n in ("x_high", "x_low"))
        acc = sb4("acc", [P, NT, DIM])
        route4 = sb4("route4", [P, NT, ALL_EXPERTS])
        w_expert = sb4("w_expert", [P, 2, W_EXPERT])
        w_high, w_low = (sb4(n, [P, 2, W_EXPERT], F32R) for n in ("w_high", "w_low"))
        silu_g = sb4("silu_g", [P, 2, TOK])
        hidden_t = sb4("hidden_t", [P, 2, TOK])
        h_high, h_low = (sb4(n, [P, SLOTS, TOK], F32R) for n in ("h_high", "h_low"))

        in4 = in3.after(PAIRS, 16)
        group_loaded = [signal(f"group_loaded{j}", 32) for j in range(2)]
        expert_loaded = [signal(f"expert_loaded{j}", 16) for j in range(2)]
        x_split = {n: signal(f"x_{n}", 1) for n in ("high", "low")}
        w_split = {n: signal(f"w_{n}", 2) for n in ("high", "low")}
        STEPS = 2 * NG
        ITERATIONS = ALL_EXPERTS // 2
        BEHIND = 2
        four = {n: signal(f"e_{n}", STEPS, base) for n, base in
                (("gu", 0), ("silu", 0), ("hidden", 2), ("high", 0), ("low", 0), ("down", 0), ("added", 2))}
        four_ln = {n: three[n].after(PAIRS, 1) for n in ("var", "rstd")}
        four_ln["out"] = signal("z_out", 1)
        stored4 = stored3.after(PAIRS, 16)
        group_slot = (xT, cT)

        def expert_loop(eng, body):
            body(0, True, False)
            with eng.Fori(1, ITERATIONS - 1) as it:
                body(it, False, False)
            body(ITERATIONS - 1, False, True)

        def sp_phase4(sp):
            sp.wait_ge(*three["route"](PAIRS - 1, 1))
            load = lambda e, j: sp.dma_start(
                w_expert[:, j, :], d["experts"][bass.ds(e, 1), :, :].rearrange("a p n -> p (a n)"))\
                .then_inc(expert_loaded[j].sem, 16)
            load(0, 0)
            for g in range(NG):
                if g >= 2:
                    sp.wait_ge(*x_split["low"](0, g - 1))
                sp.dma_start(group_slot[g % 2][:, :, :], columns(xsT["x5"], g, TILES))\
                    .then_inc(group_loaded[g % 2].sem, 16)
                sp.dma_start(acc[:, g * TILES:(g + 1) * TILES, :], rows(xs["x5"], g, TILES))\
                    .then_inc(group_loaded[g % 2].sem, 16)
                if g == 0:
                    sp.dma_start(route4[:, :, :], route_dram.rearrange("(t p) e -> p t e", p=P)).then_inc(in4.sem, 16)
                    load(1, 1)
            with sp.Fori(0, ITERATIONS - 1) as it:
                for j in range(2):
                    sp.wait_ge(*w_split["high"](it, j + 1))
                    sp.wait_ge(*w_split["low"](it, j + 1))
                    load((it + 1) * 2 + j, j)
            with sp.Fori(0, NG) as g:
                sp.wait_ge(*four_ln["out"](g, 1))
                sp.dma_start(rows(out, g, TILES), y[:, :, :]).then_inc(stored4.sem, 16)
            sp.wait_ge(*stored4(NG - 1, 16))

        def pe_phase4(pe):
            def body(it, first, final):
                def up(n):
                    j, g = n // NG, n % NG
                    if first and n < NG:
                        pe.wait_ge(*x_split["low"](0, n + 1))
                    if g == 0:
                        pe.wait_ge(*w_split["high"](it, j + 1))
                        pe.wait_ge(*w_split["low"](it, j + 1))
                    pe.wait_ge(*four["hidden"](it, n - 1))
                    for m in range(2):
                        for ki in range(KT):
                            col = (ki * 2 + m) * INNER
                            for k, (w, x_half) in enumerate(((w_high, x_high), (w_high, x_low), (w_low, x_high))):
                                last = pe.matmul(PS[:, 2 * (n % 2) + m, :], w[:, j, col:col + INNER],
                                                 x_half[:, ki, g * TOK:(g + 1) * TOK],
                                                 start=(ki == 0 and k == 0), stop=(ki == 1 and k == 2))
                    last.then_inc(four["gu"].sem, 1)

                def down(n):
                    j = n % STEPS // NG
                    pe.wait_ge(*four["low"](it, n + 1))
                    pe.wait_ge(*four["added"](it, n - 1))
                    for t in range(TILES):
                        for k, (h_half, w) in enumerate(((h_high, w_high), (h_high, w_low), (h_low, w_high))):
                            last = pe.matmul(PS[:, 4 + 2 * (n % 2) + t // 2, (t % 2) * DIM:(t % 2 + 1) * DIM],
                                             h_half[:, n % SLOTS, tokens(t)], w[:, j, 2 * KT * INNER:],
                                             start=(k == 0), stop=(k == 2))
                    last.then_inc(four["down"].sem, 1)

                for n in range(STEPS):
                    up(n)
                    if n >= BEHIND or not first:
                        down(n - BEHIND)
                if final:
                    for n in range(STEPS - BEHIND, STEPS):
                        down(n)

            expert_loop(pe, body)

        def split_expert_at(n):
            return {3: (0, 1), NG + 3: (1, 0)}.get(n)

        def act_phase4(act):
            def group_high(g):
                act.wait_ge(*group_loaded[g % 2](g // 2, 32))
                act.activation(x_high[:, :, g * TOK:(g + 1) * TOK], group_slot[g % 2][:, :, :], ACT.Copy)\
                    .then_inc(x_split["high"].sem, 1)

            def expert_high(it, j):
                act.wait_ge(*expert_loaded[j](it, 16))
                act.activation(w_high[:, j, :], w_expert[:, j, :], ACT.Copy).then_inc(w_split["high"].sem, 1)

            def body(it, first, final):
                for n in range(STEPS):
                    if first and n + 2 < NG:
                        group_high(n + 2)
                    act.wait_ge(*four["gu"](it, n + 1))
                    act.wait_ge(*four["hidden"](it, n - 1))
                    act.activation(silu_g[:, n % 2, :], PS[:, 2 * (n % 2), :], ACT.Silu).then_inc(four["silu"].sem, 1)
                    act.wait_ge(*four["hidden"](it, n + 1))
                    act.activation(h_high[:, n % SLOTS, :], hidden_t[:, n % 2, :], ACT.Copy).then_inc(four["high"].sem, 1)
                    want = split_expert_at(n)
                    if want and not (final and want[0]):
                        act.wait_ge(*four["down"](it, NG * want[0] + 1 - want[0]))
                        expert_high(it + want[0], want[1])

            expert_high(0, 0)
            group_high(0)
            group_high(1)
            expert_loop(act, body)

        def dve_phase4(dve):
            def group_low(g):
                dve.wait_ge(*x_split["high"](0, g + 1))
                dve.tensor_tensor(x_low[:, :, g * TOK:(g + 1) * TOK], group_slot[g % 2][:, :, :],
                                  x_high[:, :, g * TOK:(g + 1) * TOK].bitcast(F32), ALU.subtract)\
                    .then_inc(x_split["low"].sem, 1)

            def body(it, first, final):
                def hidden(n):
                    dve.wait_ge(*four["silu"](it, n + 1))
                    if n >= SLOTS or not first:
                        dve.wait_ge(*four["down"](it, n - SLOTS + 1))
                    if n >= 2 or not first:
                        dve.wait_ge(*four["low"](it, n - 1))
                    dve.tensor_tensor(hidden_t[:, n % 2, :], silu_g[:, n % 2, :], PS[:, 2 * (n % 2) + 1, :], ALU.mult)\
                        .then_inc(four["hidden"].sem, 1)

                def add(n):
                    j, g = n % STEPS // NG, n % NG
                    column = it * 2 + j - (2 if n < 0 else 0)
                    dve.wait_ge(*four["down"](it, n + 1))
                    for t in range(TILES):
                        tile = TILES * g + t
                        last = dve.scalar_tensor_tensor(
                            out=acc[:, tile, :], in0=PS[:, 4 + 2 * (n % 2) + t // 2, (t % 2) * DIM:(t % 2 + 1) * DIM],
                            scalar=route4[:, tile, bass.ds(column, 1)], in1=acc[:, tile, :],
                            op0=ALU.mult, op1=ALU.add)
                    last.then_inc(four["added"].sem, 1)

                for n in range(STEPS):
                    if first and n + 2 < NG:
                        group_low(n + 2)
                    hidden(n)
                    if n >= BEHIND or not first:
                        add(n - BEHIND)
                if final:
                    for n in range(STEPS - BEHIND, STEPS):
                        add(n)

            group_low(0)
            group_low(1)
            dve.wait_ge(*in4(0, 16))
            dve.sem_inc(four["hidden"].sem, 2)
            dve.sem_inc(four["added"].sem, 2)
            expert_loop(dve, body)
            dve.wait_ge(*four["added"](ITERATIONS - 1, STEPS))
            with dve.Fori(0, NG) as g:
                restart(dve, dve_chain)
                link(dve, dve_chain, dve.tensor_copy(rr[:, :, :], acc[:, bass.ds(g * TILES, TILES), :]))
                dve_stats(dve, rr, four_ln["var"])
                dve.wait_ge(*four_ln["rstd"](g, 1))
                dve.wait_ge(*stored4(g, 0))
                dve_normalise(dve, y, rr).then_inc(four_ln["out"].sem, 1)
                dve.wait_ge(*four_ln["out"](g, 1))

        def pool_phase4(pool):
            def expert_low(it, j):
                pool.wait_ge(*w_split["high"](it, j + 1))
                pool.tensor_tensor(w_low[:, j, :], w_expert[:, j, :], w_high[:, j, :].bitcast(F32), ALU.subtract)\
                    .then_inc(w_split["low"].sem, 1)

            def body(it, first, final):
                for n in range(STEPS):
                    pool.wait_ge(*four["high"](it, n + 1))
                    pool.tensor_tensor(h_low[:, n % SLOTS, :], hidden_t[:, n % 2, :], h_high[:, n % SLOTS, :].bitcast(F32),
                                       ALU.subtract).then_inc(four["low"].sem, 1)
                    want = split_expert_at(n)
                    if want and not (final and want[0]):
                        expert_low(it + want[0], want[1])

            expert_low(0, 0)
            expert_loop(pool, body)
            with pool.Fori(0, NG) as g:
                pool_rstd(pool, g, four_ln["var"], four_ln["rstd"])

        block = ctx.enter_context(nc.Block())

        @block.sync
        def _(sp):
            sp_phase1(sp)
            sp_phase2(sp)
            sp_phase3(sp)
            sp_phase4(sp)

        @block.tensor
        def _(pe):
            pe_phase1(pe)
            pe_phase2(pe)
            pe_phase3(pe)
            pe_phase4(pe)

        @block.scalar
        def _(act):
            act_phase1(act)
            act_phase2(act)
            act_phase3(act)
            act_phase4(act)

        @block.vector
        def _(dve):
            dve_phase1(dve)
            dve_phase2(dve)
            dve_phase3(dve)
            dve_phase4(dve)

        @block.gpsimd
        def _(pool):
            pool_phase1(pool)
            pool_phase2(pool)
            pool_phase3(pool)
            pool_phase4(pool)


def more_layout(f, h, np):
    E = "L0_ffn_"
    g = lambda n: f[E + n]
    qkv, outp, up, down = [], [], [], []
    for e in range(EXPERTS0):
        b = g("in_proj_b")[e]
        qkv.append(np.concatenate([_rows(g("in_proj_w")[e].T).reshape(128, -1), _spread(b[512:768]),
                                   _column(b[0:512])], 1))
        outp.append(np.concatenate([_rows(g("out_proj_w")[e].T).reshape(128, -1), _spread(g("out_proj_b")[e]),
                                    _spread(g("ln1_w")[e]), _spread(g("ln1_b")[e])], 1))
        up.append(np.concatenate([_rows(g("lin1_w")[e].T).reshape(128, -1), _column(g("lin1_b")[e])], 1))
        down.append(np.concatenate([_rows(g("lin2_w")[e].T).reshape(128, -1), _spread(g("lin2_b")[e]),
                                    _spread(g("ln2_w")[e]), _spread(g("ln2_b")[e])], 1))
    for n, v in (("f_qkv", qkv), ("f_out", outp), ("f_up", up), ("f_down", down)):
        h[n] = np.stack(v)
    h["aw"] = _rows(f["L1_attn_W_qkv"])
    M = "L1_xattn_"
    h["mgate"] = _rows(np.concatenate([f[M + "igate_kernel"], f[M + "fgate_kernel"]], 1))
    h["mgate_bias"] = _spread(np.concatenate([f[M + "igate_bias"], f[M + "fgate_bias"]]))
    h["outnorm"] = _spread(f[M + "outnorm_scale"])
    h["gate1"] = _rows(f["L1_ffn_gate_w"].T)
    h["gate1_bias"] = _spread(f["L1_ffn_gate_bias"])
    F = "L1_ffn_"
    gate = np.concatenate([f[F + "expert_gate"], f[F + "shared_gate"].reshape(2, INNER, DIM)])
    up1 = np.concatenate([f[F + "expert_up"], f[F + "shared_up"].reshape(2, INNER, DIM)])
    down1 = np.concatenate([f[F + "expert_down"], f[F + "shared_down"].reshape(DIM, 2, INNER).transpose(1, 0, 2)])
    both = np.concatenate([gate.transpose(0, 2, 1).reshape(-1, KT, 128, INNER),
                           up1.transpose(0, 2, 1).reshape(-1, KT, 128, INNER)], 3)
    both = both.transpose(0, 2, 1, 3).reshape(-1, 128, KT * 2 * INNER)
    h["experts"] = np.concatenate([both, down1.transpose(0, 2, 1)], 2)


def _rows(w, rows=128):
    import numpy as np
    return np.ascontiguousarray(w.reshape(w.shape[0] // rows, rows, w.shape[1]).transpose(1, 0, 2))


def _spread(v):
    import numpy as np
    return np.ascontiguousarray(np.broadcast_to(np.asarray(v).reshape(1, -1), (128, np.asarray(v).size)))


def _column(v):
    import numpy as np
    return np.ascontiguousarray(np.asarray(v).reshape(-1, 128).T)


def layout(a):
    import numpy as np
    f = {k: np.asarray(v) for k, v in a.items()}
    P = 128
    h = {}
    h["x"] = f["x"].reshape(-1, DIM)
    h["xT"] = np.ascontiguousarray(h["x"].T)
    h["ctx"] = f["ctx_1024"].reshape(-1, DIM)
    h["ctxT"] = np.ascontiguousarray(h["ctx"].T)
    L = "L0_attn_"
    h["wqk"] = _rows(np.concatenate([f[L + "Wq"], f[L + "Wk"]], 1))
    h["wvg"] = _rows(np.concatenate([f[L + "Wv"], f[L + "Wb"], f[L + "Wfd"], f[L + "Wsd"]], 1))
    h["decay_bias"] = _spread(np.concatenate([np.zeros(16, np.float32), f[L + "bfd"], f[L + "bsd"]]))
    h["wo"] = _rows(f[L + "Wo"])
    w1 = np.zeros((P, KT, P), np.float32)
    w2 = np.zeros((P, HEADS), np.float32)
    for n in range(HEADS):
        w1[16 * (n % 8):16 * (n % 8) + 16, n // 8, 8 * n:8 * n + 8] = f[L + "Wtf1"]
        w2[8 * n:8 * n + 8, n:n + 1] = f[L + "Wtf2"]
    h["wtf1"], h["wtf2"] = w1, w2
    h["btf1"] = np.ascontiguousarray(np.tile(f[L + "btf1"], HEADS).reshape(P, 1))
    h["btf2"] = _spread(f[L + "btf2"])
    X = "L0_xattn_"
    for n, k in (("xwq", "wq"), ("xwk", "wk"), ("xwv", "wv"), ("xwo", "wo_w")):
        h[n] = _rows(f[X + k].T)
    h["wo_b"] = _spread(f[X + "wo_b"])
    h["gate0"] = _rows(f["L0_ffn_gate_w"].T)
    h["gate0_bias"] = f["L0_ffn_gate_b"].reshape(1, -1)
    half = DIM // 2
    inv_freq = (1.0 / np.float32(10000.0) ** (np.arange(half, dtype=np.float32) / half)).astype(np.float32)
    angle = (np.arange(SEQ, dtype=np.float32)[:, None] * inv_freq[None, :]).astype(np.float32).T
    h["cosT"] = np.ascontiguousarray(np.tile(np.cos(angle), (1, 2)).astype(np.float32))
    h["sinT"] = np.ascontiguousarray(np.tile(np.sin(angle), (1, 2)).astype(np.float32))
    row = np.arange(P)
    for name, halves in (("stack_q", (0, 1, 0)), ("stack_k", (0, 0, 1))):
        place = np.zeros((P, 2, 4, P), np.float32)
        for g in range(4):
            for j in range(2):
                for n, part in enumerate(halves):
                    for e in range(HD):
                        place[32 * g + HD * j + e, part, g, 64 * j + HD * n + e] = 1.0
        h[name] = place
    pick = np.zeros((P, BATCH_UNITS, P), np.float32)
    for n in range(BATCH_UNITS):
        pick[64 * (n % 2) + n, n] = pick[64 * (n % 2) + BATCH_UNITS + n, n] = 1.0
    h["pick_head"] = pick.reshape(P, 2, 2 * DIM)
    h["block_diag"] = (row[:, None] // HD == row[None, :] // HD).astype(np.float32)
    heads = np.zeros((8, 4, P), np.float32)
    for n in range(4):
        heads[n, n, :] = heads[4 + n, n, :] = 1.0
    h["head_rows"] = heads
    h["identity"] = np.eye(P, dtype=np.float32)
    h["after"] = (row[:, None] > row[None, :]).astype(np.float32)
    h["upto"] = (row[:, None] <= row[None, :]).astype(np.float32)
    q = (np.arange(2)[:, None] * P + row[None, :])[:, :, None]
    k = np.arange(SEQ)[None, None, :]
    window = np.where(np.abs(k - q) <= WINDOW, 0.0, MASKED)
    causal = np.where(k <= q, 0.0, MASKED)
    for n, m in (("window_mask", window), ("causal_mask", causal)):
        h[n] = np.ascontiguousarray(m.transpose(1, 0, 2).astype(np.float32))
    more_layout(f, h, np)
    return h


def kernel(**inputs):
    import numpy as np
    import concourse.bacc as bacc
    from concourse import mybir as mb
    from concourse.bass_utils import run_bass_kernel_spmd

    arrays = {n: np.ascontiguousarray(v) for n, v in layout(inputs).items()}
    nc = bacc.Bacc("TRN2", target_bir_lowering=False, num_devices=1)
    d = {n: nc.dram_tensor(f"in_{n}", v.shape, mb.dt.from_np(v.dtype), kind="ExternalInput").ap()
         for n, v in arrays.items()}
    out = nc.dram_tensor("out", (BATCH * SEQ, DIM), F32, kind="ExternalOutput").ap()
    build(nc, d, out)
    r = run_bass_kernel_spmd(nc, [{f"in_{n}": v for n, v in arrays.items()}], core_ids=[0])
    return r.results[0]["out"].reshape(BATCH, SEQ, DIM)
```
